# Optimizing a Trainium2 kernel written in Bass

```python
import numpy as np
import jax
import jax.numpy as jnp

def _softmax(x, axis=-1):
    return jax.nn.softmax(x, axis=axis)

def _gelu(x):
    return jax.nn.gelu(x, approximate=True)

def _silu(x):
    return jax.nn.silu(x)

def _sigmoid(x):
    return jax.nn.sigmoid(x)

def _layernorm(x, axis=-1, eps=1e-05):
    m = jnp.mean(x, axis=axis, keepdims=True)
    v = jnp.var(x, axis=axis, keepdims=True)
    return (x - m) / jnp.sqrt(v + eps)

def _scatter_add(tgt, idx, src, axis=0):
    return tgt.at[idx].add(src)

def _segment_sum(src, seg, n):
    return jax.ops.segment_sum(src, seg, n)
kernel_name = 'mk_gnn_preln_d4_gnn_r64_7c5ecc'

def setup_inputs(seed: int=0):
    np.random.seed(seed)
    _w = jnp.asarray

    def _rec_inputs():
        import jax
        import jax.numpy as jnp
        _gk = jax.random.key(seed)
        x = -0.0003713 + 1 * jax.random.normal(jax.random.fold_in(_gk, 1), (50000, 128), jnp.float32)
        src = jax.random.randint(jax.random.fold_in(_gk, 2), (25000,), 0, 50000, jnp.int32)
        dst = jnp.minimum((50000 * jax.random.uniform(jax.random.fold_in(_gk, 3), (25000,)) ** 2.0).astype(jnp.int32), 49999)
        _o = jnp.argsort(dst, stable=True)
        src = src[_o]
        dst = dst[_o]
        edge_attr_128 = -5.16925e-05 + 1.00005 * jax.random.normal(jax.random.fold_in(_gk, 12), (25000, 128), jnp.float32)
        edge_attr_50 = 0.000164634 + 1.0002 * jax.random.normal(jax.random.fold_in(_gk, 13), (25000, 50), jnp.float32)
        return (x, src, dst, edge_attr_128, edge_attr_50)
    x, src, dst, edge_attr_128, edge_attr_50 = _rec_inputs()

    def _L0_gnn_setup():
        import jax, jax.numpy as jnp
        import numpy as np
        N_NODES = 100000
        D_IN = 128
        D_HID = 128
        N_EDGES = 25000

        def _sage_conv(x, src, dst, Wl, Wr, b, n_nodes):
            msgs = x[src]
            agg = jax.ops.segment_sum(msgs, dst, num_segments=n_nodes)
            cnt = jax.ops.segment_sum(jnp.ones((src.shape[0],), x.dtype), dst, num_segments=n_nodes)
            agg = agg / jnp.maximum(cnt, 1.0)[:, None]
            return agg @ Wl + x @ Wr + b
        key = jax.random.key(seed)
        ks = jax.random.split(key, 8)
        x = jax.random.normal(ks[0], (N_NODES, D_IN), dtype=jnp.float32)
        edge_index = jax.random.randint(ks[1], (2, N_EDGES), 0, N_NODES, dtype=jnp.int64)
        s = 1.0 / np.sqrt(D_IN)
        W1l = jax.random.uniform(ks[2], (D_IN, D_HID), jnp.float32, -s, s)
        W1r = jax.random.uniform(ks[3], (D_IN, D_HID), jnp.float32, -s, s)
        b1 = jnp.zeros((D_HID,), jnp.float32)
        sh = 1.0 / np.sqrt(D_HID)
        W2l = jax.random.uniform(ks[4], (D_HID, D_HID), jnp.float32, -sh, sh)
        W2r = jax.random.uniform(ks[5], (D_HID, D_HID), jnp.float32, -sh, sh)
        b2 = jnp.zeros((D_HID,), jnp.float32)
        return {'x': x, 'edge_index': edge_index, 'W1l': W1l, 'W1r': W1r, 'b1': b1, 'W2l': W2l, 'W2r': W2r, 'b2': b2}
    _L0_gnn_all = _L0_gnn_setup()
    _L0_gnn_in = {k: v for k, v in _L0_gnn_all.items() if k in ('W1l', 'W1r', 'b1', 'W2l', 'W2r', 'b2')}
    del _L0_gnn_all

    def _L1_gnn_setup():
        import jax, jax.numpy as jnp
        import numpy as np
        N_NODES = 50000
        N_EDGES = 12500
        NODE_DIM = 128
        EDGE_DIM = 50
        HIDDEN_DIM = 128

        def _linear_params(key, fan_in, fan_out):
            kw, kb = jax.random.split(key)
            bound = 1.0 / np.sqrt(fan_in)
            W = jax.random.uniform(kw, (fan_in, fan_out), minval=-bound, maxval=bound, dtype=jnp.float32)
            b = jax.random.uniform(kb, (fan_out,), minval=-bound, maxval=bound, dtype=jnp.float32)
            return (W, b)
        key = jax.random.key(seed)
        ks = jax.random.split(key, 7)
        x = jax.random.normal(ks[0], (N_NODES, NODE_DIM), dtype=jnp.float32)
        edge_index = jax.random.randint(ks[1], (2, N_EDGES), 0, N_NODES, dtype=jnp.int64)
        edge_features = jax.random.normal(ks[2], (N_EDGES, EDGE_DIM), dtype=jnp.float32)
        We1, be1 = _linear_params(ks[3], EDGE_DIM, HIDDEN_DIM)
        We2, be2 = _linear_params(ks[4], HIDDEN_DIM, NODE_DIM)
        Wn1, bn1 = _linear_params(ks[5], NODE_DIM, HIDDEN_DIM)
        Wn2, bn2 = _linear_params(ks[6], HIDDEN_DIM, NODE_DIM)
        return {'x': x, 'edge_index': edge_index, 'edge_features': edge_features, 'We1': We1, 'be1': be1, 'We2': We2, 'be2': be2, 'Wn1': Wn1, 'bn1': bn1, 'Wn2': Wn2, 'bn2': bn2}
    _L1_gnn_all = _L1_gnn_setup()
    _L1_gnn_in = {k: v for k, v in _L1_gnn_all.items() if k in ('We1', 'be1', 'We2', 'be2', 'Wn1', 'bn1', 'Wn2', 'bn2')}
    del _L1_gnn_all

    def _L2_gnn_setup():
        import jax, jax.numpy as jnp
        import numpy as np
        N_NODES = 50000
        N_EDGES = 12500
        D = 128
        OUT = 128
        N_GRAPHS = 64
        IN1 = 4 * D
        IN2 = D + OUT + D
        key = jax.random.key(seed)
        ks = jax.random.split(key, 10)
        x = jax.random.normal(ks[0], (N_NODES, D), dtype=jnp.float32)
        edge_index = jax.random.randint(ks[1], (2, N_EDGES), 0, N_NODES, dtype=jnp.int64)
        edge_attr = jax.random.normal(ks[2], (N_EDGES, D), dtype=jnp.float32)
        u = jax.random.normal(ks[3], (N_GRAPHS, D), dtype=jnp.float32)
        batch = jnp.sort(jax.random.randint(ks[4], (N_NODES,), 0, N_GRAPHS, dtype=jnp.int64))
        W1 = jax.random.normal(ks[5], (OUT, IN1), dtype=jnp.float32) / np.sqrt(IN1)
        b1 = jnp.zeros((OUT,), dtype=jnp.float32)
        W2 = jax.random.normal(ks[6], (OUT, IN2), dtype=jnp.float32) / np.sqrt(IN2)
        b2 = jnp.zeros((OUT,), dtype=jnp.float32)
        return {'x': x, 'edge_index': edge_index, 'edge_attr': edge_attr, 'u': u, 'batch': batch, 'W1': W1, 'b1': b1, 'W2': W2, 'b2': b2}
    _L2_gnn_all = _L2_gnn_setup()
    _L2_gnn_in = {k: v for k, v in _L2_gnn_all.items() if k in ('u', 'W1', 'b1', 'W2', 'b2')}
    del _L2_gnn_all

    def _L3_gnn_setup():
        import jax, jax.numpy as jnp
        import numpy as np
        N = 20000
        DEG = 16
        E = N * DEG
        DIM = 128
        H = 8
        HD = DIM // H
        HE = 8
        SCALE = HD ** (-0.5)
        key = jax.random.key(seed)
        ks = jax.random.split(key, 10)
        s = 0.05
        x = jax.random.normal(ks[0], (N, DIM), jnp.float32)
        edges = jax.random.normal(ks[1], (E, DIM), jnp.float32)
        src = jnp.repeat(jnp.arange(N, dtype=jnp.int32), DEG)
        off = jnp.tile(jnp.arange(1, DEG + 1, dtype=jnp.int32), N)
        dst = (src + off) % N
        edge_index = jnp.stack([src, dst], axis=0)
        Wq = jax.random.normal(ks[2], (DIM, DIM), jnp.float32) * s
        Wk = jax.random.normal(ks[3], (DIM, DIM), jnp.float32) * s
        Wv = jax.random.normal(ks[4], (DIM, HE * HD), jnp.float32) * s
        Wek = jax.random.normal(ks[5], (DIM, DIM), jnp.float32) * s
        Wev = jax.random.normal(ks[6], (DIM, HE * HD), jnp.float32) * s
        Wexp = jax.random.normal(ks[7], (H, HE), jnp.float32) * s
        Wout = jax.random.normal(ks[8], (HE * HD, DIM), jnp.float32) * s
        bout = jnp.zeros((DIM,), jnp.float32)
        return {'x': x, 'edges': edges, 'edge_index': edge_index, 'Wq': Wq, 'Wk': Wk, 'Wv': Wv, 'Wek': Wek, 'Wev': Wev, 'Wexp': Wexp, 'Wout': Wout, 'bout': bout}
    _L3_gnn_all = _L3_gnn_setup()
    _L3_gnn_in = {k: v for k, v in _L3_gnn_all.items() if k in ('Wq', 'Wk', 'Wv', 'Wek', 'Wev', 'Wexp', 'Wout', 'bout')}
    del _L3_gnn_all
    return {'x': x, 'src': src, 'dst': dst, 'edge_attr_128': edge_attr_128, 'edge_attr_50': edge_attr_50, 'L0_gnn_W1l': _L0_gnn_in['W1l'], 'L0_gnn_W1r': _L0_gnn_in['W1r'], 'L0_gnn_b1': _L0_gnn_in['b1'], 'L0_gnn_W2l': _L0_gnn_in['W2l'], 'L0_gnn_W2r': _L0_gnn_in['W2r'], 'L0_gnn_b2': _L0_gnn_in['b2'], 'L1_gnn_We1': _L1_gnn_in['We1'], 'L1_gnn_be1': _L1_gnn_in['be1'], 'L1_gnn_We2': _L1_gnn_in['We2'], 'L1_gnn_be2': _L1_gnn_in['be2'], 'L1_gnn_Wn1': _L1_gnn_in['Wn1'], 'L1_gnn_bn1': _L1_gnn_in['bn1'], 'L1_gnn_Wn2': _L1_gnn_in['Wn2'], 'L1_gnn_bn2': _L1_gnn_in['bn2'], 'L2_gnn_u': _L2_gnn_in['u'], 'L2_gnn_W1': _L2_gnn_in['W1'], 'L2_gnn_b1': _L2_gnn_in['b1'], 'L2_gnn_W2': _L2_gnn_in['W2'], 'L2_gnn_b2': _L2_gnn_in['b2'], 'L3_gnn_Wq': _L3_gnn_in['Wq'], 'L3_gnn_Wk': _L3_gnn_in['Wk'], 'L3_gnn_Wv': _L3_gnn_in['Wv'], 'L3_gnn_Wek': _L3_gnn_in['Wek'], 'L3_gnn_Wev': _L3_gnn_in['Wev'], 'L3_gnn_Wexp': _L3_gnn_in['Wexp'], 'L3_gnn_Wout': _L3_gnn_in['Wout'], 'L3_gnn_bout': _L3_gnn_in['bout']}

def reference(x, src, dst, edge_attr_128, edge_attr_50, L0_gnn_W1l, L0_gnn_W1r, L0_gnn_b1, L0_gnn_W2l, L0_gnn_W2r, L0_gnn_b2, L1_gnn_We1, L1_gnn_be1, L1_gnn_We2, L1_gnn_be2, L1_gnn_Wn1, L1_gnn_bn1, L1_gnn_Wn2, L1_gnn_bn2, L2_gnn_u, L2_gnn_W1, L2_gnn_b1, L2_gnn_W2, L2_gnn_b2, L3_gnn_Wq, L3_gnn_Wk, L3_gnn_Wv, L3_gnn_Wek, L3_gnn_Wev, L3_gnn_Wexp, L3_gnn_Wout, L3_gnn_bout):
    import jax
    import jax.numpy as jnp

    def _L0_gnn_ref(x, edge_index, W1l, W1r, b1, W2l, W2r, b2):
        import jax, jax.numpy as jnp
        import numpy as np
        N_NODES = 100000
        D_IN = 128
        D_HID = 128
        N_EDGES = 25000

        def _sage_conv(x, src, dst, Wl, Wr, b, n_nodes):
            msgs = x[src]
            agg = jax.ops.segment_sum(msgs, dst, num_segments=n_nodes)
            cnt = jax.ops.segment_sum(jnp.ones((src.shape[0],), x.dtype), dst, num_segments=n_nodes)
            agg = agg / jnp.maximum(cnt, 1.0)[:, None]
            return agg @ Wl + x @ Wr + b
        src, dst = (edge_index[0], edge_index[1])
        n = x.shape[0]
        h = jax.nn.relu(_sage_conv(x, src, dst, W1l, W1r, b1, n))
        return _sage_conv(h, src, dst, W2l, W2r, b2, n)

    def _L1_gnn_ref(x, edge_index, edge_features, We1, be1, We2, be2, Wn1, bn1, Wn2, bn2):
        import jax, jax.numpy as jnp
        import numpy as np
        N_NODES = 50000
        N_EDGES = 12500
        NODE_DIM = 128
        EDGE_DIM = 50
        HIDDEN_DIM = 128

        def _linear_params(key, fan_in, fan_out):
            kw, kb = jax.random.split(key)
            bound = 1.0 / np.sqrt(fan_in)
            W = jax.random.uniform(kw, (fan_in, fan_out), minval=-bound, maxval=bound, dtype=jnp.float32)
            b = jax.random.uniform(kb, (fan_out,), minval=-bound, maxval=bound, dtype=jnp.float32)
            return (W, b)
        src = edge_index[0]
        dst = edge_index[1]
        edge_weights = jax.nn.silu(edge_features @ We1 + be1) @ We2 + be2
        messages = x[src] * edge_weights
        agg = jax.ops.segment_sum(messages, dst, num_segments=x.shape[0])
        out = jax.nn.silu(agg @ Wn1 + bn1) @ Wn2 + bn2
        return x + out

    def _L2_gnn_ref(x, edge_index, edge_attr, u, batch, W1, b1, W2, b2):
        import jax, jax.numpy as jnp
        import numpy as np
        N_NODES = 50000
        N_EDGES = 12500
        D = 128
        OUT = 128
        N_GRAPHS = 64
        IN1 = 4 * D
        IN2 = D + OUT + D
        src, dst = (edge_index[0], edge_index[1])
        source_features = x[src]
        dest_features = x[dst]
        u_edge = u[batch[dst]]
        edge_input = jnp.concatenate([dest_features, source_features, edge_attr, u_edge], axis=1)
        edge_messages = jax.nn.relu(edge_input @ W1.T + b1)
        aggregated = jax.ops.segment_sum(edge_messages, dst, num_segments=x.shape[0])
        u_expanded = u[batch]
        node_input = jnp.concatenate([x, aggregated, u_expanded], axis=1)
        return jax.nn.relu(node_input @ W2.T + b2)

    def _L3_gnn_ref(x, edges, edge_index, Wq, Wk, Wv, Wek, Wev, Wexp, Wout, bout):
        import jax, jax.numpy as jnp
        import numpy as np
        N = 20000
        DEG = 16
        E = N * DEG
        DIM = 128
        H = 8
        HD = DIM // H
        HE = 8
        SCALE = HD ** (-0.5)
        n = x.shape[0]
        src, dst = (edge_index[0], edge_index[1])
        qg = (x @ Wq)[src].reshape(-1, H, HD)
        kg = ((x @ Wk)[dst] * SCALE + edges @ Wek * SCALE).reshape(-1, H, HD)
        scores = jnp.einsum('ehd,ehd->eh', qg, kg)
        scores = scores @ Wexp
        seg_max = jax.ops.segment_max(scores, src, num_segments=n)
        exps = jnp.exp(scores - seg_max[src])
        denom = jax.ops.segment_sum(exps, src, num_segments=n)
        a = exps / denom[src]
        v_e = ((x @ Wv)[dst] + edges @ Wev).reshape(-1, HE, HD)
        agg = jax.ops.segment_sum(a[:, :, None] * v_e, src, num_segments=n)
        self_m = (src == dst).astype(x.dtype)
        self_c = jax.ops.segment_sum(v_e * self_m[:, None, None], src, num_segments=n)
        out = (self_c - agg).reshape(n, HE * HD)
        return out @ Wout + bout
    edge_index = jnp.stack([src, dst])
    batch0 = jnp.zeros((50000,), jnp.int32)
    h = jnp.maximum(_layernorm(x, axis=-1), 0.0)
    x = x + _L0_gnn_ref(h, edge_index, L0_gnn_W1l, L0_gnn_W1r, L0_gnn_b1, L0_gnn_W2l, L0_gnn_W2r, L0_gnn_b2)
    h = jnp.maximum(_layernorm(x, axis=-1), 0.0)
    x = x + _L1_gnn_ref(h, edge_index, edge_attr_50, L1_gnn_We1, L1_gnn_be1, L1_gnn_We2, L1_gnn_be2, L1_gnn_Wn1, L1_gnn_bn1, L1_gnn_Wn2, L1_gnn_bn2)
    h = jnp.maximum(_layernorm(x, axis=-1), 0.0)
    x = x + _L2_gnn_ref(h, edge_index, edge_attr_128, L2_gnn_u, batch0, L2_gnn_W1, L2_gnn_b1, L2_gnn_W2, L2_gnn_b2)
    h = jnp.maximum(_layernorm(x, axis=-1), 0.0)
    x = x + _L3_gnn_ref(h, edge_attr_128, edge_index, L3_gnn_Wq, L3_gnn_Wk, L3_gnn_Wv, L3_gnn_Wek, L3_gnn_Wev, L3_gnn_Wexp, L3_gnn_Wout, L3_gnn_bout)
    return x

_drawn_inputs = setup_inputs


def setup_inputs(seed=0):
    import zlib

    import numpy as np

    out = dict(_drawn_inputs(seed))
    spreads = {'L0_gnn_b1': (0.0, 0.1),
     'L0_gnn_b2': (0.0, 0.1),
     'L2_gnn_b1': (0.0, 2.0),
     'L2_gnn_b2': (0.0, 2.0),
     'L3_gnn_bout': (0.0, 2.0)}
    factors = {'edge_attr_50': 6.19,
     'L1_gnn_We1': 6.192,
     'L1_gnn_be1': 8.0,
     'L1_gnn_We2': 5.509,
     'L1_gnn_be2': 47.173,
     'L1_gnn_Wn1': 4.776,
     'L1_gnn_bn1': 52.352,
     'L1_gnn_Wn2': 3.833,
     'L3_gnn_Wq': 64.0,
     'L3_gnn_Wk': 64.0,
     'L3_gnn_Wek': 64.0,
     'L3_gnn_Wexp': 64.0,
     'edge_attr_128': 8.0,
     'L1_gnn_bn2': 22.485,
     'L2_gnn_u': 8.0,
     'L2_gnn_W1': 8.0,
     'L2_gnn_W2': 8.0,
     'L3_gnn_Wv': 8.0,
     'L3_gnn_Wev': 8.0,
     'L3_gnn_Wout': 8.0}
    for name, (base, spread) in spreads.items():
        noise = np.random.default_rng([zlib.crc32(name.encode()), seed]).standard_normal(out[name].shape)
        drawn = base * np.exp(spread * noise) if base else spread * noise
        out[name] = jnp.asarray(drawn.astype(out[name].dtype))
    for name, factor in factors.items():
        out[name] = (out[name] * factor).astype(out[name].dtype)
    return out
```

```python
import concourse.bass as bass
from concourse import mybir
from contextlib import ExitStack

F32 = mybir.dt.float32
F16 = mybir.dt.float16
I32 = mybir.dt.int32
U32 = mybir.dt.uint32
ALU = mybir.AluOpType
ACT = mybir.ActivationFunctionType
AX_X = mybir.AxisListType.X

P = 128
D = 128
J = 4
ROWS = J * P
HEADS = 8
HEAD_DIM = D // HEADS
SCALE = HEAD_DIM ** -0.5
EPS = 1e-5
LO_BITS = 9
LO = 1 << LO_BITS
SC_W = 16
FAR = 1.0e38


def padded(n, unit):
    return -(-n // unit) * unit


def two_slot_loop(eng, steps, stages):
    def step(t, static):
        for lag, fn in stages:
            if static:
                b = t - lag
                if 0 <= b < steps:
                    fn(b, b // 2, b % 2, b < 2)
            else:
                i, s = t
                slot = (s - lag) % 2
                fn(i * 2 + (s - lag), i + (s - lag - slot) // 2, slot, False)

    assert steps % 2 == 0 and steps > 4
    for t in range(4):
        step(t, True)
    with eng.Fori(2, steps // 2) as i:
        step((i, 0), False)
        step((i, 1), False)
    for t in range(steps, steps + max(lag for lag, _ in stages)):
        step(t, True)


def gnn_kernel(nc, ins, out, n_nodes, n_edges):
    NODES = padded(n_nodes, 2 * ROWS)
    EDGES = padded(n_edges, 2 * ROWS)
    NB = NODES // ROWS
    NG = EDGES // ROWS
    HI = NODES // LO
    NT = EDGES // P
    TABLE = NODES + ROWS

    with ExitStack() as ctx:
        def sb(name, shape, dt=F32):
            return ctx.enter_context(nc.sbuf_tensor(name, shape, dt))

        in_use = []

        def sem(name):
            in_use.append(nc.alloc_semaphore(name=name))
            return in_use[-1]

        def sem2(name):
            return [sem(name + "_0"), sem(name + "_1")]

        def dram(name, shape, dt=F32):
            return nc.dram_tensor(name, shape, dt, kind="Internal").ap()

        h0, h1, h2, h3, h4 = [dram(f"h{n}", (NODES, D)) for n in range(5)]
        y1, y2, z1, y3 = [dram(n, (TABLE, D)) for n in ("y1", "y2", "z1", "y3")]
        x1h = dram("x1h", (NODES, D))
        x2 = dram("x2", (NODES, D))
        values = dram("values", (NG, P, J * D))
        sorted_scores = dram("sorted_scores", (EDGES + 2, SC_W))
        sorted_weights = dram("sorted_weights", (EDGES + 2, HEADS))

        psum = [ctx.enter_context(nc.psum_tensor(f"bank{n}", [P, ROWS], F32)) for n in range(8)]
        T = [sb(f"tile{n}", [P, 2, ROWS]) for n in range(8)]
        same = sb("same", [P, 2, J, ROWS])
        idx_row = sb("idx_row", [P, 2, ROWS], I32)

        ident = sb("ident", [P, P])
        ident16 = sb("ident16", [P, P], F16)
        ones = sb("ones", [P, P])
        iota_lo = sb("iota_lo", [P, LO], F16)
        before = sb("before", [P, J, ROWS])
        upper = sb("upper", [P, P])
        spare = sb("spare", [P, J])
        eps = sb("eps", [P, 1])
        zeros = sb("zeros", [P, ROWS])
        minus_ones = sb("minus_ones", [P, SC_W])

        weights = {}
        for name in ("L0_gnn_W1l", "L0_gnn_W1r", "L0_gnn_W2l", "L0_gnn_W2r", "L1_gnn_We2", "L1_gnn_Wn1",
                     "L1_gnn_Wn2", "L3_gnn_Wq", "L3_gnn_Wout"):
            weights[name] = sb("w_" + name, [P, D])
        w_e1 = sb("w_e1", [50, D])
        w_kv = sb("w_kv", [P, 2 * D])
        w_ekv = sb("w_ekv", [P, 2 * D])
        w_1 = sb("w_1", [P, 4, D])
        w_2 = sb("w_2", [P, 3, D])
        w_exp = sb("w_exp", [P, HEADS * HEADS])
        be1 = sb("be1", [P, 1])
        u0 = sb("u0", [P, 1])
        u_cols = sb("u_cols", [P, P])
        rows = {}
        for name in ("L0_gnn_b1", "L0_gnn_b2", "L1_gnn_be2", "L1_gnn_bn1", "L1_gnn_bn2", "L2_gnn_b1",
                     "L2_gnn_b2", "L3_gnn_bout"):
            rows[name] = sb("b_" + name, [P, D])
        z_init = sb("z_init", [P, ROWS])
        c1 = sb("c1", [P, D])
        c2 = sb("c2", [P, D])

        src_i = sb("src_i", [P, NT], I32)
        dst_i = sb("dst_i", [P, NT], I32)
        hl_i = sb("hl_i", [P, 4, NT], I32)
        src_f = sb("src_f", [P, NT])
        dst_f = sb("dst_f", [P, NT])
        hl_f = sb("hl_f", [P, 4, NT])
        dup = sb("dup", [P, 2, NT])
        flag = sb("flag", [P, NT])
        tmp_t = sb("tmp_t", [P, NT])
        src_add = sb("src_add", [P, NT])
        dst_add = sb("dst_add", [P, NT])
        inv_count = sb("inv_count", [P, NT])
        looked_up = sb("looked_up", [P, 2, NT])
        sort_pos = sb("sort_pos", [P, NT])
        is_self = sb("is_self", [P, NT])

        stats = sb("stats", [P, 2, J, 6])
        mean_var = sb("mean_var", [P, 2, J, 2])
        std = sb("std", [P, 2, J])
        rstd = sb("rstd", [P, 2, J])
        shift = sb("shift", [P, 2, J])

        gather_a = sb("gather_a", [P, 2, J], U32)
        gather_b = sb("gather_b", [P, 2, J], U32)
        add_to = sb("add_to", [P, 2, J], U32)

        onehot_hi = sb("onehot_hi", [P, 2, J, HI], F16)
        onehot_lo = sb("onehot_lo", [P, 2, J, LO], F16)
        hi_turned = sb("hi_turned", [HI, 2, J, P])
        hist = sb("hist", [HI, LO])
        hist_run = sb("hist_run", [HI, LO])
        hist_base = sb("hist_base", [HI, LO])
        table = sb("table", [HI, 2, LO])
        row_off = sb("row_off", [HI, 1])
        picked = sb("picked", [P, 2, LO])
        idx_cols = sb("idx_cols", [P, 2, J])
        dup_cols = sb("dup_cols", [P, J])
        picked_cols = sb("picked_cols", [P, J])

        score = sb("score", [P, 2, J, SC_W])
        qk_sum = sb("qk_sum", [P, 2, J * HEADS])
        mixed = sb("mixed", [P, J * HEADS * HEADS])
        weight_in = sb("weight_in", [P, 2, J, HEADS])
        self_minus = sb("self_minus", [P, 2, J, HEADS])

        ss = sb("ss", [P, NT + 2, SC_W])
        keep = sb("keep", [P, 2, NT])
        drop = sb("drop", [P, 2, NT])
        cum = sb("cum", [P, 2, 2, NT])
        scan_f = sb("scan_f", [P, HEADS, NT])
        scan_b = sb("scan_b", [P, HEADS, NT])
        expd = sb("expd", [P, HEADS, NT])
        edge_in = sb("edge_in", [P, 2, HEADS])
        turned = sb("turned", [HEADS, 2, P])
        carry = sb("carry", [HEADS, P + 1])
        carry_in = sb("carry_in", [P, HEADS])

        def wait_on_pool(pool, s, value):
            pool.wait_ge(s, value)
            pool.sem_inc(pool_waits, 1)

        pool_waits = nc.alloc_semaphore(name="pool_waits")
        dve_waits = nc.alloc_semaphore(name="dve_waits")

        def block_rows(table_ap, b):
            return table_ap[bass.ds(b * ROWS, ROWS), :].rearrange("(p j) d -> p (j d)", j=J)

        def across(row, n=J):
            return row.unsqueeze(1).to_broadcast([P, n, D])

        def jd(ap):
            return ap.rearrange("p (j d) -> p j d", j=J)

        def end_phase():
            nc.clear_and_free_semaphores(in_use)
            in_use.clear()
            nc.all_engine_barrier()

        def setup():
            loads = sem("setup_loads")
            consts = sem("setup_consts")
            vec = sem("setup_vec")
            u_ready = sem("setup_u_cols")
            c_mm = sem("setup_c_products")
            n_loads = [0]

            with nc.Block() as block:
                @block.sync
                def _(sp):
                    def load(dst, src):
                        sp.dma_start(dst, src).then_inc(loads, 16)
                        n_loads[0] += 1
                    load(src_i[:, :], ins["src_cols"])
                    load(dst_i[:, :], ins["dst_cols"])
                    for name, t in weights.items():
                        load(t[:, :], ins[name])
                    load(w_e1[:, :], ins["L1_gnn_We1"])
                    load(w_kv[:, 0:D], ins["L3_gnn_Wk"])
                    load(w_kv[:, D:2 * D], ins["L3_gnn_Wv"])
                    load(w_ekv[:, 0:D], ins["L3_gnn_Wek"])
                    load(w_ekv[:, D:2 * D], ins["L3_gnn_Wev"])
                    load(w_1[:, :, :], ins["L2_gnn_W1"].rearrange("(k p) n -> p k n", p=P))
                    load(w_2[:, :, :], ins["L2_gnn_W2"].rearrange("(k p) n -> p k n", p=P))
                    load(w_exp[:, :], ins["L3_gnn_Wexp"].partition_broadcast(P))
                    load(be1[:, :], ins["L1_gnn_be1"].rearrange("(p a) -> p a", a=1))
                    load(u0[:, :], ins["L2_gnn_u"][0, :].rearrange("(p a) -> p a", a=1))
                    for name, t in rows.items():
                        load(t[:, :], ins[name].partition_broadcast(P))
                    sp.wait_ge(consts, 12)
                    for t in (y1, y2, z1, y3, out):
                        load(t[NODES:TABLE, :].rearrange("(p j) d -> p (j d)", j=J), zeros[:, :])
                    load(sorted_scores[0:1, :], minus_ones[0:1, :])
                    load(sorted_scores[EDGES + 1:EDGES + 2, :], minus_ones[0:1, :])
                    load(sorted_weights[0:1, :], minus_ones[0:1, 0:HEADS])
                    load(sorted_weights[EDGES + 1:EDGES + 2, :], minus_ones[0:1, 0:HEADS])
                    sp.wait_ge(loads, 16 * n_loads[0])

                @block.gpsimd
                def _(pool):
                    pool.memset(ident[:, :], 0.0).then_inc(consts, 1)
                    pool.memset(ones[:, :], 1.0).then_inc(consts, 1)
                    pool.memset(before[:, :, :], 1.0).then_inc(consts, 1)
                    pool.memset(eps[:, :], EPS).then_inc(consts, 1)
                    pool.memset(zeros[:, :], 0.0).then_inc(consts, 1)
                    pool.memset(minus_ones[:, :], -1.0).then_inc(consts, 1)
                    pool.wait_ge(consts, 6)
                    pool.affine_select(out=ident[:, :], in_=ident[:, :], compare_op=ALU.not_equal, fill=1.0, base=0,
                                       pattern=[[-1, P]], channel_multiplier=1).then_inc(consts, 1)
                    pool.affine_select(out=before[:, :, :], in_=before[:, :, :], compare_op=ALU.is_gt, fill=0.0, base=0,
                                       pattern=[[P, J], [-1, ROWS]], channel_multiplier=1).then_inc(consts, 1)
                    pool.affine_select(out=upper[:, :], in_=ones[:, :], compare_op=ALU.is_gt, fill=0.0, base=0,
                                       pattern=[[1, P]], channel_multiplier=-1).then_inc(consts, 1)
                    pool.iota(same[:, 0, 0, :], [[1, LO]], base=0, channel_multiplier=0,
                              allow_small_or_imprecise_dtypes=True).then_inc(consts, 1)
                    pool.iota(spare[:, :], [[P, J]], base=NODES, channel_multiplier=1,
                              allow_small_or_imprecise_dtypes=True).then_inc(consts, 1)
                    pool.memset(score[:, :, :, :], 0.0).then_inc(consts, 1)

                @block.vector
                def _(dve):
                    dve.wait_ge(consts, 12)
                    dve.wait_ge(loads, 16 * n_loads[0])
                    dve.tensor_copy(ident16[:, :], ident[:, :]).then_inc(vec, 1)
                    dve.tensor_copy(iota_lo[:, :], same[:, 0, 0, :]).then_inc(vec, 1)
                    dve.tensor_copy(u_cols[:, :], u0[:, 0:1].to_broadcast([P, P])).then_inc(u_ready, 1)
                    dve.tensor_copy(jd(z_init[:, :]), across(rows["L1_gnn_bn1"][:, :])).then_inc(vec, 1)
                    for n, (t, f) in enumerate(((src_i, src_f), (dst_i, dst_f))):
                        dve.tensor_copy(f[:, :], t[:, :]).then_inc(vec, 1)
                        dve.tensor_scalar(hl_i[:, 2 * n, :], t[:, :], LO_BITS, None,
                                          ALU.logical_shift_right).then_inc(vec, 1)
                        dve.tensor_scalar(hl_i[:, 2 * n + 1, :], t[:, :], LO - 1, None, ALU.bitwise_and).then_inc(vec, 1)
                    dve.wait_ge(vec, 9)
                    dve.tensor_copy(hl_f[:, :, :], hl_i[:, :, :]).then_inc(vec, 1)
                    dve.tensor_tensor(is_self[:, :], src_f[:, :], dst_f[:, :], ALU.is_equal).then_inc(vec, 1)
                    dve.wait_ge(c_mm, 1)
                    dve.tensor_tensor(c1[:, :], psum[0][:, 0:D], rows["L2_gnn_b1"][:, :], ALU.add).then_inc(vec, 1)
                    dve.tensor_tensor(c2[:, :], psum[1][:, 0:D], rows["L2_gnn_b2"][:, :], ALU.add).then_inc(vec, 1)

                @block.tensor
                def _(pe):
                    pe.wait_ge(u_ready, 1)
                    pe.matmul(psum[0][:, 0:D], u_cols[:, :], w_1[:, 3, :], start=True, stop=True)
                    pe.matmul(psum[1][:, 0:D], u_cols[:, :], w_2[:, 2, :], start=True, stop=True).then_inc(c_mm, 1)
            end_phase()

        def prepare_indices(name, which, idx_rows, running):
            
            idx_f = (src_f, dst_f)[which]
            row_landed = sem2(name + "_row_landed")
            dup_done = sem(name + "_dup_done")
            dup_taken = sem(name + "_dup_taken")
            cols_taken = sem(name + "_cols_taken")
            pick_taken = sem(name + "_pick_taken")
            onehots = sem(name + "_onehots")
            counted = sem(name + "_counted")
            hist_ready = sem(name + "_hist_ready")
            vec = sem(name + "_vec")
            off_mm = sem(name + "_off_mm")
            base_in = sem(name + "_base_in")
            onehots2 = sem(name + "_onehots2")
            turned_mm = sem(name + "_turned_mm")
            turned_ready = sem(name + "_turned_ready")
            table_ready = sem(name + "_table_ready")
            row_mm = sem(name + "_row_mm")
            picked_done = sem(name + "_picked_done")
            counted2 = sem(name + "_counted2")

            def build_onehots(dve, g, s, done):
                for a in range(J):
                    dve.tensor_scalar(onehot_hi[:, s, a, :], iota_lo[:, 0:HI],
                                      hl_f[:, 2 * which, bass.ds(g * J + a, 1)], None, ALU.is_equal)
                    last = dve.tensor_scalar(onehot_lo[:, s, a, :], iota_lo[:, :],
                                             hl_f[:, 2 * which + 1, bass.ds(g * J + a, 1)], None,
                                             ALU.is_equal)
                last.then_inc(done, 1)

            with nc.Block() as block:
                @block.sync
                def _(sp):
                    def load_row(g, k, s, first):
                        if not first:
                            sp.wait_ge(dup_done, g - 1)
                        sp.dma_start(idx_row[:, s, :],
                                     idx_rows[bass.ds(g, 1), :].rearrange("a e -> (a e)").partition_broadcast(P)
                                     ).then_inc(row_landed[s], 16)
                    two_slot_loop(sp, NG, [(0, load_row)])

                @block.vector
                def _(dve):
                    def count(g, k, s, first):
                        if not first:
                            dve.wait_ge(counted, g - 1)
                        build_onehots(dve, g, s, onehots)
                        if not (first and g == 0):
                            dve.wait_ge(dup_taken, g)
                        dve.tensor_copy(idx_cols[:, s, :], idx_f[:, bass.ds(g * J, J)]).then_inc(cols_taken, 1)
                        dve.wait_ge(cols_taken, g + 1)
                        dve.wait_ge(row_landed[s], 16 * (k + 1))
                        for a in range(J):
                            w = (a + 1) * P
                            last = dve.scalar_tensor_tensor(same[:, s, a, 0:w], idx_row[:, s, 0:w],
                                                            idx_cols[:, s, a:a + 1], before[:, a, 0:w],
                                                            ALU.is_equal, ALU.mult,
                                                            accum_out=dup_cols[:, a:a + 1])
                        last.then_inc(dup_done, 1)
                        dve.wait_ge(dup_done, g + 1)
                        dve.tensor_copy(dup[:, which, bass.ds(g * J, J)], dup_cols[:, :]
                                        ).then_inc(dup_taken, 1)
                    two_slot_loop(dve, NG, [(0, count)])
                    v = vec
                    add_rows = (src_add, dst_add)[which]
                    dve.wait_ge(dup_taken, NG)
                    dve.tensor_scalar(flag[:, :], dup[:, which, :], 1.0, None, ALU.min).then_inc(v, 1)
                    dve.tensor_tensor(tmp_t[:, :].rearrange("p (g a) -> p g a", a=J),
                                      spare[:, :].unsqueeze(1).to_broadcast([P, NG, J]),
                                      idx_f[:, :].rearrange("p (g a) -> p g a", a=J), ALU.subtract).then_inc(v, 1)
                    dve.wait_ge(v, 2)
                    dve.tensor_tensor(tmp_t[:, :], tmp_t[:, :], flag[:, :], ALU.mult).then_inc(v, 1)
                    dve.wait_ge(v, 3)
                    dve.tensor_tensor(add_rows[:, :], tmp_t[:, :], idx_f[:, :], ALU.add).then_inc(v, 1)
                    dve.wait_ge(hist_ready, 1)
                    if running:
                        dve.tensor_tensor_scan(hist_run[:, :], zeros[0:HI, 0:LO], hist[:, :], 0.0, ALU.add,
                                               ALU.add).then_inc(v, 1)
                        dve.wait_ge(v, 5)
                        dve.tensor_tensor(hist_base[:, :], hist_run[:, :], hist[:, :], ALU.subtract).then_inc(v, 1)
                        dve.wait_ge(off_mm, 1)
                        dve.tensor_copy(row_off[:, :], psum[1][0:HI, 0:1]).then_inc(v, 1)
                        dve.wait_ge(v, 7)
                        dve.tensor_scalar(hist_base[:, :], hist_base[:, :], row_off[:, 0:1], None,
                                          ALU.add).then_inc(v, 1)

                    def encode(g, k, s, first):
                        if not first:
                            dve.wait_ge(picked_done, J * (g - 1))
                            dve.wait_ge(turned_mm, g - 1)
                            if running:
                                dve.wait_ge(counted2, g - 1)
                        build_onehots(dve, g, s, onehots2)

                    def pick(g, k, s, first):
                        for a in range(J):
                            dve.wait_ge(row_mm, g * J + (a + 1))
                            if a == 0 and not (first and g == 0):
                                dve.wait_ge(pick_taken, g)
                            if a > 1:
                                dve.wait_ge(picked_done, g * J + (a - 1))
                            dve.tensor_tensor_reduce(picked[:, a % 2, :], psum[2 + a % 2][:, :], onehot_lo[:, s, a, :], 1.0,
                                                     0.0, ALU.mult, ALU.add,
                                                     picked_cols[:, a:a + 1]).then_inc(picked_done, 1)
                        dve.wait_ge(picked_done, J * (g + 1))
                        dve.tensor_copy(looked_up[:, which, bass.ds(g * J, J)], picked_cols[:, :]
                                        ).then_inc(pick_taken, 1)
                    two_slot_loop(dve, NG, [(0, encode), (1, pick)])
                    dve.wait_ge(pick_taken, NG)
                    if running:
                        dve.tensor_scalar(tmp_t[:, :], looked_up[:, which, :], 1.0, None, ALU.add).then_inc(v, 1)
                        dve.wait_ge(v, 9)
                        dve.tensor_tensor(sort_pos[:, :], tmp_t[:, :], dup[:, which, :], ALU.add).then_inc(v, 1)
                    else:
                        dve.tensor_scalar(tmp_t[:, :], looked_up[:, which, :], 1.0, None, ALU.max).then_inc(v, 1)
                        dve.wait_ge(v, 5)
                        dve.reciprocal(inv_count[:, :], tmp_t[:, :]).then_inc(v, 1)

                @block.scalar
                def _(act):
                    act.wait_ge(counted, NG)
                    act.activation(hist[:, :], psum[0][0:HI, :], ACT.Copy).then_inc(hist_ready, 1)
                    if running:
                        act.wait_ge(base_in, 1)

                    def take(g, k, s, first):
                        if running:
                            if not first:
                                act.wait_ge(row_mm, J * (g - 1))
                            if not (first and g == 0):
                                act.wait_ge(counted2, g)
                            act.activation(table[:, s, :], psum[0][0:HI, :], ACT.Copy).then_inc(table_ready, 1)
                        act.wait_ge(turned_mm, g + 1)
                        if not first:
                            act.wait_ge(row_mm, J * (g - 1))
                        act.activation(hi_turned[:, s, :, :].rearrange("h a p -> h (a p)"),
                                       psum[4 + s][0:HI, :].bitcast(F16)[:, 0:ROWS], ACT.Copy).then_inc(turned_ready, 1)
                    two_slot_loop(act, NG, [(0, take)])

                @block.tensor
                def _(pe):
                    def count(g, k, s, first):
                        pe.wait_ge(onehots, g + 1)
                        for a in range(J):
                            start = first and g == 0 and a == 0
                            last = pe.matmul(psum[0][0:HI, :], onehot_hi[:, s, a, :], onehot_lo[:, s, a, :],
                                             start=start, stop=False, skip_group_check=True)
                        last.then_inc(counted, 1)
                    two_slot_loop(pe, NG, [(0, count)])
                    pe.wait_ge(hist_ready, 1)
                    if running:
                        pe.wait_ge(vec, 5)
                        pe.matmul(psum[1][0:HI, 0:1], upper[0:HI, 0:HI], hist_run[:, LO - 1:LO], start=True,
                                  stop=True).then_inc(off_mm, 1)
                        pe.wait_ge(vec, 8)
                        pe.matmul(psum[0][0:HI, :], ident[0:HI, 0:HI], hist_base[:, :], start=True, stop=False,
                                  skip_group_check=True).then_inc(base_in, 1)

                    def turn(g, k, s, first):
                        pe.wait_ge(onehots2, g + 1)
                        if not first:
                            pe.wait_ge(turned_ready, g - 1)
                        for a in range(J):
                            last = pe.transpose(psum[4 + s][0:HI, :].bitcast(F16)[:, a * P:(a + 1) * P],
                                                onehot_hi[:, s, a, :], ident16[:, :])
                        last.then_inc(turned_mm, 1)
                        if running:
                            pe.wait_ge(table_ready, g + 1)
                            for a in range(J):
                                last = pe.matmul(psum[0][0:HI, :], onehot_hi[:, s, a, :], onehot_lo[:, s, a, :],
                                                 start=False, stop=False, skip_group_check=True)
                            last.then_inc(counted2, 1)

                    def rows_of(g, k, s, first):
                        pe.wait_ge(turned_ready, g + 1)
                        for a in range(J):
                            if not (first and g == 0 and a < 2):
                                pe.wait_ge(picked_done, g * J + (a - 1))
                            pe.matmul(psum[2 + a % 2][:, :], hi_turned[:, s, a, :],
                                      table[:, s, :] if running else hist[:, :], start=True,
                                      stop=True).then_inc(row_mm, 1)
                    two_slot_loop(pe, NG, [(0, turn), (1, rows_of)])
            end_phase()

        def norm_semaphores(name):
            return [sem(name + n) for n in ("_stats_done", "_var_ready", "_std_ready", "_rstd_done",
                                            "_shift_ready")]

        def norm_statistics(norm, dve, x, b, s):
            stats_done, var_ready, _, _, _ = norm
            for j in range(J):
                last = dve.bn_stats(stats[:, s, j, :], x[:, j * D:(j + 1) * D])
            last.then_inc(stats_done, 1)
            dve.wait_ge(stats_done, b + 1)
            dve.sem_inc(dve_waits, 1)
            for j in range(J):
                last = dve.bn_aggr(mean_var[:, s, j, :], stats[:, s, j, :])
            last.then_inc(var_ready, 1)

        def norm_root(norm, act, b, s):
            _, var_ready, std_ready, _, _ = norm
            act.wait_ge(var_ready, b + 1)
            act.activation(std[:, s, :], mean_var[:, s, :, 1], ACT.Sqrt, bias=eps[:, 0:1]).then_inc(std_ready, 1)

        def norm_factors(norm, dve, b, s):
            _, _, std_ready, rstd_done, shift_ready = norm
            dve.wait_ge(std_ready, b + 1)
            dve.reciprocal(rstd[:, s, :], std[:, s, :]).then_inc(rstd_done, 1)
            dve.wait_ge(rstd_done, b + 1)
            dve.scalar_tensor_tensor(shift[:, s, :], mean_var[:, s, :, 0], -1.0, rstd[:, s, :], ALU.mult,
                                     ALU.mult).then_inc(shift_ready, 1)

        def norm_apply(norm, act, out_t, x, b, s):
            _, _, _, _, shift_ready = norm
            act.wait_ge(shift_ready, b + 1)
            for j in range(J):
                last = act.activation(out_t[:, j * D:(j + 1) * D], x[:, j * D:(j + 1) * D], ACT.Relu,
                                      bias=shift[:, s, j:j + 1], scale=rstd[:, s, j:j + 1])
            return last

        def products(pe, bank, left, right, width=D):
            for j in range(J):
                last = pe.matmul(bank[:, j * width:(j + 1) * width], left[:, j * P:(j + 1) * P], right,
                                 start=True, stop=True)
            return last

        def turn_tiles(pe, bank, t):
            for j in range(J):
                last = pe.transpose(bank[:, j * P:(j + 1) * P], t[:, j * D:(j + 1) * D], ident[:, :])
            return last

        def nodes_into_layer_0():
            norm = norm_semaphores("nA")
            x_landed = sem2("nA_x_landed")
            h_stored = sem2("nA_h_stored")
            y_stored = sem2("nA_y_stored")
            h_done = sem("nA_h_done")
            turned_mm = sem("nA_turned_mm")
            ht_ready = sem("nA_ht_ready")
            y_mm = sem("nA_y_mm")
            y_done = sem("nA_y_done")

            with nc.Block() as block:
                @block.sync
                def _(sp):
                    def load(b, k, s, first):
                        if not first:
                            sp.wait_ge(h_done, b - 1)
                        sp.dma_start(T[0][:, s, :], block_rows(ins["x"], b)).then_inc(x_landed[s], 16)

                    def store(b, k, s, first):
                        sp.wait_ge(h_done, b + 1)
                        sp.dma_start(block_rows(h0, b), T[1][:, s, :]).then_inc(h_stored[s], 16)
                        sp.wait_ge(y_done, b + 1)
                        sp.dma_start(block_rows(y1, b), T[3][:, s, :]).then_inc(y_stored[s], 16)
                    two_slot_loop(sp, NB, [(0, load), (2, store)])
                    for q in h_stored + y_stored:
                        sp.wait_ge(q, 16 * (NB // 2))

                @block.vector
                def _(dve):
                    def normalise(b, k, s, first):
                        dve.wait_ge(x_landed[s], 16 * (k + 1))
                        norm_statistics(norm, dve, T[0][:, s, :], b, s)
                        if not first:
                            dve.wait_ge(h_done, b - 1)
                        norm_factors(norm, dve, b, s)

                    def finish(b, k, s, first):
                        dve.wait_ge(y_mm, b + 1)
                        if not first:
                            dve.wait_ge(y_stored[s], 16 * k)
                        dve.tensor_tensor(jd(T[3][:, s, :]), jd(psum[2 + s][:, :]), across(rows["L0_gnn_b1"][:, :]),
                                          ALU.add).then_inc(y_done, 1)
                    two_slot_loop(dve, NB, [(0, normalise), (1, finish)])

                @block.scalar
                def _(act):
                    def normalise(b, k, s, first):
                        norm_root(norm, act, b, s)
                        if not first:
                            act.wait_ge(h_stored[s], 16 * k)
                            act.wait_ge(turned_mm, b - 1)
                        norm_apply(norm, act, T[1][:, s, :], T[0][:, s, :], b, s).then_inc(h_done, 1)

                    def copy_turned(b, k, s, first):
                        act.wait_ge(turned_mm, b + 1)
                        if not first:
                            act.wait_ge(y_mm, b - 1)
                        act.activation(T[2][:, s, :], psum[s][:, :], ACT.Copy).then_inc(ht_ready, 1)
                    two_slot_loop(act, NB, [(0, normalise), (1, copy_turned)])

                @block.tensor
                def _(pe):
                    def turn(b, k, s, first):
                        pe.wait_ge(h_done, b + 1)
                        if not first:
                            pe.wait_ge(ht_ready, b - 1)
                        turn_tiles(pe, psum[s], T[1][:, s, :]).then_inc(turned_mm, 1)

                    def multiply(b, k, s, first):
                        pe.wait_ge(ht_ready, b + 1)
                        if not first:
                            pe.wait_ge(y_done, b - 1)
                        products(pe, psum[2 + s], T[2][:, s, :], weights["L0_gnn_W1r"][:, :]).then_inc(y_mm, 1)
                    two_slot_loop(pe, NB, [(0, turn), (1, multiply)])
            end_phase()

        def nodes_between_convolutions():
            y_landed = sem2("nC_y_landed")
            x_landed = sem2("nC_x_landed")
            h_stored = sem2("nC_h_stored")
            y_stored = sem2("nC_y_stored")
            h_done = sem("nC_h_done")
            xb_done = sem("nC_xb_done")
            turned_mm = sem("nC_turned_mm")
            ht_ready = sem("nC_ht_ready")
            y_mm = sem("nC_y_mm")
            y_done = sem("nC_y_done")

            with nc.Block() as block:
                @block.sync
                def _(sp):
                    def load(b, k, s, first):
                        if not first:
                            sp.wait_ge(h_done, b - 1)
                        sp.dma_start(T[0][:, s, :], block_rows(y1, b)).then_inc(y_landed[s], 16)
                        if not first:
                            sp.wait_ge(y_done, b - 1)
                        sp.dma_start(T[1][:, s, :], block_rows(ins["x"], b)).then_inc(x_landed[s], 16)

                    def store(b, k, s, first):
                        sp.wait_ge(h_done, b + 1)
                        sp.dma_start(block_rows(h1, b), T[2][:, s, :]).then_inc(h_stored[s], 16)
                        sp.wait_ge(y_done, b + 1)
                        sp.dma_start(block_rows(y2, b), T[4][:, s, :]).then_inc(y_stored[s], 16)
                    two_slot_loop(sp, NB, [(0, load), (2, store)])
                    for q in h_stored + y_stored:
                        sp.wait_ge(q, 16 * (NB // 2))

                @block.vector
                def _(dve):
                    def add_bias(b, k, s, first):
                        dve.wait_ge(x_landed[s], 16 * (k + 1))
                        dve.tensor_tensor(jd(T[1][:, s, :]), jd(T[1][:, s, :]), across(rows["L0_gnn_b2"][:, :]),
                                          ALU.add).then_inc(xb_done, 1)

                    def finish(b, k, s, first):
                        dve.wait_ge(y_mm, b + 1)
                        dve.wait_ge(xb_done, b + 1)
                        if not first:
                            dve.wait_ge(y_stored[s], 16 * k)
                        dve.tensor_tensor(T[4][:, s, :], psum[2 + s][:, :], T[1][:, s, :],
                                          ALU.add).then_inc(y_done, 1)
                    two_slot_loop(dve, NB, [(0, add_bias), (1, finish)])

                @block.scalar
                def _(act):
                    def relu(b, k, s, first):
                        act.wait_ge(y_landed[s], 16 * (k + 1))
                        if not first:
                            act.wait_ge(h_stored[s], 16 * k)
                            act.wait_ge(turned_mm, b - 1)
                        act.activation(T[2][:, s, :], T[0][:, s, :], ACT.Relu).then_inc(h_done, 1)

                    def copy_turned(b, k, s, first):
                        act.wait_ge(turned_mm, b + 1)
                        if not first:
                            act.wait_ge(y_mm, b - 1)
                        act.activation(T[3][:, s, :], psum[s][:, :], ACT.Copy).then_inc(ht_ready, 1)
                    two_slot_loop(act, NB, [(0, relu), (1, copy_turned)])

                @block.tensor
                def _(pe):
                    def turn(b, k, s, first):
                        pe.wait_ge(h_done, b + 1)
                        if not first:
                            pe.wait_ge(ht_ready, b - 1)
                        turn_tiles(pe, psum[s], T[2][:, s, :]).then_inc(turned_mm, 1)

                    def multiply(b, k, s, first):
                        pe.wait_ge(ht_ready, b + 1)
                        if not first:
                            pe.wait_ge(y_done, b - 1)
                        products(pe, psum[2 + s], T[3][:, s, :], weights["L0_gnn_W2r"][:, :]).then_inc(y_mm, 1)
                    two_slot_loop(pe, NB, [(0, turn), (1, multiply)])
            end_phase()

        def nodes_into_layer_1():
            norm = norm_semaphores("nE")
            x_landed = sem2("nE_x_landed")
            h_stored = sem2("nE_h_stored")
            xh_stored = sem2("nE_xh_stored")
            xb_done = sem("nE_xb_done")
            h_done = sem("nE_h_done")
            xh_done = sem("nE_xh_done")

            with nc.Block() as block:
                @block.sync
                def _(sp):
                    def load(b, k, s, first):
                        if not first:
                            sp.wait_ge(h_done, b - 1)
                            sp.wait_ge(xb_done, b - 1)
                        sp.dma_start(T[0][:, s, :], block_rows(y2, b)).then_inc(x_landed[s], 16)

                    def store(b, k, s, first):
                        sp.wait_ge(h_done, b + 1)
                        sp.dma_start(block_rows(h2, b), T[1][:, s, :]).then_inc(h_stored[s], 16)
                        sp.wait_ge(xh_done, b + 1)
                        sp.dma_start(block_rows(x1h, b), T[3][:, s, :]).then_inc(xh_stored[s], 16)
                    two_slot_loop(sp, NB, [(0, load), (2, store)])
                    for q in h_stored + xh_stored:
                        sp.wait_ge(q, 16 * (NB // 2))

                @block.vector
                def _(dve):
                    def normalise(b, k, s, first):
                        dve.wait_ge(x_landed[s], 16 * (k + 1))
                        norm_statistics(norm, dve, T[0][:, s, :], b, s)
                        if not first:
                            dve.wait_ge(h_done, b - 1)
                        norm_factors(norm, dve, b, s)
                        dve.tensor_tensor(jd(T[2][:, s, :]), jd(T[0][:, s, :]), across(rows["L1_gnn_bn2"][:, :]),
                                          ALU.add).then_inc(xb_done, 1)

                    def finish(b, k, s, first):
                        dve.wait_ge(h_done, b + 1)
                        dve.wait_ge(xb_done, b + 1)
                        if not first:
                            dve.wait_ge(xh_stored[s], 16 * k)
                        dve.tensor_tensor(T[3][:, s, :], T[2][:, s, :], T[1][:, s, :],
                                          ALU.add).then_inc(xh_done, 1)
                    two_slot_loop(dve, NB, [(0, normalise), (1, finish)])

                @block.scalar
                def _(act):
                    def normalise(b, k, s, first):
                        norm_root(norm, act, b, s)
                        if not first:
                            act.wait_ge(h_stored[s], 16 * k)
                            act.wait_ge(xh_done, b - 1)
                        norm_apply(norm, act, T[1][:, s, :], T[0][:, s, :], b, s).then_inc(h_done, 1)
                    two_slot_loop(act, NB, [(0, normalise)])
            end_phase()

        def nodes_into_layer_2():
            norm = norm_semaphores("nG")
            z_landed = sem2("nG_z_landed")
            x_landed = sem2("nG_x_landed")
            x2_stored = sem2("nG_x2_stored")
            h_stored = sem2("nG_h_stored")
            y_stored = sem2("nG_y_stored")
            silu_done = sem("nG_silu_done")
            silu_turned = sem("nG_silu_turned")
            st_ready = sem("nG_st_ready")
            x2_mm = sem("nG_x2_mm")
            x2_done = sem("nG_x2_done")
            h_done = sem("nG_h_done")
            h_turned = sem("nG_h_turned")
            ht_ready = sem("nG_ht_ready")
            y_mm = sem("nG_y_mm")
            y_done = sem("nG_y_done")

            with nc.Block() as block:
                @block.sync
                def _(sp):
                    def load(b, k, s, first):
                        if not first:
                            sp.wait_ge(silu_done, b - 1)
                        sp.dma_start(T[0][:, s, :], block_rows(z1, b)).then_inc(z_landed[s], 16)
                        if not first:
                            sp.wait_ge(x2_done, b - 1)
                        sp.dma_start(T[1][:, s, :], block_rows(x1h, b)).then_inc(x_landed[s], 16)

                    def store(b, k, s, first):
                        sp.wait_ge(x2_done, b + 1)
                        sp.dma_start(block_rows(x2, b), T[4][:, s, :]).then_inc(x2_stored[s], 16)
                        sp.wait_ge(h_done, b + 1)
                        sp.dma_start(block_rows(h3, b), T[5][:, s, :]).then_inc(h_stored[s], 16)
                        sp.wait_ge(y_done, b + 1)
                        sp.dma_start(block_rows(y3, b), T[7][:, s, :]).then_inc(y_stored[s], 16)
                    two_slot_loop(sp, NB, [(0, load), (2, store)])
                    for q in x2_stored + h_stored + y_stored:
                        sp.wait_ge(q, 16 * (NB // 2))

                @block.vector
                def _(dve):
                    def middle(b, k, s, first):
                        dve.wait_ge(x2_mm, b + 1)
                        dve.wait_ge(x_landed[s], 16 * (k + 1))
                        if not first:
                            dve.wait_ge(x2_stored[s], 16 * k)
                            dve.wait_ge(h_done, b - 1)
                        dve.tensor_tensor(T[4][:, s, :], psum[2 + s][:, :], T[1][:, s, :],
                                          ALU.add).then_inc(x2_done, 1)
                        dve.wait_ge(x2_done, b + 1)
                        norm_statistics(norm, dve, T[4][:, s, :], b, s)
                        norm_factors(norm, dve, b, s)

                    def finish(b, k, s, first):
                        dve.wait_ge(y_mm, b + 1)
                        if not first:
                            dve.wait_ge(y_stored[s], 16 * k)
                        dve.tensor_tensor(jd(T[7][:, s, :]), jd(psum[6][:, :]), across(c2[:, :]),
                                          ALU.add).then_inc(y_done, 1)
                    two_slot_loop(dve, NB, [(1, middle), (2, finish)])

                @block.scalar
                def _(act):
                    def silu(b, k, s, first):
                        act.wait_ge(z_landed[s], 16 * (k + 1))
                        if not first:
                            act.wait_ge(silu_turned, b - 1)
                        act.activation(T[2][:, s, :], T[0][:, s, :], ACT.Silu).then_inc(silu_done, 1)
                        act.wait_ge(silu_turned, b + 1)
                        if not first:
                            act.wait_ge(x2_mm, b - 1)
                        act.activation(T[3][:, s, :], psum[s][:, :], ACT.Copy).then_inc(st_ready, 1)

                    def normalise(b, k, s, first):
                        norm_root(norm, act, b, s)
                        if not first:
                            act.wait_ge(h_stored[s], 16 * k)
                            act.wait_ge(h_turned, b - 1)
                        norm_apply(norm, act, T[5][:, s, :], T[4][:, s, :], b, s).then_inc(h_done, 1)

                    def copy_turned(b, k, s, first):
                        act.wait_ge(h_turned, b + 1)
                        if not first:
                            act.wait_ge(y_mm, b - 1)
                        act.activation(T[6][:, s, :], psum[4 + s][:, :], ACT.Copy).then_inc(ht_ready, 1)
                    two_slot_loop(act, NB, [(0, silu), (1, normalise), (1, copy_turned)])

                @block.tensor
                def _(pe):
                    def turn_silu(b, k, s, first):
                        pe.wait_ge(silu_done, b + 1)
                        if not first:
                            pe.wait_ge(st_ready, b - 1)
                        turn_tiles(pe, psum[s], T[2][:, s, :]).then_inc(silu_turned, 1)
                        pe.wait_ge(st_ready, b + 1)
                        if not first:
                            pe.wait_ge(x2_done, b - 1)
                        products(pe, psum[2 + s], T[3][:, s, :], weights["L1_gnn_Wn2"][:, :]).then_inc(x2_mm, 1)

                    def turn_h(b, k, s, first):
                        pe.wait_ge(h_done, b + 1)
                        if not first:
                            pe.wait_ge(ht_ready, b - 1)
                        turn_tiles(pe, psum[4 + s], T[5][:, s, :]).then_inc(h_turned, 1)
                        pe.wait_ge(ht_ready, b + 1)
                        if not (first and b == 0):
                            pe.wait_ge(y_done, b)
                        products(pe, psum[6], T[6][:, s, :], w_2[:, 0, :]).then_inc(y_mm, 1)
                    two_slot_loop(pe, NB, [(0, turn_silu), (1, turn_h)])
            end_phase()

        def nodes_into_layer_3():
            norm = norm_semaphores("nI")
            y_landed = sem2("nI_y_landed")
            x_landed = sem2("nI_x_landed")
            h_stored = sem2("nI_h_stored")
            o_stored = sem2("nI_o_stored")
            x3_done = sem("nI_x3_done")
            h_done = sem("nI_h_done")
            o_done = sem("nI_o_done")

            with nc.Block() as block:
                @block.sync
                def _(sp):
                    def load(b, k, s, first):
                        if not first:
                            sp.wait_ge(x3_done, b - 1)
                        sp.dma_start(T[0][:, s, :], block_rows(y3, b)).then_inc(y_landed[s], 16)
                        sp.dma_start(T[1][:, s, :], block_rows(x2, b)).then_inc(x_landed[s], 16)

                    def store(b, k, s, first):
                        sp.wait_ge(h_done, b + 1)
                        sp.dma_start(block_rows(h4, b), T[3][:, s, :]).then_inc(h_stored[s], 16)
                        sp.wait_ge(o_done, b + 1)
                        sp.dma_start(block_rows(out, b), T[4][:, s, :]).then_inc(o_stored[s], 16)
                    two_slot_loop(sp, NB, [(0, load), (2, store)])
                    for q in h_stored + o_stored:
                        sp.wait_ge(q, 16 * (NB // 2))

                @block.vector
                def _(dve):
                    def normalise(b, k, s, first):
                        dve.wait_ge(y_landed[s], 16 * (k + 1))
                        dve.wait_ge(x_landed[s], 16 * (k + 1))
                        if not first:
                            dve.wait_ge(h_done, b - 1)
                            dve.wait_ge(o_done, b - 1)
                        dve.scalar_tensor_tensor(T[2][:, s, :], T[0][:, s, :], 0.0, T[1][:, s, :], ALU.max,
                                                 ALU.add).then_inc(x3_done, 1)
                        dve.wait_ge(x3_done, b + 1)
                        norm_statistics(norm, dve, T[2][:, s, :], b, s)
                        norm_factors(norm, dve, b, s)

                    def finish(b, k, s, first):
                        if not first:
                            dve.wait_ge(o_stored[s], 16 * k)
                        dve.tensor_tensor(jd(T[4][:, s, :]), jd(T[2][:, s, :]), across(rows["L3_gnn_bout"][:, :]),
                                          ALU.add).then_inc(o_done, 1)
                    two_slot_loop(dve, NB, [(0, normalise), (1, finish)])

                @block.scalar
                def _(act):
                    def normalise(b, k, s, first):
                        norm_root(norm, act, b, s)
                        if not first:
                            act.wait_ge(h_stored[s], 16 * k)
                        norm_apply(norm, act, T[3][:, s, :], T[2][:, s, :], b, s).then_inc(h_done, 1)
                    two_slot_loop(act, NB, [(0, normalise)])
            end_phase()

        def summed_edges(name, which, into, weight, messages, scaled=False):

            idx_f = (src_f, dst_f)[which]
            idx_rows = (ins["src_rows"], ins["dst_rows"])[which]
            add_rows = (src_add, dst_add)[which]
            row_landed = sem2(name + "_row_landed")
            same_ready = sem(name + "_same_ready")
            sum_mm = sem(name + "_sum_mm")
            sum_ready = sem(name + "_sum_ready")
            out_mm = sem(name + "_out_mm")
            out_done = sem(name + "_out_done")
            add_to_ready = sem(name + "_add_to_ready")
            added = sem2(name + "_added")

            def load_row(sp, g, k, s, first):
                if not first:
                    sp.wait_ge(same_ready, g - 1)
                sp.dma_start(idx_row[:, s, :],
                             idx_rows[bass.ds(g, 1), :].rearrange("a e -> (a e)").partition_broadcast(P)
                             ).then_inc(row_landed[s], 16)

            def compare(dve, g, k, s, first):
                dve.wait_ge(row_landed[s], 16 * (k + 1))
                if not first:
                    dve.wait_ge(sum_mm, g - 1)
                for a in range(J):
                    last = dve.tensor_scalar(same[:, s, a, :], idx_row[:, s, :],
                                             idx_f[:, bass.ds(g * J + a, 1)], None, ALU.is_equal)
                last.then_inc(same_ready, 1)

            def sum_equal(pe, g, k, s, first):
                pe.wait_ge(same_ready, g + 1)
                if not first:
                    pe.wait_ge(sum_ready, g - 1)
                for a in range(J):
                    last = pe.matmul(psum[s][:, :], messages[:, s, a * D:(a + 1) * D], same[:, s, a, :],
                                     start=(a == 0), stop=(a == J - 1))
                last.then_inc(sum_mm, 1)

            def copy_sum(act, g, k, s, first):
                act.wait_ge(sum_mm, g + 1)
                if not first:
                    act.wait_ge(out_mm, g - 1)
                act.activation(T[2][:, s, :], psum[s][:, :], ACT.Copy).then_inc(sum_ready, 1)

            def copy_rows(act, g, k, s, first):
                if not first:
                    act.wait_ge(added[s], 16 * J * k)
                act.activation(add_to[:, s, :], add_rows[:, bass.ds(g * J, J)],
                               ACT.Copy).then_inc(add_to_ready, 1)

            def multiply(pe, g, k, s, first):
                pe.wait_ge(sum_ready, g + 1)
                if not first:
                    pe.wait_ge(out_done, g - 1)
                products(pe, psum[2 + s], T[2][:, s, :], weight).then_inc(out_mm, 1)

            def take_out(dve, g, k, s, first):
                dve.wait_ge(out_mm, g + 1)
                if not first:
                    dve.wait_ge(added[s], 16 * J * k)
                if scaled:
                    dve.tensor_tensor(jd(T[3][:, s, :]), jd(psum[2 + s][:, :]),
                                      inv_count[:, bass.ds(g * J, J)].unsqueeze(2).to_broadcast([P, J, D]),
                                      ALU.mult).then_inc(out_done, 1)
                else:
                    dve.tensor_copy(T[3][:, s, :], psum[2 + s][:, :]).then_inc(out_done, 1)

            def add(pool, g, k, s, first):
                wait_on_pool(pool, out_done, g + 1)
                wait_on_pool(pool, add_to_ready, g + 1)
                if not (first and g == 0):
                    wait_on_pool(pool, added[1 - s], 16 * J * (k + s))
                for a in range(J):
                    pool.indirect_dma_start(into, bass.IndirectOffsetOnAxis(ap=add_to[:, s, a:a + 1], axis=0),
                                            T[3][:, s, a * D:(a + 1) * D], None,
                                            compute_op=ALU.add).then_inc(added[s], 16)

            def all_added(pool):
                for q in added:
                    pool.wait_ge(q, 16 * J * (NG // 2))

            return (load_row, compare, sum_equal, copy_sum, copy_rows, multiply, take_out, add, all_added,
                    sum_mm)

        def load_index(sp, idx, name, landed, used, per_group, g, k, s, first):
            if not first:
                sp.wait_ge(used[s], 16 * per_group * k)
            sp.dma_start(idx[:, s, :],
                         ins[name][bass.ds(g, 1), :, :].rearrange("a p j -> (a p) j")).then_inc(landed[s], 16)

        def gather(pool, into, idx, s, table_ap, done):
            for a in range(J):
                pool.indirect_dma_start(into[:, s, a * D:(a + 1) * D], None, table_ap,
                                        bass.IndirectOffsetOnAxis(ap=idx[:, s, a:a + 1], axis=0)).then_inc(done, 16)

        def edges_convolution(name, h, y, weight, fill=None):
            (edge_load_row, edge_compare, edge_sum_equal, edge_copy_sum, edge_copy_rows, edge_multiply,
             edge_take_out, edge_add, edge_all_added, edge_sum_mm) = summed_edges(name, 1, y, weight, T[0], scaled=True)
            idx_landed = sem2(name + "_idx_landed")
            gathered = sem2(name + "_gathered")
            filled = sem(name + "_filled")

            with nc.Block() as block:
                @block.sync
                def _(sp):
                    def load(g, k, s, first):
                        load_index(sp, gather_a, "src_groups", idx_landed, gathered, J, g, k, s, first)
                        edge_load_row(sp, g, k, s, first)
                        if fill is not None:
                            for n in range(2):
                                if n * NG + NG <= NB:
                                    sp.dma_start(block_rows(fill, g + n * NG),
                                                 z_init[:, :]).then_inc(filled, 16)
                    two_slot_loop(sp, NG, [(0, load)])
                    if fill is not None:
                        done = NG
                        for b in range(NG, NB):
                            sp.dma_start(block_rows(fill, b), z_init[:, :]).then_inc(filled, 16)
                        sp.wait_ge(filled, 16 * NB)

                @block.gpsimd
                def _(pool):
                    def fetch(g, k, s, first):
                        wait_on_pool(pool, idx_landed[s], 16 * (k + 1))
                        if not first:
                            wait_on_pool(pool, edge_sum_mm, g - 1)
                        gather(pool, T[0], gather_a, s, h, gathered[s])

                    def add(g, k, s, first):
                        edge_add(pool, g, k, s, first)
                    two_slot_loop(pool, NG, [(0, fetch), (2, add)])
                    edge_all_added(pool)

                @block.vector
                def _(dve):
                    def compare(g, k, s, first):
                        edge_compare(dve, g, k, s, first)

                    def take_out(g, k, s, first):
                        edge_take_out(dve, g, k, s, first)
                    two_slot_loop(dve, NG, [(0, compare), (1, take_out)])

                @block.scalar
                def _(act):
                    def copy_sum(g, k, s, first):
                        edge_copy_sum(act, g, k, s, first)

                    def copy_rows(g, k, s, first):
                        edge_copy_rows(act, g, k, s, first)
                    two_slot_loop(act, NG, [(0, copy_sum), (1, copy_rows)])

                @block.tensor
                def _(pe):
                    def sum_equal(g, k, s, first):
                        pe.wait_ge(gathered[s], 16 * J * (k + 1))
                        edge_sum_equal(pe, g, k, s, first)

                    def multiply(g, k, s, first):
                        edge_multiply(pe, g, k, s, first)
                    two_slot_loop(pe, NG, [(0, sum_equal), (1, multiply)])
            end_phase()

        def edges_layer_1():
            (edge_load_row, edge_compare, edge_sum_equal, edge_copy_sum, edge_copy_rows, edge_multiply,
             edge_take_out, edge_add, edge_all_added, edge_sum_mm) = summed_edges("eF", 1, z1, weights["L1_gnn_Wn1"][:, :], T[1])
            idx_landed = sem2("eF_idx_landed")
            gathered = sem2("eF_gathered")
            ea_landed = sem2("eF_ea_landed")
            hid_mm = sem("eF_hid_mm")
            hid_ready = sem("eF_hid_ready")
            ew_mm = sem("eF_ew_mm")
            ew_done = sem("eF_ew_done")
            msg_done = sem("eF_msg_done")

            with nc.Block() as block:
                @block.sync
                def _(sp):
                    def load(g, k, s, first):
                        load_index(sp, gather_a, "src_groups", idx_landed, gathered, J, g, k, s, first)
                        edge_load_row(sp, g, k, s, first)
                        if not first:
                            sp.wait_ge(hid_mm, g - 1)
                        sp.dma_start(T[4][0:50, s, :], ins["edge50"][:, bass.ds(g * ROWS, ROWS)]
                                     ).then_inc(ea_landed[s], 16)
                    two_slot_loop(sp, NG, [(0, load)])

                @block.gpsimd
                def _(pool):
                    def fetch(g, k, s, first):
                        wait_on_pool(pool, idx_landed[s], 16 * (k + 1))
                        if not first:
                            wait_on_pool(pool, msg_done, g - 1)
                        gather(pool, T[0], gather_a, s, h2, gathered[s])

                    def add(g, k, s, first):
                        edge_add(pool, g, k, s, first)
                    two_slot_loop(pool, NG, [(0, fetch), (2, add)])
                    edge_all_added(pool)

                @block.vector
                def _(dve):
                    def compare(g, k, s, first):
                        edge_compare(dve, g, k, s, first)

                    def message(g, k, s, first):
                        dve.wait_ge(ew_mm, g + 1)
                        dve.tensor_tensor(jd(T[6][:, s, :]), jd(psum[5][:, :]), across(rows["L1_gnn_be2"][:, :]),
                                          ALU.add).then_inc(ew_done, 1)
                        dve.wait_ge(ew_done, g + 1)
                        dve.wait_ge(gathered[s], 16 * J * (k + 1))
                        if not first:
                            dve.wait_ge(edge_sum_mm, g - 1)
                        dve.tensor_tensor(T[1][:, s, :], T[0][:, s, :], T[6][:, s, :],
                                          ALU.mult).then_inc(msg_done, 1)

                    def take_out(g, k, s, first):
                        edge_take_out(dve, g, k, s, first)
                    two_slot_loop(dve, NG, [(0, compare), (1, take_out), (0, message)])

                @block.scalar
                def _(act):
                    def silu(g, k, s, first):
                        act.wait_ge(hid_mm, g + 1)
                        if not first:
                            act.wait_ge(ew_mm, g - 1)
                        act.activation(T[5][:, s, :], psum[4][:, :], ACT.Silu,
                                       bias=be1[:, 0:1]).then_inc(hid_ready, 1)

                    def copy_sum(g, k, s, first):
                        edge_copy_sum(act, g, k, s, first)

                    def copy_rows(g, k, s, first):
                        edge_copy_rows(act, g, k, s, first)
                    two_slot_loop(act, NG, [(0, silu), (1, copy_sum), (1, copy_rows)])

                @block.tensor
                def _(pe):
                    def hidden(g, k, s, first):
                        pe.wait_ge(ea_landed[s], 16 * (k + 1))
                        if not (first and g == 0):
                            pe.wait_ge(hid_ready, g)
                        pe.matmul(psum[4][:, :], w_e1[:, :], T[4][0:50, s, :], start=True,
                                  stop=True).then_inc(hid_mm, 1)

                    def edge_weight(g, k, s, first):
                        pe.wait_ge(hid_ready, g + 1)
                        if not (first and g == 0):
                            pe.wait_ge(ew_done, g)
                        products(pe, psum[5], T[5][:, s, :], weights["L1_gnn_We2"][:, :]).then_inc(ew_mm, 1)

                    def sum_equal(g, k, s, first):
                        pe.wait_ge(msg_done, g + 1)
                        edge_sum_equal(pe, g, k, s, first)

                    def multiply(g, k, s, first):
                        edge_multiply(pe, g, k, s, first)
                    two_slot_loop(pe, NG, [(0, hidden), (1, sum_equal), (0, edge_weight), (1, multiply)])
            end_phase()

        def edges_layer_2():
            (edge_load_row, edge_compare, edge_sum_equal, edge_copy_sum, edge_copy_rows, edge_multiply,
             edge_take_out, edge_add, edge_all_added, edge_sum_mm) = summed_edges("eH", 1, y3, w_2[:, 1, :], T[1])
            a_landed = sem2("eH_src_idx_landed")
            b_landed = sem2("eH_dst_idx_landed")
            got_a = sem2("eH_src_gathered")
            got_b = sem2("eH_dst_gathered")
            ea_landed = sem2("eH_ea_landed")
            turned_mm = sem("eH_turned_mm")
            turned_ready = sem("eH_turned_ready")
            pre_mm = sem("eH_pre_mm")
            pre_done = sem("eH_pre_done")
            msg_done = sem("eH_msg_done")

            with nc.Block() as block:
                @block.sync
                def _(sp):
                    def load(g, k, s, first):
                        load_index(sp, gather_a, "src_groups", a_landed, got_a, J, g, k, s, first)
                        load_index(sp, gather_b, "dst_groups", b_landed, got_b, J, g, k, s, first)
                        edge_load_row(sp, g, k, s, first)
                        if not first:
                            sp.wait_ge(pre_mm, g - 1)
                        sp.dma_start(T[5][:, s, :], ins["edge128"][:, bass.ds(g * ROWS, ROWS)]
                                     ).then_inc(ea_landed[s], 16)
                    two_slot_loop(sp, NG, [(0, load)])

                @block.gpsimd
                def _(pool):
                    def fetch(g, k, s, first):
                        wait_on_pool(pool, a_landed[s], 16 * (k + 1))
                        wait_on_pool(pool, b_landed[s], 16 * (k + 1))
                        if not first:
                            wait_on_pool(pool, turned_mm, g - 1)
                        gather(pool, T[0], gather_a, s, h3, got_a[s])
                        gather(pool, T[4], gather_b, s, h3, got_b[s])

                    def add(g, k, s, first):
                        edge_add(pool, g, k, s, first)
                    two_slot_loop(pool, NG, [(0, fetch), (2, add)])
                    edge_all_added(pool)

                @block.vector
                def _(dve):
                    def compare(g, k, s, first):
                        edge_compare(dve, g, k, s, first)

                    def message(g, k, s, first):
                        dve.wait_ge(pre_mm, g + 1)
                        if not first:
                            dve.wait_ge(edge_sum_mm, g - 1)
                        dve.tensor_tensor(jd(T[1][:, s, :]), jd(psum[6][:, :]), across(c1[:, :]),
                                          ALU.add).then_inc(pre_done, 1)
                        dve.wait_ge(pre_done, g + 1)
                        dve.tensor_scalar(T[1][:, s, :], T[1][:, s, :], 0.0, None, ALU.max).then_inc(msg_done, 1)

                    def take_out(g, k, s, first):
                        edge_take_out(dve, g, k, s, first)
                    two_slot_loop(dve, NG, [(0, compare), (1, take_out), (0, message)])

                @block.scalar
                def _(act):
                    def copy_turned(g, k, s, first):
                        act.wait_ge(turned_mm, g + 1)
                        if not first:
                            act.wait_ge(pre_mm, g - 1)
                        act.activation(T[6][:, s, :], psum[4][:, :], ACT.Copy)
                        act.activation(T[7][:, s, :], psum[5][:, :], ACT.Copy).then_inc(turned_ready, 1)

                    def copy_sum(g, k, s, first):
                        edge_copy_sum(act, g, k, s, first)

                    def copy_rows(g, k, s, first):
                        edge_copy_rows(act, g, k, s, first)
                    two_slot_loop(act, NG, [(0, copy_turned), (1, copy_sum), (1, copy_rows)])

                @block.tensor
                def _(pe):
                    def turn(g, k, s, first):
                        pe.wait_ge(got_a[s], 16 * J * (k + 1))
                        if not (first and g == 0):
                            pe.wait_ge(turned_ready, g)
                        turn_tiles(pe, psum[4], T[0][:, s, :])
                        pe.wait_ge(got_b[s], 16 * J * (k + 1))
                        turn_tiles(pe, psum[5], T[4][:, s, :]).then_inc(turned_mm, 1)

                    def pre(g, k, s, first):
                        pe.wait_ge(turned_ready, g + 1)
                        pe.wait_ge(ea_landed[s], 16 * (k + 1))
                        if not (first and g == 0):
                            pe.wait_ge(pre_done, g)
                        for j in range(J):
                            o = psum[6][:, j * D:(j + 1) * D]
                            c = slice(j * P, (j + 1) * P)
                            pe.matmul(o, T[7][:, s, c], w_1[:, 0, :], start=True, stop=False)
                            pe.matmul(o, T[6][:, s, c], w_1[:, 1, :], start=False, stop=False)
                            last = pe.matmul(o, T[5][:, s, c], w_1[:, 2, :], start=False, stop=True)
                        last.then_inc(pre_mm, 1)

                    def sum_equal(g, k, s, first):
                        pe.wait_ge(msg_done, g + 1)
                        edge_sum_equal(pe, g, k, s, first)

                    def multiply(g, k, s, first):
                        edge_multiply(pe, g, k, s, first)
                    two_slot_loop(pe, NG, [(0, turn), (1, sum_equal), (0, pre), (1, multiply)])
            end_phase()

        def edges_scores():
            a_landed = sem2("eJ_src_idx_landed")
            b_landed = sem2("eJ_dst_idx_landed")
            got_a = sem2("eJ_src_gathered")
            got_b = sem2("eJ_dst_gathered")
            ea_landed = sem2("eJ_ea_landed")
            turned_mm = sem("eJ_turned_mm")
            turned_ready = sem("eJ_turned_ready")
            q_mm = sem("eJ_q_mm")
            kv_mm = sem("eJ_kv_mm")
            kv_ready = sem("eJ_kv_ready")
            v_stored = sem2("eJ_v_stored")
            qk_done = sem("eJ_qk_done")
            vec = sem("eJ_vec")
            score_done = sem("eJ_score_done")
            place_ready = sem("eJ_place_ready")
            placed = sem2("eJ_placed")

            with nc.Block() as block:
                @block.sync
                def _(sp):
                    def load(g, k, s, first):
                        load_index(sp, gather_a, "src_groups", a_landed, got_a, J, g, k, s, first)
                        load_index(sp, gather_b, "dst_groups", b_landed, got_b, J, g, k, s, first)
                        if not first:
                            sp.wait_ge(kv_mm, g - 1)
                        sp.dma_start(T[5][:, s, :], ins["edge128"][:, bass.ds(g * ROWS, ROWS)]
                                     ).then_inc(ea_landed[s], 16)

                    def store(g, k, s, first):
                        sp.wait_ge(kv_ready, g + 1)
                        sp.dma_start(values[bass.ds(g, 1), :, :].rearrange("a p n -> (a p) n"), T[2][:, s, :]
                                     ).then_inc(v_stored[s], 16)
                    two_slot_loop(sp, NG, [(0, load), (1, store)])
                    for q in v_stored:
                        sp.wait_ge(q, 16 * (NG // 2))

                @block.gpsimd
                def _(pool):
                    def fetch(g, k, s, first):
                        wait_on_pool(pool, a_landed[s], 16 * (k + 1))
                        wait_on_pool(pool, b_landed[s], 16 * (k + 1))
                        if not first:
                            wait_on_pool(pool, turned_mm, g - 1)
                        gather(pool, T[0], gather_a, s, h4, got_a[s])
                        gather(pool, T[4], gather_b, s, h4, got_b[s])

                    def place(g, k, s, first):
                        wait_on_pool(pool, score_done, g + 1)
                        wait_on_pool(pool, place_ready, g + 1)
                        for a in range(J):
                            pool.indirect_dma_start(sorted_scores,
                                                    bass.IndirectOffsetOnAxis(ap=add_to[:, s, a:a + 1], axis=0),
                                                    score[:, s, a, :], None).then_inc(placed[s], 16)
                    two_slot_loop(pool, NG, [(0, fetch), (2, place)])
                    for q in placed:
                        pool.wait_ge(q, 16 * J * (NG // 2))

                @block.vector
                def _(dve):
                    def scores(g, k, s, first):
                        dve.wait_ge(q_mm, g + 1)
                        dve.wait_ge(kv_ready, g + 1)
                        dve.tensor_tensor(T[3][:, s, :], psum[6][:, :], T[1][:, s, :],
                                          ALU.mult).then_inc(qk_done, 1)
                        dve.wait_ge(qk_done, g + 1)
                        dve.tensor_reduce(qk_sum[:, s, :], T[3][:, s, :].rearrange("p (n d) -> p n d", d=HEAD_DIM),
                                          AX_X, ALU.add).then_inc(vec, 1)
                        dve.wait_ge(vec, g * 2 + 1)
                        for j in range(J):
                            last = dve.tensor_tensor(
                                mixed[:, j * 64:(j + 1) * 64].rearrange("p (o h) -> p o h", h=HEADS),
                                qk_sum[:, s, j * HEADS:(j + 1) * HEADS].unsqueeze(1).to_broadcast([P, HEADS, HEADS]),
                                w_exp[:, :].rearrange("p (o h) -> p o h", h=HEADS), ALU.mult)
                        last.then_inc(vec, 1)
                        dve.wait_ge(vec, g * 2 + 2)
                        if not first:
                            dve.wait_ge(placed[s], 16 * J * k)
                        dve.tensor_reduce(score[:, s, :, 0:HEADS],
                                          mixed[:, :].rearrange("p (j o h) -> p j o h", j=J, h=HEADS), AX_X, ALU.add)
                        dve.tensor_copy(score[:, s, :, HEADS], src_f[:, bass.ds(g * J, J)]
                                        ).then_inc(score_done, 1)
                    two_slot_loop(dve, NG, [(1, scores)])

                @block.scalar
                def _(act):
                    def copy_turned(g, k, s, first):
                        act.wait_ge(turned_mm, g + 1)
                        if not first:
                            act.wait_ge(kv_mm, g - 1)
                        act.activation(T[6][:, s, :], psum[4][:, :], ACT.Copy)
                        act.activation(T[7][:, s, :], psum[5][:, :], ACT.Copy).then_inc(turned_ready, 1)

                    def copy_kv(g, k, s, first):
                        act.wait_ge(kv_mm, g + 1)
                        if not first:
                            act.wait_ge(qk_done, g - 1)
                            act.wait_ge(v_stored[s], 16 * k)
                        for n in range(2):
                            kv = psum[2 + n][:, :].rearrange("p (j w d) -> p j w d", j=2, w=2)
                            act.activation(T[1][:, s, n * 2 * D:(n + 1) * 2 * D].rearrange("p (j d) -> p j d", j=2),
                                           kv[:, :, 0, :], ACT.Copy, scale=SCALE)
                            last = act.activation(
                                T[2][:, s, n * 2 * D:(n + 1) * 2 * D].rearrange("p (j d) -> p j d", j=2),
                                kv[:, :, 1, :], ACT.Copy)
                        last.then_inc(kv_ready, 1)
                        if not first:
                            act.wait_ge(placed[s], 16 * J * k)
                        act.activation(add_to[:, s, :], sort_pos[:, bass.ds(g * J, J)],
                                       ACT.Copy).then_inc(place_ready, 1)
                    two_slot_loop(act, NG, [(0, copy_turned), (1, copy_kv)])

                @block.tensor
                def _(pe):
                    def turn(g, k, s, first):
                        pe.wait_ge(got_a[s], 16 * J * (k + 1))
                        if not (first and g == 0):
                            pe.wait_ge(turned_ready, g)
                        turn_tiles(pe, psum[4], T[0][:, s, :])
                        pe.wait_ge(got_b[s], 16 * J * (k + 1))
                        turn_tiles(pe, psum[5], T[4][:, s, :]).then_inc(turned_mm, 1)

                    def project(g, k, s, first):
                        pe.wait_ge(turned_ready, g + 1)
                        if not (first and g == 0):
                            pe.wait_ge(qk_done, g)
                        products(pe, psum[6], T[6][:, s, :], weights["L3_gnn_Wq"][:, :]).then_inc(q_mm, 1)
                        pe.wait_ge(ea_landed[s], 16 * (k + 1))
                        if not (first and g == 0):
                            pe.wait_ge(kv_ready, g)
                        for j in range(J):
                            o = psum[2 + j // 2][:, (j % 2) * 2 * D:(j % 2 + 1) * 2 * D]
                            c = slice(j * P, (j + 1) * P)
                            pe.matmul(o, T[7][:, s, c], w_kv[:, :], start=True, stop=False)
                            last = pe.matmul(o, T[5][:, s, c], w_ekv[:, :], start=False, stop=True)
                        last.then_inc(kv_mm, 1)
                    two_slot_loop(pe, NG, [(0, turn), (1, project)])
            end_phase()

        def softmax_by_source():
            landed = sem("sm_landed")
            v = sem("sm_v")
            turned_mm = sem("sm_turned")
            back = sem("sm_back")
            exp_done = sem("sm_exp_done")
            diff_done = sem("sm_diff_done")
            stored = sem("sm_stored")
            done = sem("sm_done")
            ask = sem("sm_ask")
            ask_back = sem("sm_ask_back")

            with nc.Block() as block:
                @block.sync
                def _(sp):
                    main = sorted_scores[1:EDGES + 1, :].rearrange("(p n) c -> p n c", p=P)
                    front = sorted_scores[0:EDGES, :].rearrange("(p n) c -> p n c", p=P)
                    behind = sorted_scores[2:EDGES + 2, :].rearrange("(p n) c -> p n c", p=P)
                    sp.dma_start(ss[:, 1:NT + 1, :], main).then_inc(landed, 16)
                    sp.dma_start(ss[:, 0, :], front[:, 0, :]).then_inc(landed, 16)
                    sp.dma_start(ss[:, NT + 1, :], behind[:, NT - 1, :]).then_inc(landed, 16)
                    sp.wait_ge(done, 1)
                    sp.dma_start(sorted_weights[1:EDGES + 1, :].rearrange("(p n) h -> p (n h)", p=P),
                                 ss[:, 0:NT // 2, :].rearrange("p n c -> p (n c)")).then_inc(stored, 16)
                    sp.wait_ge(stored, 16)

                @block.vector
                def _(dve):
                    count = [0]

                    def link(instruction):
                        instruction.then_inc(v, 1)
                        count[0] += 1
                        dve.wait_ge(v, count[0])

                    dve.wait_ge(landed, 48)
                    node = ss[:, :, HEADS]
                    link(dve.tensor_tensor(keep[:, 0, :], node[:, 1:NT + 1], node[:, 0:NT], ALU.is_equal))
                    link(dve.tensor_tensor(keep[:, 1, :], node[:, 1:NT + 1], node[:, 2:NT + 2], ALU.is_equal))
                    link(dve.tensor_scalar(drop[:, :, :], keep[:, :, :], -1.0, FAR, ALU.add, ALU.mult))

                    rounds = [0]

                    def scan(result, mask, source, op0, op1, neutral, backward):
                        n = rounds[0]
                        rounds[0] += 1

                        def way(ap):
                            return ap[:, ::-1] if backward else ap
                        for h in range(HEADS):
                            last = dve.tensor_tensor_scan(way(result[:, h, :]), way(mask), way(source[:, h, :]),
                                                          neutral, op0, op1)
                        link(last)
                        running_mask = cum[:, n // 2, n % 2, :]
                        link(dve.tensor_tensor_scan(way(running_mask), way(mask), way(mask), FAR, ALU.min, ALU.min))
                        end = 0 if backward else NT - 1
                        link(dve.tensor_copy(edge_in[:, 0, :], result[:, :, end]))
                        dve.tensor_copy(edge_in[:, 1, :], running_mask[:, end:end + 1].to_broadcast([P, HEADS])
                                        ).then_inc(ask, 1)
                        dve.wait_ge(turned_mm, n + 1)
                        link(dve.tensor_copy(turned[:, :, :].rearrange("h t p -> h (t p)"), psum[0][0:HEADS, 0:2 * P]))
                        link(dve.memset(carry[:, :], neutral))
                        place = carry[:, 0:P] if backward else carry[:, 1:P + 1]
                        dve.tensor_tensor_scan(way(place), way(turned[:, 1, :]), way(turned[:, 0, :]), neutral, op0,
                                               op1).then_inc(ask_back, 1)
                        dve.wait_ge(back, n + 1)
                        link(dve.tensor_copy(carry_in[:, :], psum[1][:, 0:HEADS]))
                        for h in range(HEADS):
                            last = dve.scalar_tensor_tensor(result[:, h, :], running_mask, carry_in[:, h:h + 1],
                                                            result[:, h, :], op0, op1)
                        link(last)

                    raw = ss[:, 1:NT + 1, 0:HEADS].rearrange("p n h -> p h n")
                    scan(scan_f, drop[:, 0, :], raw, ALU.add, ALU.max, -FAR, False)
                    scan(scan_b, drop[:, 1, :], raw, ALU.add, ALU.max, -FAR, True)
                    link(dve.tensor_tensor(scan_f[:, :, :], scan_f[:, :, :], scan_b[:, :, :], ALU.max))
                    dve.tensor_tensor(expd[:, :, :], raw, scan_f[:, :, :], ALU.subtract).then_inc(diff_done, 1)
                    dve.wait_ge(exp_done, 1)
                    scan(scan_f, keep[:, 0, :], expd, ALU.mult, ALU.add, 0.0, False)
                    scan(scan_b, keep[:, 1, :], expd, ALU.mult, ALU.add, 0.0, True)
                    link(dve.tensor_tensor(scan_b[:, :, :], scan_b[:, :, :], expd[:, :, :], ALU.subtract))
                    link(dve.tensor_tensor(scan_f[:, :, :], scan_f[:, :, :], scan_b[:, :, :], ALU.add))
                    link(dve.reciprocal(scan_b[:, :, :], scan_f[:, :, :]))
                    weights_out = ss[:, 0:NT // 2, :].rearrange("p n c -> p (n c)").rearrange("p (n h) -> p h n",
                                                                                             h=HEADS)
                    dve.tensor_tensor(weights_out, expd[:, :, :], scan_b[:, :, :], ALU.mult).then_inc(done, 1)

                @block.scalar
                def _(act):
                    act.wait_ge(diff_done, 1)
                    act.activation(expd[:, :, :], expd[:, :, :], ACT.Exp).then_inc(exp_done, 1)

                @block.tensor
                def _(pe):
                    for n in range(4):
                        pe.wait_ge(ask, n + 1)
                        pe.transpose(psum[0][0:HEADS, 0:P], edge_in[:, 0, :], ident[:, :])
                        pe.transpose(psum[0][0:HEADS, P:2 * P], edge_in[:, 1, :], ident[:, :]
                                     ).then_inc(turned_mm, 1)
                        pe.wait_ge(ask_back, n + 1)
                        off = n % 2
                        pe.transpose(psum[1][:, 0:HEADS], carry[:, off:off + P], ident[0:HEADS, 0:HEADS]
                                     ).then_inc(back, 1)
            end_phase()

        def edges_layer_3():
            (edge_load_row, edge_compare, edge_sum_equal, edge_copy_sum, edge_copy_rows, edge_multiply,
             edge_take_out, edge_add, edge_all_added, edge_sum_mm) = summed_edges("eK", 0, out, weights["L3_gnn_Wout"][:, :], T[1])
            v_landed = sem2("eK_v_landed")
            place_ready = sem("eK_place_ready")
            gathered = sem2("eK_gathered")
            factor_done = sem("eK_factor_done")
            msg_done = sem("eK_msg_done")

            with nc.Block() as block:
                @block.sync
                def _(sp):
                    def load(g, k, s, first):
                        edge_load_row(sp, g, k, s, first)
                        if not first:
                            sp.wait_ge(msg_done, g - 1)
                        sp.dma_start(T[0][:, s, :], values[bass.ds(g, 1), :, :].rearrange("a p n -> (a p) n")
                                     ).then_inc(v_landed[s], 16)
                    two_slot_loop(sp, NG, [(0, load)])

                @block.gpsimd
                def _(pool):
                    def fetch(g, k, s, first):
                        wait_on_pool(pool, place_ready, g + 1)
                        if not first:
                            wait_on_pool(pool, factor_done, g - 1)
                        for a in range(J):
                            pool.indirect_dma_start(weight_in[:, s, a, :], None, sorted_weights,
                                                    bass.IndirectOffsetOnAxis(ap=gather_a[:, s, a:a + 1], axis=0)
                                                    ).then_inc(gathered[s], 16)

                    def add(g, k, s, first):
                        edge_add(pool, g, k, s, first)
                    two_slot_loop(pool, NG, [(0, fetch), (2, add)])
                    edge_all_added(pool)

                @block.vector
                def _(dve):
                    def compare(g, k, s, first):
                        edge_compare(dve, g, k, s, first)

                    def message(g, k, s, first):
                        dve.wait_ge(gathered[s], 16 * J * (k + 1))
                        dve.tensor_tensor(self_minus[:, s, :, :],
                                          is_self[:, bass.ds(g * J, J)].unsqueeze(2).to_broadcast([P, J, HEADS]),
                                          weight_in[:, s, :, :], ALU.subtract).then_inc(factor_done, 1)
                        dve.wait_ge(factor_done, g + 1)
                        dve.wait_ge(v_landed[s], 16 * (k + 1))
                        if not first:
                            dve.wait_ge(edge_sum_mm, g - 1)
                        dve.tensor_tensor(T[1][:, s, :].rearrange("p (n d) -> p n d", d=HEAD_DIM),
                                          T[0][:, s, :].rearrange("p (n d) -> p n d", d=HEAD_DIM),
                                          self_minus[:, s, :, :].rearrange("p j h -> p (j h)").unsqueeze(2)
                                          .to_broadcast([P, J * HEADS, HEAD_DIM]), ALU.mult).then_inc(msg_done, 1)

                    def take_out(g, k, s, first):
                        edge_take_out(dve, g, k, s, first)
                    two_slot_loop(dve, NG, [(0, compare), (0, message), (1, take_out)])

                @block.scalar
                def _(act):
                    def place(g, k, s, first):
                        if not first:
                            act.wait_ge(gathered[s], 16 * J * k)
                        act.activation(gather_a[:, s, :], sort_pos[:, bass.ds(g * J, J)],
                                       ACT.Copy).then_inc(place_ready, 1)

                    def copy_sum(g, k, s, first):
                        edge_copy_sum(act, g, k, s, first)

                    def copy_rows(g, k, s, first):
                        edge_copy_rows(act, g, k, s, first)
                    two_slot_loop(act, NG, [(0, place), (1, copy_sum), (1, copy_rows)])

                @block.tensor
                def _(pe):
                    def sum_equal(g, k, s, first):
                        pe.wait_ge(msg_done, g + 1)
                        edge_sum_equal(pe, g, k, s, first)

                    def multiply(g, k, s, first):
                        edge_multiply(pe, g, k, s, first)
                    two_slot_loop(pe, NG, [(0, sum_equal), (1, multiply)])
            end_phase()

        setup()
        prepare_indices("pD", 1, ins["dst_rows"], False)
        prepare_indices("pS", 0, ins["src_rows"], True)
        nodes_into_layer_0()
        edges_convolution("eB", h0, y1, weights["L0_gnn_W1l"][:, :], fill=z1)
        nodes_between_convolutions()
        edges_convolution("eD", h1, y2, weights["L0_gnn_W2l"][:, :])
        nodes_into_layer_1()
        edges_layer_1()
        nodes_into_layer_2()
        edges_layer_2()
        nodes_into_layer_3()
        edges_scores()
        softmax_by_source()
        edges_layer_3()


def kernel(**inputs):
    import numpy as np
    import concourse.bacc as bacc
    from concourse.bass_utils import run_bass_kernel_spmd as run

    a = {n: np.asarray(v) for n, v in inputs.items()}
    n_nodes, n_edges = a["x"].shape[0], a["src"].shape[0]
    nodes, edges = padded(n_nodes, 2 * ROWS), padded(n_edges, 2 * ROWS)

    def pad_rows(v, n, fill=0):
        return np.concatenate([v, np.full((n - v.shape[0],) + v.shape[1:], fill, v.dtype)])

    src = pad_rows(a.pop("src"), edges, n_nodes)
    dst = pad_rows(a.pop("dst"), edges, n_nodes)
    feed = {"x": pad_rows(a.pop("x"), nodes)}
    for name, v in (("src", src), ("dst", dst)):
        feed[name + "_cols"] = v.reshape(edges // P, P).T
        feed[name + "_rows"] = v.reshape(edges // ROWS, ROWS)
        feed[name + "_groups"] = v.reshape(edges // ROWS, J, P).transpose(0, 2, 1).view(np.uint32)
    feed["edge50"] = pad_rows(a.pop("edge_attr_50"), edges).T
    feed["edge128"] = pad_rows(a.pop("edge_attr_128"), edges).T
    for name in ("L2_gnn_W1", "L2_gnn_W2"):
        feed[name] = a.pop(name).T
    feed["L3_gnn_Wexp"] = a.pop("L3_gnn_Wexp").T.reshape(-1)
    feed.update(a)
    feed = {n: np.ascontiguousarray(v) for n, v in feed.items()}

    nc = bacc.Bacc("TRN2", target_bir_lowering=False, num_devices=1)
    ins = {n: nc.dram_tensor(n, v.shape, mybir.dt.from_np(v.dtype), kind="ExternalInput").ap()
           for n, v in feed.items()}
    out = nc.dram_tensor("out", (nodes + ROWS, D), F32, kind="ExternalOutput").ap()
    gnn_kernel(nc, ins, out, n_nodes, n_edges)
    r = run(nc, [feed], core_ids=[0])
    return r.results[0]["out"][:n_nodes]
```

```python
import concourse.bass as bass
from concourse import mybir
from contextlib import ExitStack

F32 = mybir.dt.float32
F16 = mybir.dt.float16
I32 = mybir.dt.int32
U32 = mybir.dt.uint32
ALU = mybir.AluOpType
ACT = mybir.ActivationFunctionType
AX_X = mybir.AxisListType.X

P = 128
D = 128
J = 4
ROWS = J * P
HEADS = 8
HEAD_DIM = D // HEADS
SCALE = HEAD_DIM ** -0.5
EPS = 1e-5
LO_BITS = 9
LO = 1 << LO_BITS
SC_W = 16
FAR = 1.0e38


def padded(n, unit):
    return -(-n // unit) * unit


def uses(steps, slots, slot):
    return -(-(steps - slot) // slots)


def ring_loop(eng, steps, slots, stages):
    def step(i, u):
        for lag, fn in stages:
            s = (u - lag) % slots
            if isinstance(i, int):
                b = i * slots + u - lag
                if 0 <= b < steps:
                    fn(b, b // slots, s, b < slots)
            else:
                fn(i * slots + (u - lag), i + (u - lag - s) // slots, s, False)

    most = max(lag for lag, _ in stages)
    head = padded(slots + most, slots) // slots
    whole = steps // slots
    for i in range(head):
        for u in range(slots):
            step(i, u)
    with eng.Fori(head, whole) as i:
        for u in range(slots):
            step(i, u)
    for t in range(whole * slots, steps + most):
        step(t // slots, t % slots)


def every_second(fn):
    def stage(b, k, s, first):
        if s % 2 == 0:
            if first:
                fn(b // 2, k, s // 2, True)
            else:
                fn(k * 2 + s // 2, k, s // 2, False)
    return stage


def quad(fn):
    def stage(b, k, s, first):
        fn(b, 2 * k + s // 4, s % 4, first and b < 4)
    return stage


def gnn_kernel(nc, ins, out, n_nodes, n_edges):
    NODES = padded(n_nodes, ROWS)
    EDGES = padded(n_edges, ROWS)
    NB = NODES // ROWS
    NG = EDGES // ROWS
    HI = NODES // LO
    NT = EDGES // P
    assert NB == 2 * NG
    TABLE = NODES + ROWS

    with ExitStack() as ctx:
        def sb(name, shape, dt=F32):
            return ctx.enter_context(nc.sbuf_tensor(name, shape, dt))

        in_use = []

        def sem(name):
            in_use.append(nc.alloc_semaphore(name=name))
            return in_use[-1]

        def sem2(name):
            return [sem(f"{name}_{n}") for n in range(2)]

        def sem4(name):
            return [sem(f"{name}_{n}") for n in range(4)]

        def dram(name, shape, dt=F32):
            return nc.dram_tensor(name, shape, dt, kind="Internal").ap()

        h0, h1, h2, h3, h4 = [dram(f"h{n}", (NODES, D)) for n in range(5)]
        y1, y2, z1, y3 = [dram(n, (TABLE, D)) for n in ("y1", "y2", "z1", "y3")]
        x1h = dram("x1h", (NODES, D))
        x2 = dram("x2", (NODES, D))
        values = dram("values", (NG, P, J * D))
        sorted_scores = dram("sorted_scores", (EDGES + 2, SC_W))
        sorted_weights = dram("sorted_weights", (EDGES + 2, HEADS))

        psum = [ctx.enter_context(nc.psum_tensor(f"bank{n}", [P, ROWS], F32)) for n in range(8)]
        T = [sb(f"tile{n}", [P, 4 if n < 6 else 2, ROWS]) for n in range(8)]
        same = sb("same", [P, 2, J, ROWS])
        found = sb("found", [P, J, ROWS])
        idx_row = sb("idx_row", [P, 2, ROWS], I32)

        ident = sb("ident", [P, P])
        ident16 = sb("ident16", [P, P], F16)
        ones = sb("ones", [P, P])
        iota_lo = sb("iota_lo", [P, LO], F16)
        before = sb("before", [P, J, ROWS])
        upper = sb("upper", [P, P])
        spare = sb("spare", [P, J])
        eps = sb("eps", [P, 1])
        zeros = sb("zeros", [P, ROWS])
        minus_ones = sb("minus_ones", [P, SC_W])

        weights = {}
        for name in ("L0_gnn_W1l", "L0_gnn_W1r", "L0_gnn_W2l", "L0_gnn_W2r", "L1_gnn_We2", "L1_gnn_Wn1",
                     "L1_gnn_Wn2", "L3_gnn_Wq", "L3_gnn_Wout"):
            weights[name] = sb("w_" + name, [P, D])
        w_e1 = sb("w_e1", [50, D])
        w_kv = sb("w_kv", [P, 2 * D])
        w_ekv = sb("w_ekv", [P, 2 * D])
        w_1 = sb("w_1", [P, 4, D])
        w_2 = sb("w_2", [P, 3, D])
        w_exp = sb("w_exp", [P, HEADS * HEADS])
        be1 = sb("be1", [P, 1])
        u0 = sb("u0", [P, 1])
        u_cols = sb("u_cols", [P, P])
        rows = {}
        for name in ("L0_gnn_b1", "L0_gnn_b2", "L1_gnn_be2", "L1_gnn_bn1", "L1_gnn_bn2", "L2_gnn_b1",
                     "L2_gnn_b2", "L3_gnn_bout"):
            rows[name] = sb("b_" + name, [P, D])
        z_init = sb("z_init", [P, ROWS])
        y3_init = sb("y3_init", [P, ROWS])
        c1 = sb("c1", [P, D])
        c2 = sb("c2", [P, D])

        src_i = sb("src_i", [P, NT], I32)
        dst_i = sb("dst_i", [P, NT], I32)
        hl_i = sb("hl_i", [P, 4, NT], I32)
        src_f = sb("src_f", [P, NT])
        dst_f = sb("dst_f", [P, NT])
        hl_f = sb("hl_f", [P, 4, NT])
        dup = sb("dup", [P, 2, NT])
        flag = sb("flag", [P, NT])
        tmp_t = sb("tmp_t", [P, NT])
        src_add = sb("src_add", [P, NT])
        dst_add = sb("dst_add", [P, NT])
        inv_count = sb("inv_count", [P, NT])
        start_in = sb("start_in", [P, NT])
        sort_pos = sb("sort_pos", [P, NT])
        is_self = sb("is_self", [P, NT])

        stats = sb("stats", [P, 4, J, 6])
        mean_var = sb("mean_var", [P, 4, J, 2])
        std = sb("std", [P, 4, J])
        rstd = sb("rstd", [P, 4, J])
        shift = sb("shift", [P, 4, J])

        gather_a = sb("gather_a", [P, 2, J], U32)
        gather_b = sb("gather_b", [P, 2, J], U32)
        add_to = sb("add_to", [P, 2, J], U32)

        onehot_hi = sb("onehot_hi", [P, 2, J, HI], F16)
        onehot_lo = sb("onehot_lo", [P, 2, J, LO], F16)
        hi_turned = sb("hi_turned", [HI, 2, J, P], F16)
        hist = sb("hist", [HI, LO])
        hist_run = sb("hist_run", [HI, LO])
        hist_base = sb("hist_base", [HI, LO])
        table = sb("table", [HI, 2, 2, LO], F16)
        row_off = sb("row_off", [HI, 1])
        picked = sb("picked", [P, 2, LO])
        idx_cols = sb("idx_cols", [P, 2, J])
        count_cols = sb("count_cols", [P, J])
        dup_cols = sb("dup_cols", [P, J])
        picked_cols = sb("picked_cols", [P, J])

        score = sb("score", [P, 2, J, SC_W])
        qk_sum = sb("qk_sum", [P, 2, J * HEADS])
        mixed = sb("mixed", [P, J * HEADS * HEADS])
        weight_in = sb("weight_in", [P, 2, J, HEADS])
        self_minus = sb("self_minus", [P, 2, J, HEADS])

        ss = sb("ss", [P, NT + 2, SC_W])
        keep = sb("keep", [P, 2, NT])
        drop = sb("drop", [P, 2, NT])
        cum = sb("cum", [P, 2, 2, NT])
        scan_f = sb("scan_f", [P, HEADS, NT])
        scan_b = sb("scan_b", [P, HEADS, NT])
        expd = sb("expd", [P, HEADS, NT])
        edge_in = sb("edge_in", [P, 2, HEADS])
        turned = sb("turned", [HEADS, 2, P])
        carry = sb("carry", [HEADS, P + 1])
        carry_in = sb("carry_in", [P, HEADS])

        def wait_on_pool(pool, s, value):
            pool.wait_ge(s, value)
            pool.sem_inc(pool_waits, 1)

        pool_waits = nc.alloc_semaphore(name="pool_waits")
        dve_waits = nc.alloc_semaphore(name="dve_waits")

        def block_rows(table_ap, b):
            return table_ap[bass.ds(b * ROWS, ROWS), :].rearrange("(p j) d -> p (j d)", j=J)

        def group_row(table_ap, g):
            return table_ap[bass.ds(g, 1), :].rearrange("a e -> (a e)").partition_broadcast(P)

        def across(row, n=J):
            return row.unsqueeze(1).to_broadcast([P, n, D])

        def jd(ap):
            return ap.rearrange("p (j d) -> p j d", j=J)

        def end_phase():
            nc.clear_and_free_semaphores(in_use)
            in_use.clear()
            nc.all_engine_barrier()

        def setup():
            loads = sem("setup_loads")
            consts = sem("setup_consts")
            vec = sem("setup_vec")
            u_ready = sem("setup_u_cols")
            c_mm = sem("setup_c_products")
            n_loads = [0]

            with nc.Block() as block:
                @block.sync
                def _(sp):
                    def load(dst, src):
                        sp.dma_start(dst, src).then_inc(loads, 16)
                        n_loads[0] += 1
                    load(src_i[:, :], ins["src_cols"])
                    load(dst_i[:, :], ins["dst_cols"])
                    for name, t in weights.items():
                        load(t[:, :], ins[name])
                    load(w_e1[:, :], ins["L1_gnn_We1"])
                    load(w_kv[:, 0:D], ins["L3_gnn_Wk"])
                    load(w_kv[:, D:2 * D], ins["L3_gnn_Wv"])
                    load(w_ekv[:, 0:D], ins["L3_gnn_Wek"])
                    load(w_ekv[:, D:2 * D], ins["L3_gnn_Wev"])
                    load(w_1[:, :, :], ins["L2_gnn_W1"].rearrange("(k p) n -> p k n", p=P))
                    load(w_2[:, :, :], ins["L2_gnn_W2"].rearrange("(k p) n -> p k n", p=P))
                    load(w_exp[:, :], ins["L3_gnn_Wexp"].partition_broadcast(P))
                    load(be1[:, :], ins["L1_gnn_be1"].rearrange("(p a) -> p a", a=1))
                    load(u0[:, :], ins["L2_gnn_u"][0, :].rearrange("(p a) -> p a", a=1))
                    for name, t in rows.items():
                        load(t[:, :], ins[name].partition_broadcast(P))
                    sp.wait_ge(consts, 12)
                    for t in (y1, y2, z1, y3, out):
                        load(t[NODES:TABLE, :].rearrange("(p j) d -> p (j d)", j=J), zeros[:, :])
                    load(sorted_scores[0:1, :], minus_ones[0:1, :])
                    load(sorted_scores[EDGES + 1:EDGES + 2, :], minus_ones[0:1, :])
                    load(sorted_weights[0:1, :], minus_ones[0:1, 0:HEADS])
                    load(sorted_weights[EDGES + 1:EDGES + 2, :], minus_ones[0:1, 0:HEADS])
                    sp.wait_ge(loads, 16 * n_loads[0])

                @block.gpsimd
                def _(pool):
                    pool.memset(ident[:, :], 0.0).then_inc(consts, 1)
                    pool.memset(ones[:, :], 1.0).then_inc(consts, 1)
                    pool.memset(before[:, :, :], 1.0).then_inc(consts, 1)
                    pool.memset(eps[:, :], EPS).then_inc(consts, 1)
                    pool.memset(zeros[:, :], 0.0).then_inc(consts, 1)
                    pool.memset(minus_ones[:, :], -1.0).then_inc(consts, 1)
                    pool.wait_ge(consts, 6)
                    pool.affine_select(out=ident[:, :], in_=ident[:, :], compare_op=ALU.not_equal, fill=1.0, base=0,
                                       pattern=[[-1, P]], channel_multiplier=1).then_inc(consts, 1)
                    pool.affine_select(out=before[:, :, :], in_=before[:, :, :], compare_op=ALU.is_gt, fill=0.0, base=0,
                                       pattern=[[P, J], [-1, ROWS]], channel_multiplier=1).then_inc(consts, 1)
                    pool.affine_select(out=upper[:, :], in_=ones[:, :], compare_op=ALU.is_gt, fill=0.0, base=0,
                                       pattern=[[1, P]], channel_multiplier=-1).then_inc(consts, 1)
                    pool.iota(found[:, 0, :], [[1, LO]], base=0, channel_multiplier=0,
                              allow_small_or_imprecise_dtypes=True).then_inc(consts, 1)
                    pool.iota(spare[:, :], [[P, J]], base=NODES, channel_multiplier=1,
                              allow_small_or_imprecise_dtypes=True).then_inc(consts, 1)
                    pool.memset(score[:, :, :, :], 0.0).then_inc(consts, 1)

                @block.vector
                def _(dve):
                    dve.wait_ge(consts, 12)
                    dve.wait_ge(loads, 16 * n_loads[0])
                    dve.tensor_copy(ident16[:, :], ident[:, :]).then_inc(vec, 1)
                    dve.tensor_copy(iota_lo[:, :], found[:, 0, :]).then_inc(vec, 1)
                    dve.tensor_copy(u_cols[:, :], u0[:, 0:1].to_broadcast([P, P])).then_inc(u_ready, 1)
                    dve.tensor_copy(jd(z_init[:, :]), across(rows["L1_gnn_bn1"][:, :])).then_inc(vec, 1)
                    for n, (t, f) in enumerate(((src_i, src_f), (dst_i, dst_f))):
                        dve.tensor_copy(f[:, :], t[:, :]).then_inc(vec, 1)
                        dve.tensor_scalar(hl_i[:, 2 * n, :], t[:, :], LO_BITS, None,
                                          ALU.logical_shift_right).then_inc(vec, 1)
                        dve.tensor_scalar(hl_i[:, 2 * n + 1, :], t[:, :], LO - 1, None, ALU.bitwise_and).then_inc(vec, 1)
                    dve.wait_ge(vec, 9)
                    dve.tensor_copy(hl_f[:, :, :], hl_i[:, :, :]).then_inc(vec, 1)
                    dve.tensor_tensor(is_self[:, :], src_f[:, :], dst_f[:, :], ALU.is_equal).then_inc(vec, 1)
                    dve.wait_ge(c_mm, 1)
                    dve.tensor_tensor(c1[:, :], psum[0][:, 0:D], rows["L2_gnn_b1"][:, :], ALU.add).then_inc(vec, 1)
                    dve.tensor_tensor(c2[:, :], psum[1][:, 0:D], rows["L2_gnn_b2"][:, :], ALU.add).then_inc(vec, 1)
                    dve.wait_ge(vec, 13)
                    dve.tensor_copy(jd(y3_init[:, :]), across(c2[:, :])).then_inc(vec, 1)

                @block.tensor
                def _(pe):
                    pe.wait_ge(u_ready, 1)
                    pe.matmul(psum[0][:, 0:D], u_cols[:, :], w_1[:, 3, :], start=True, stop=True)
                    pe.matmul(psum[1][:, 0:D], u_cols[:, :], w_2[:, 2, :], start=True, stop=True).then_inc(c_mm, 1)
            end_phase()

        def build_onehots(dve, which, g, s):
            for a in range(J):
                dve.tensor_scalar(onehot_hi[:, s, a, :], iota_lo[:, 0:HI],
                                  hl_f[:, 2 * which, bass.ds(g * J + a, 1)], None, ALU.is_equal)
                last = dve.tensor_scalar(onehot_lo[:, s, a, :], iota_lo[:, :],
                                         hl_f[:, 2 * which + 1, bass.ds(g * J + a, 1)], None, ALU.is_equal)
            return last

        def node_counting(name, which, bank, row_landed):
            idx_f = (src_f, dst_f)[which]
            add_rows = (src_add, dst_add)[which]
            dup_done = sem(name + "_dup_done")
            dup_taken = sem(name + "_dup_taken")
            cols_taken = sem(name + "_cols_taken")
            onehots = sem(name + "_onehots")
            counted = sem(name + "_counted")
            hist_ready = sem(name + "_hist_ready")
            vec = sem(name + "_vec")

            def repeats_dve(dve):
                def repeats(g, k, s, first):
                    if not first:
                        dve.wait_ge(counted, g - 1)
                    build_onehots(dve, which, g, s).then_inc(onehots, 1)
                    if not (first and g == 0):
                        dve.wait_ge(dup_taken, g)
                    dve.tensor_copy(idx_cols[:, s, :], idx_f[:, bass.ds(g * J, J)]).then_inc(cols_taken, 1)
                    dve.wait_ge(cols_taken, g + 1)
                    dve.wait_ge(row_landed[s], 16 * (k + 1))
                    for a in range(J):
                        w = (a + 1) * P
                        last = dve.scalar_tensor_tensor(found[:, a, 0:w], idx_row[:, s, 0:w],
                                                        idx_cols[:, s, a:a + 1], before[:, a, 0:w],
                                                        ALU.is_equal, ALU.mult, accum_out=dup_cols[:, a:a + 1])
                    last.then_inc(dup_done, 1)
                    dve.wait_ge(dup_done, g + 1)
                    dve.tensor_copy(dup[:, which, bass.ds(g * J, J)], dup_cols[:, :]).then_inc(dup_taken, 1)
                return repeats

            def count_pe(pe):
                def count(g, k, s, first):
                    pe.wait_ge(onehots, g + 1)
                    for a in range(J):
                        last = pe.matmul(bank[0:HI, :], onehot_hi[:, s, a, :], onehot_lo[:, s, a, :],
                                         start=(first and g == 0 and a == 0), stop=False, skip_group_check=True)
                    last.then_inc(counted, 1)
                return count

            def finish_act(act):
                act.wait_ge(counted, NG)
                act.activation(hist[:, :], bank[0:HI, :], ACT.Copy).then_inc(hist_ready, 1)

            def finish_dve(dve):
                dve.wait_ge(dup_taken, NG)
                dve.tensor_scalar(flag[:, :], dup[:, which, :], 1.0, None, ALU.min).then_inc(vec, 1)
                dve.tensor_tensor(tmp_t[:, :].rearrange("p (g a) -> p g a", a=J),
                                  spare[:, :].unsqueeze(1).to_broadcast([P, NG, J]),
                                  idx_f[:, :].rearrange("p (g a) -> p g a", a=J), ALU.subtract).then_inc(vec, 1)
                dve.wait_ge(vec, 2)
                dve.tensor_tensor(tmp_t[:, :], tmp_t[:, :], flag[:, :], ALU.mult).then_inc(vec, 1)
                dve.wait_ge(vec, 3)
                dve.tensor_tensor(add_rows[:, :], tmp_t[:, :], idx_f[:, :], ALU.add).then_inc(vec, 1)

            return repeats_dve, count_pe, finish_act, finish_dve, dup_done

        def node_lookup(name, which, running, turn_banks, row_banks, table_bank, keep):
            encoded = sem(name + "_encoded")
            turned_mm = sem(name + "_turned_mm")
            turned_ready = sem(name + "_turned_ready")
            rounded = sem(name + "_rounded")
            table_ready = sem(name + "_table_ready")
            row_mm = sem(name + "_row_mm")
            picked_done = sem(name + "_picked_done")
            counted = sem(name + "_counted")
            vec = sem(name + "_vec")
            off_mm = sem(name + "_off_mm")
            base_in = sem(name + "_base_in")
            NTB, NRB = len(turn_banks), len(row_banks)

            def start_dve(dve):
                if running:
                    dve.tensor_tensor_scan(hist_run[:, :], zeros[0:HI, 0:LO], hist[:, :], 0.0, ALU.add,
                                           ALU.add).then_inc(vec, 1)
                    dve.wait_ge(vec, 1)
                    dve.tensor_tensor(hist_base[:, :], hist_run[:, :], hist[:, :], ALU.subtract).then_inc(vec, 1)
                    dve.wait_ge(off_mm, 1)
                    dve.tensor_copy(row_off[:, :], row_banks[0][0:HI, 0:1]).then_inc(vec, 1)
                    dve.wait_ge(vec, 3)
                    dve.tensor_scalar(hist_base[:, :], hist_base[:, :], row_off[:, 0:1], None,
                                      ALU.add).then_inc(vec, 1)
                else:
                    dve.tensor_copy(table[:, 0, 0, :], hist[:, :]).then_inc(vec, 1)
                    dve.wait_ge(vec, 1)
                    dve.tensor_tensor(table[:, 0, 1, :], hist[:, :], table[:, 0, 0, :],
                                      ALU.subtract).then_inc(table_ready, 1)

            def start_pe(pe):
                if running:
                    pe.wait_ge(vec, 2)
                    pe.matmul(row_banks[0][0:HI, 0:1], upper[0:HI, 0:HI], hist_run[:, LO - 1:LO], start=True,
                              stop=True).then_inc(off_mm, 1)
                    pe.wait_ge(vec, 4)
                    pe.matmul(table_bank[0:HI, :], ident[0:HI, 0:HI], hist_base[:, :], start=True, stop=False,
                              skip_group_check=True).then_inc(base_in, 1)
                else:
                    pe.wait_ge(table_ready, 1)

            def encode_dve(dve):
                def encode(g, k, s, first):
                    if not first:
                        dve.wait_ge(picked_done, J * (g - 1))
                        dve.wait_ge(turned_mm, g - 1)
                        if running:
                            dve.wait_ge(counted, g - 1)
                    build_onehots(dve, which, g, s).then_inc(encoded, 1)
                    if running:
                        dve.wait_ge(rounded, g + 1)
                        if not first:
                            dve.wait_ge(row_mm, J * (g - 1))
                        dve.tensor_tensor(table[:, s, 1, :], table_bank[0:HI, :], table[:, s, 0, :],
                                          ALU.subtract).then_inc(table_ready, 1)
                return encode

            def pick_dve(dve):
                def pick(g, k, s, first):
                    for a in range(J):
                        dve.wait_ge(row_mm, g * J + (a + 1))
                        if not (first and g == 0 and a < 2):
                            dve.wait_ge(picked_done, g * J + (a - 1))
                        dve.tensor_tensor_reduce(picked[:, a % 2, :], row_banks[a % NRB][:, :],
                                                 onehot_lo[:, s, a, :], 1.0, 0.0, ALU.mult, ALU.add,
                                                 picked_cols[:, a:a + 1]).then_inc(picked_done, 1)
                    dve.wait_ge(picked_done, J * (g + 1))
                    keep(dve, g)
                return pick

            def turn_pe(pe):
                def turn(g, k, s, first):
                    pe.wait_ge(encoded, g + 1)
                    if not first or g >= NTB:
                        pe.wait_ge(turned_ready, g - (NTB - 1))
                    for a in range(J):
                        last = pe.transpose(turn_banks[s % NTB][0:HI, :].bitcast(F16)[:, a * P:(a + 1) * P],
                                            onehot_hi[:, s, a, :], ident16[:, :])
                    last.then_inc(turned_mm, 1)
                    if running:
                        pe.wait_ge(table_ready, g + 1)
                        for a in range(J):
                            last = pe.matmul(table_bank[0:HI, :], onehot_hi[:, s, a, :], onehot_lo[:, s, a, :],
                                             start=False, stop=False, skip_group_check=True)
                        last.then_inc(counted, 1)
                return turn

            def rows_pe(pe):
                def rows_of(g, k, s, first):
                    pe.wait_ge(turned_ready, g + 1)
                    t = s if running else 0
                    for a in range(J):
                        if not (first and g == 0 and a < NRB):
                            pe.wait_ge(picked_done, g * J + (a + 1 - NRB))
                        for part in range(2):
                            last = pe.matmul(row_banks[a % NRB][:, :], hi_turned[:, s, a, :],
                                             table[:, t, part, :], start=(part == 0), stop=(part == 1))
                        last.then_inc(row_mm, 1)
                return rows_of

            def start_act(act):
                if running:
                    act.wait_ge(base_in, 1)

            def take_act(act):
                def take(g, k, s, first):
                    if not first:
                        act.wait_ge(row_mm, J * (g - 1))
                    if running:
                        if not (first and g == 0):
                            act.wait_ge(counted, g)
                        act.activation(table[:, s, 0, :], table_bank[0:HI, :], ACT.Copy).then_inc(rounded, 1)
                    act.wait_ge(turned_mm, g + 1)
                    act.activation(hi_turned[:, s, :, :].rearrange("h a p -> h (a p)"),
                                   turn_banks[s % NTB][0:HI, :].bitcast(F16)[:, 0:ROWS],
                                   ACT.Copy).then_inc(turned_ready, 1)
                return take

            return (start_dve, start_pe, start_act, encode_dve, pick_dve, turn_pe, rows_pe, take_act)

        def norm_semaphores(name):
            return [sem(name + n) for n in ("_stats_done", "_var_ready", "_std_ready", "_rstd_done",
                                            "_shift_ready")]

        def norm_statistics(norm, dve, x, b, s):
            stats_done, var_ready, _, _, _ = norm
            for j in range(J):
                last = dve.bn_stats(stats[:, s, j, :], x[:, j * D:(j + 1) * D])
            last.then_inc(stats_done, 1)
            dve.wait_ge(stats_done, b + 1)
            dve.sem_inc(dve_waits, 1)
            for j in range(J):
                last = dve.bn_aggr(mean_var[:, s, j, :], stats[:, s, j, :])
            last.then_inc(var_ready, 1)

        def norm_root(norm, act, b, s):
            _, var_ready, std_ready, _, _ = norm
            act.wait_ge(var_ready, b + 1)
            act.activation(std[:, s, :], mean_var[:, s, :, 1], ACT.Sqrt, bias=eps[:, 0:1]).then_inc(std_ready, 1)

        def norm_factors(norm, dve, b, s):
            _, _, std_ready, rstd_done, shift_ready = norm
            dve.wait_ge(std_ready, b + 1)
            dve.reciprocal(rstd[:, s, :], std[:, s, :]).then_inc(rstd_done, 1)
            dve.wait_ge(rstd_done, b + 1)
            dve.scalar_tensor_tensor(shift[:, s, :], mean_var[:, s, :, 0], -1.0, rstd[:, s, :], ALU.mult,
                                     ALU.mult).then_inc(shift_ready, 1)

        def norm_apply(norm, act, out_t, x, b, s):
            _, _, _, _, shift_ready = norm
            act.wait_ge(shift_ready, b + 1)
            for j in range(J):
                last = act.activation(out_t[:, j * D:(j + 1) * D], x[:, j * D:(j + 1) * D], ACT.Relu,
                                      bias=shift[:, s, j:j + 1], scale=rstd[:, s, j:j + 1])
            return last

        def products(pe, bank, left, right, width=D):
            for j in range(J):
                last = pe.matmul(bank[:, j * width:(j + 1) * width], left[:, j * P:(j + 1) * P], right,
                                 start=True, stop=True)
            return last

        def turn_tiles(pe, bank, t):
            for j in range(J):
                last = pe.transpose(bank[:, j * P:(j + 1) * P], t[:, j * D:(j + 1) * D], ident[:, :])
            return last

        def all_landed(eng, sems, steps):
            for n, q in enumerate(sems):
                eng.wait_ge(q, 16 * uses(steps, len(sems), n))

        def nodes_into_layer_0():
            norm = norm_semaphores("nA")
            x_landed = sem4("nA_x_landed")
            h_stored = sem4("nA_h_stored")
            y_stored = sem4("nA_y_stored")
            h_done = sem("nA_h_done")
            turned_mm = sem("nA_turned_mm")
            ht_ready = sem("nA_ht_ready")
            y_mm = sem("nA_y_mm")
            y_done = sem("nA_y_done")
            row_landed = sem2("nA_row_landed")
            repeats_dve, count_pe, finish_act, finish_dve, dup_done = node_counting("nA", 1, psum[7], row_landed)

            with nc.Block() as block:
                @block.sync
                def _(sp):
                    def load(b, k, s, first):
                        if not first:
                            sp.wait_ge(h_done, b - 3)
                        sp.dma_start(T[0][:, s, :], block_rows(ins["x"], b)).then_inc(x_landed[s], 16)

                    def load_row(g, k, s, first):
                        if not first:
                            sp.wait_ge(dup_done, g - 1)
                        sp.dma_start(idx_row[:, s, :], group_row(ins["dst_rows"], g)).then_inc(row_landed[s], 16)

                    def store_h(b, k, s, first):
                        sp.wait_ge(h_done, b + 1)
                        sp.dma_start(block_rows(h0, b), T[1][:, s, :]).then_inc(h_stored[s], 16)

                    def store_y(b, k, s, first):
                        sp.wait_ge(y_done, b + 1)
                        sp.dma_start(block_rows(y1, b), T[2][:, s, :]).then_inc(y_stored[s], 16)
                    ring_loop(sp, NB, 4, [(0, load), (0, every_second(load_row)), (4, store_h), (8, store_y)])
                    all_landed(sp, h_stored, NB)
                    all_landed(sp, y_stored, NB)

                @block.vector
                def _(dve):
                    def measure(b, k, s, first):
                        dve.wait_ge(x_landed[s], 16 * (k + 1))
                        norm_statistics(norm, dve, T[0][:, s, :], b, s)

                    def factors(b, k, s, first):
                        if not first:
                            dve.wait_ge(h_done, b - 3)
                        norm_factors(norm, dve, b, s)
                    ring_loop(dve, NB, 4, [(1, factors), (0, measure), (0, every_second(repeats_dve(dve)))])
                    finish_dve(dve)

                @block.scalar
                def _(act):
                    def copy_turned(b, k, s, first):
                        act.wait_ge(turned_mm, b + 1)
                        if not first or b >= 2:
                            act.wait_ge(y_mm, b - 1)
                        act.activation(T[6][:, s % 2, :], psum[s % 2][:, :], ACT.Copy).then_inc(ht_ready, 1)

                    def finish(b, k, s, first):
                        act.wait_ge(y_mm, b + 1)
                        if not first:
                            act.wait_ge(y_stored[s], 16 * k)
                        act.activation(T[2][:, s, :], psum[2 + s % 2][:, :], ACT.Copy).then_inc(y_done, 1)

                    def root(b, k, s, first):
                        norm_root(norm, act, b, s)

                    def normalise(b, k, s, first):
                        if not first:
                            act.wait_ge(h_stored[s], 16 * k)
                            act.wait_ge(turned_mm, b - 3)
                        norm_apply(norm, act, T[1][:, s, :], T[0][:, s, :], b, s).then_inc(h_done, 1)
                    ring_loop(act, NB, 4, [(6, finish), (4, copy_turned), (2, normalise), (0, root)])
                    finish_act(act)

                @block.tensor
                def _(pe):
                    def multiply(b, k, s, first):
                        pe.wait_ge(ht_ready, b + 1)
                        if not first or b >= 2:
                            pe.wait_ge(y_done, b - 1)
                        products(pe, psum[2 + s % 2], T[6][:, s % 2, :],
                                 weights["L0_gnn_W1r"][:, :]).then_inc(y_mm, 1)

                    def turn(b, k, s, first):
                        pe.wait_ge(h_done, b + 1)
                        if not first or b >= 2:
                            pe.wait_ge(ht_ready, b - 1)
                        turn_tiles(pe, psum[s % 2], T[1][:, s, :]).then_inc(turned_mm, 1)
                    ring_loop(pe, NB, 4, [(5, multiply), (3, turn), (1, every_second(count_pe(pe)))])
            end_phase()

        def nodes_between_convolutions():
            y_landed = sem4("nC_y_landed")
            h_stored = sem4("nC_h_stored")
            yb_done = sem("nC_yb_done")
            h_done = sem("nC_h_done")
            row_landed = sem2("nC_row_landed")
            repeats_dve, count_pe, finish_act, finish_dve, dup_done = node_counting("nC", 0, psum[7], row_landed)

            with nc.Block() as block:
                @block.sync
                def _(sp):
                    def load_row(g, k, s, first):
                        if not first:
                            sp.wait_ge(dup_done, g - 1)
                        sp.dma_start(idx_row[:, s, :], group_row(ins["src_rows"], g)).then_inc(row_landed[s], 16)

                    def load(b, k, s, first):
                        if not first:
                            sp.wait_ge(h_done, b - 3)
                        sp.dma_start(T[0][:, s, :], block_rows(y1, b)).then_inc(y_landed[s], 16)

                    def store(b, k, s, first):
                        sp.wait_ge(h_done, b + 1)
                        sp.dma_start(block_rows(h1, b), T[1][:, s, :]).then_inc(h_stored[s], 16)
                    ring_loop(sp, NB, 4, [(0, load), (0, every_second(load_row)), (3, store)])
                    all_landed(sp, h_stored, NB)

                @block.gpsimd
                def _(pool):
                    def add_bias(b, k, s, first):
                        wait_on_pool(pool, y_landed[s], 16 * (k + 1))
                        pool.tensor_tensor(jd(T[0][:, s, :]), jd(T[0][:, s, :]), across(rows["L0_gnn_b1"][:, :]),
                                           ALU.add).then_inc(yb_done, 1)
                    ring_loop(pool, NB, 4, [(0, add_bias)])

                @block.vector
                def _(dve):
                    ring_loop(dve, NB, 4, [(0, every_second(repeats_dve(dve)))])
                    finish_dve(dve)

                @block.scalar
                def _(act):
                    def relu(b, k, s, first):
                        act.wait_ge(yb_done, b + 1)
                        if not first:
                            act.wait_ge(h_stored[s], 16 * k)
                        act.activation(T[1][:, s, :], T[0][:, s, :], ACT.Relu).then_inc(h_done, 1)
                    ring_loop(act, NB, 4, [(0, relu)])
                    finish_act(act)

                @block.tensor
                def _(pe):
                    ring_loop(pe, NB, 4, [(0, every_second(count_pe(pe)))])
            end_phase()

        def nodes_into_layer_1():
            norm = norm_semaphores("nE")
            y_landed = sem4("nE_y_landed")
            h1_landed = sem4("nE_h1_landed")
            h_stored = sem4("nE_h_stored")
            xh_stored = sem4("nE_xh_stored")
            turned_mm = sem("nE_turned_mm")
            ht_ready = sem("nE_ht_ready")
            x_mm = sem("nE_x_mm")
            x_done = sem("nE_x_done")
            xb_done = sem("nE_xb_done")
            h_done = sem("nE_h_done")
            xh_done = sem("nE_xh_done")

            with nc.Block() as block:
                @block.sync
                def _(sp):
                    def load(b, k, s, first):
                        if not first:
                            sp.wait_ge(turned_mm, b - 3)
                        sp.dma_start(T[1][:, s, :], block_rows(h1, b)).then_inc(h1_landed[s], 16)
                        if not first:
                            sp.wait_ge(x_done, b - 3)
                        sp.dma_start(T[0][:, s, :], block_rows(y2, b)).then_inc(y_landed[s], 16)

                    def store(b, k, s, first):
                        sp.wait_ge(h_done, b + 1)
                        sp.dma_start(block_rows(h2, b), T[3][:, s, :]).then_inc(h_stored[s], 16)
                        sp.wait_ge(xh_done, b + 1)
                        sp.dma_start(block_rows(x1h, b), T[4][:, s, :]).then_inc(xh_stored[s], 16)
                    ring_loop(sp, NB, 4, [(0, load), (6, store)])
                    all_landed(sp, h_stored, NB)
                    all_landed(sp, xh_stored, NB)

                @block.gpsimd
                def _(pool):
                    def add_bias(b, k, s, first):
                        wait_on_pool(pool, x_done, b + 1)
                        if not first:
                            wait_on_pool(pool, xh_stored[s], 16 * k)
                        pool.tensor_tensor(jd(T[4][:, s, :]), jd(T[2][:, s, :]), across(rows["L1_gnn_bn2"][:, :]),
                                           ALU.add).then_inc(xb_done, 1)
                    ring_loop(pool, NB, 4, [(0, add_bias)])

                @block.vector
                def _(dve):
                    def add_h(b, k, s, first):
                        dve.wait_ge(h_done, b + 1)
                        dve.wait_ge(xb_done, b + 1)
                        dve.tensor_tensor(T[4][:, s, :], T[4][:, s, :], T[3][:, s, :], ALU.add).then_inc(xh_done, 1)

                    def measure(b, k, s, first):
                        dve.wait_ge(x_mm, b + 1)
                        dve.wait_ge(y_landed[s], 16 * (k + 1))
                        if not first:
                            dve.wait_ge(h_done, b - 3)
                            dve.wait_ge(xb_done, b - 3)
                        dve.tensor_tensor(T[2][:, s, :], psum[2 + s % 2][:, :], T[0][:, s, :],
                                          ALU.add).then_inc(x_done, 1)
                        dve.wait_ge(x_done, b + 1)
                        norm_statistics(norm, dve, T[2][:, s, :], b, s)

                    def factors(b, k, s, first):
                        norm_factors(norm, dve, b, s)
                    ring_loop(dve, NB, 4, [(3, add_h), (0, measure), (1, factors)])

                @block.scalar
                def _(act):
                    def copy_turned(b, k, s, first):
                        act.wait_ge(turned_mm, b + 1)
                        if not first or b >= 2:
                            act.wait_ge(x_mm, b - 1)
                        act.activation(T[6][:, s % 2, :], psum[s % 2][:, :], ACT.Copy).then_inc(ht_ready, 1)

                    def root(b, k, s, first):
                        norm_root(norm, act, b, s)

                    def normalise(b, k, s, first):
                        if not first:
                            act.wait_ge(h_stored[s], 16 * k)
                            act.wait_ge(xh_done, b - 3)
                        norm_apply(norm, act, T[3][:, s, :], T[2][:, s, :], b, s).then_inc(h_done, 1)
                    ring_loop(act, NB, 4, [(0, copy_turned), (2, root), (3, normalise)])

                @block.tensor
                def _(pe):
                    def multiply(b, k, s, first):
                        pe.wait_ge(ht_ready, b + 1)
                        if not first or b >= 2:
                            pe.wait_ge(x_done, b - 1)
                        products(pe, psum[2 + s % 2], T[6][:, s % 2, :],
                                 weights["L0_gnn_W2r"][:, :]).then_inc(x_mm, 1)

                    def turn(b, k, s, first):
                        pe.wait_ge(h1_landed[s], 16 * (k + 1))
                        if not first or b >= 2:
                            pe.wait_ge(ht_ready, b - 1)
                        turn_tiles(pe, psum[s % 2], T[1][:, s, :]).then_inc(turned_mm, 1)
                    ring_loop(pe, NB, 4, [(0, turn), (1, multiply)])
            end_phase()

        def nodes_into_layer_2():
            norm = norm_semaphores("nG")
            z_landed = [sem(f"nG_z_landed_{n}") for n in range(8)]
            x_landed = sem4("nG_x_landed")
            x2_stored = sem4("nG_x2_stored")
            h_stored = sem4("nG_h_stored")
            silu_done = sem("nG_silu_done")
            turned_mm = sem("nG_turned_mm")
            st_ready = sem("nG_st_ready")
            x_mm = sem("nG_x_mm")
            x_done = sem("nG_x_done")
            h_done = sem("nG_h_done")

            z_tiles = (T[0], T[5])

            with nc.Block() as block:
                @block.sync
                def _(sp):
                    def load(b, k, s, first):
                        if not first:
                            sp.wait_ge(silu_done, b - 7)
                        sp.dma_start(z_tiles[s // 4][:, s % 4, :], block_rows(z1, b)).then_inc(z_landed[s], 16)

                    def load_x(b, k, s, first):
                        if not first:
                            sp.wait_ge(x_done, b - 3)
                        sp.dma_start(T[1][:, s, :], block_rows(x1h, b)).then_inc(x_landed[s], 16)

                    def store_x(b, k, s, first):
                        sp.wait_ge(x_done, b + 1)
                        sp.dma_start(block_rows(x2, b), T[3][:, s, :]).then_inc(x2_stored[s], 16)

                    def store(b, k, s, first):
                        sp.wait_ge(h_done, b + 1)
                        sp.dma_start(block_rows(h3, b), T[4][:, s, :]).then_inc(h_stored[s], 16)
                    ring_loop(sp, NB, 8, [(0, load), (2, quad(load_x)), (6, quad(store_x)), (8, quad(store))])
                    all_landed(sp, x2_stored, NB)
                    all_landed(sp, h_stored, NB)

                @block.vector
                def _(dve):
                    def copy_turned(b, k, s, first):
                        dve.wait_ge(turned_mm, b + 1)
                        if not first or b >= 2:
                            dve.wait_ge(x_mm, b - 1)
                        dve.tensor_copy(T[6][:, s % 2, :], psum[s % 2][:, :]).then_inc(st_ready, 1)

                    def measure(b, k, s, first):
                        dve.wait_ge(x_mm, b + 1)
                        dve.wait_ge(x_landed[s], 16 * (k + 1))
                        if not first:
                            dve.wait_ge(x2_stored[s], 16 * k)
                            dve.wait_ge(h_done, b - 3)
                        dve.tensor_tensor(T[3][:, s, :], psum[2 + s % 2][:, :], T[1][:, s, :],
                                          ALU.add).then_inc(x_done, 1)
                        dve.wait_ge(x_done, b + 1)
                        norm_statistics(norm, dve, T[3][:, s, :], b, s)

                    def factors(b, k, s, first):
                        norm_factors(norm, dve, b, s)
                    ring_loop(dve, NB, 8, [(4, quad(measure)), (3, quad(copy_turned)), (6, quad(factors))])

                @block.scalar
                def _(act):
                    def silu(b, k, s, first):
                        if s % 4 == 0:
                            for n in range(4):
                                if not isinstance(b, int) or b + n < NB:
                                    act.wait_ge(z_landed[s + n], 16 * (k + 1))
                                    if not first or s > 0:
                                        act.wait_ge(turned_mm, b + (n - 3))
                                    act.activation(T[2][:, n, :], z_tiles[s // 4][:, n, :], ACT.Silu).then_inc(silu_done, 1)

                    def root(b, k, s, first):
                        norm_root(norm, act, b, s)

                    def normalise(b, k, s, first):
                        if not first:
                            act.wait_ge(h_stored[s], 16 * k)
                        norm_apply(norm, act, T[4][:, s, :], T[3][:, s, :], b, s).then_inc(h_done, 1)
                    ring_loop(act, NB, 8, [(3, silu), (5, quad(root)), (7, quad(normalise))])

                @block.tensor
                def _(pe):
                    def turn(b, k, s, first):
                        pe.wait_ge(silu_done, b + 1)
                        if not first or b >= 2:
                            pe.wait_ge(st_ready, b - 1)
                        turn_tiles(pe, psum[s % 2], T[2][:, s, :]).then_inc(turned_mm, 1)

                    def multiply(b, k, s, first):
                        pe.wait_ge(st_ready, b + 1)
                        if not first or b >= 2:
                            pe.wait_ge(x_done, b - 1)
                        products(pe, psum[2 + s % 2], T[6][:, s % 2, :],
                                 weights["L1_gnn_Wn2"][:, :]).then_inc(x_mm, 1)
                    ring_loop(pe, NB, 8, [(4, quad(multiply)), (3, quad(turn))])
            end_phase()

        def nodes_into_layer_3():
            norm = norm_semaphores("nI")
            h3_landed = sem4("nI_h3_landed")
            y_landed = sem4("nI_y_landed")
            x_landed = sem4("nI_x_landed")
            h_stored = sem4("nI_h_stored")
            o_stored = sem4("nI_o_stored")
            turned_mm = sem("nI_turned_mm")
            ht_ready = sem("nI_ht_ready")
            y_mm = sem("nI_y_mm")
            y_done = sem("nI_y_done")
            x3_done = sem("nI_x3_done")
            h_done = sem("nI_h_done")
            o_done = sem("nI_o_done")

            with nc.Block() as block:
                @block.sync
                def _(sp):
                    def load(b, k, s, first):
                        if not first:
                            sp.wait_ge(turned_mm, b - 3)
                        sp.dma_start(T[1][:, s, :], block_rows(h3, b)).then_inc(h3_landed[s], 16)
                        if not first:
                            sp.wait_ge(x3_done, b - 3)
                        sp.dma_start(T[0][:, s, :], block_rows(y3, b)).then_inc(y_landed[s], 16)
                        sp.dma_start(T[2][:, s, :], block_rows(x2, b)).then_inc(x_landed[s], 16)

                    def store(b, k, s, first):
                        sp.wait_ge(h_done, b + 1)
                        sp.dma_start(block_rows(h4, b), T[4][:, s, :]).then_inc(h_stored[s], 16)
                        sp.wait_ge(o_done, b + 1)
                        sp.dma_start(block_rows(out, b), T[5][:, s, :]).then_inc(o_stored[s], 16)
                    ring_loop(sp, NB, 4, [(0, load), (6, store)])
                    all_landed(sp, h_stored, NB)
                    all_landed(sp, o_stored, NB)

                @block.gpsimd
                def _(pool):
                    def add_bias(b, k, s, first):
                        wait_on_pool(pool, x3_done, b + 1)
                        if not first:
                            wait_on_pool(pool, o_stored[s], 16 * k)
                        pool.tensor_tensor(jd(T[5][:, s, :]), jd(T[3][:, s, :]), across(rows["L3_gnn_bout"][:, :]),
                                           ALU.add).then_inc(o_done, 1)
                    ring_loop(pool, NB, 4, [(0, add_bias)])

                @block.vector
                def _(dve):
                    def measure(b, k, s, first):
                        dve.wait_ge(y_mm, b + 1)
                        dve.wait_ge(y_landed[s], 16 * (k + 1))
                        dve.tensor_tensor(T[0][:, s, :], psum[2 + s % 2][:, :], T[0][:, s, :],
                                          ALU.add).then_inc(y_done, 1)
                        dve.wait_ge(y_done, b + 1)
                        dve.wait_ge(x_landed[s], 16 * (k + 1))
                        if not first:
                            dve.wait_ge(h_done, b - 3)
                            dve.wait_ge(o_done, b - 3)
                        dve.scalar_tensor_tensor(T[3][:, s, :], T[0][:, s, :], 0.0, T[2][:, s, :], ALU.max,
                                                 ALU.add).then_inc(x3_done, 1)
                        dve.wait_ge(x3_done, b + 1)
                        norm_statistics(norm, dve, T[3][:, s, :], b, s)

                    def factors(b, k, s, first):
                        norm_factors(norm, dve, b, s)
                    ring_loop(dve, NB, 4, [(0, measure), (1, factors)])

                @block.scalar
                def _(act):
                    def copy_turned(b, k, s, first):
                        act.wait_ge(turned_mm, b + 1)
                        if not first or b >= 2:
                            act.wait_ge(y_mm, b - 1)
                        act.activation(T[6][:, s % 2, :], psum[s % 2][:, :], ACT.Copy).then_inc(ht_ready, 1)

                    def root(b, k, s, first):
                        norm_root(norm, act, b, s)

                    def normalise(b, k, s, first):
                        if not first:
                            act.wait_ge(h_stored[s], 16 * k)
                        norm_apply(norm, act, T[4][:, s, :], T[3][:, s, :], b, s).then_inc(h_done, 1)
                    ring_loop(act, NB, 4, [(0, copy_turned), (2, root), (3, normalise)])

                @block.tensor
                def _(pe):
                    def turn(b, k, s, first):
                        pe.wait_ge(h3_landed[s], 16 * (k + 1))
                        if not first or b >= 2:
                            pe.wait_ge(ht_ready, b - 1)
                        turn_tiles(pe, psum[s % 2], T[1][:, s, :]).then_inc(turned_mm, 1)

                    def multiply(b, k, s, first):
                        pe.wait_ge(ht_ready, b + 1)
                        if not first or b >= 2:
                            pe.wait_ge(y_done, b - 1)
                        products(pe, psum[2 + s % 2], T[6][:, s % 2, :], w_2[:, 0, :]).then_inc(y_mm, 1)
                    ring_loop(pe, NB, 4, [(0, turn), (1, multiply)])
            end_phase()

        def summed_edges(name, which, into, weight, messages, scaled=False, sum_banks=psum[0:2],
                         out_banks=psum[2:4]):

            idx_f = (src_f, dst_f)[which]
            idx_rows = (ins["src_rows"], ins["dst_rows"])[which]
            add_rows = (src_add, dst_add)[which]
            row_landed = sem2(name + "_row_landed")
            same_ready = sem(name + "_same_ready")
            sum_mm = sem(name + "_sum_mm")
            sum_ready = sem(name + "_sum_ready")
            out_mm = sem(name + "_out_mm")
            out_done = sem(name + "_out_done")
            add_to_ready = sem(name + "_add_to_ready")
            added = sem2(name + "_added")

            def load_row(sp, g, k, s, first):
                if not first:
                    sp.wait_ge(same_ready, g - 1)
                sp.dma_start(idx_row[:, s, :],
                             group_row(idx_rows, g)
                             ).then_inc(row_landed[s], 16)

            def compare(dve, g, k, s, first):
                dve.wait_ge(row_landed[s], 16 * (k + 1))
                if not first:
                    dve.wait_ge(sum_mm, g - 1)
                for a in range(J):
                    last = dve.tensor_scalar(same[:, s, a, :], idx_row[:, s, :],
                                             idx_f[:, bass.ds(g * J + a, 1)], None, ALU.is_equal)
                last.then_inc(same_ready, 1)

            def sum_equal(pe, g, k, s, first):
                pe.wait_ge(same_ready, g + 1)
                n = len(sum_banks)
                if not first or g >= n:
                    pe.wait_ge(sum_ready, g - (n - 1))
                for a in range(J):
                    last = pe.matmul(sum_banks[s % n][:, :], messages[:, s, a * D:(a + 1) * D], same[:, s, a, :],
                                     start=(a == 0), stop=(a == J - 1))
                last.then_inc(sum_mm, 1)

            def copy_sum(act, g, k, s, first):
                act.wait_ge(sum_mm, g + 1)
                if not first:
                    act.wait_ge(out_mm, g - 1)
                act.activation(T[2][:, s, :], sum_banks[s % len(sum_banks)][:, :], ACT.Copy).then_inc(sum_ready, 1)

            def copy_rows(act, g, k, s, first):
                if not first:
                    act.wait_ge(added[s], 16 * J * k)
                act.activation(add_to[:, s, :], add_rows[:, bass.ds(g * J, J)],
                               ACT.Copy).then_inc(add_to_ready, 1)

            def multiply(pe, g, k, s, first):
                pe.wait_ge(sum_ready, g + 1)
                n = len(out_banks)
                if not first or g >= n:
                    pe.wait_ge(out_done, g - (n - 1))
                products(pe, out_banks[s % n], T[2][:, s, :], weight).then_inc(out_mm, 1)

            def take_out(dve, g, k, s, first):
                dve.wait_ge(out_mm, g + 1)
                if not first:
                    dve.wait_ge(added[s], 16 * J * k)
                if scaled:
                    dve.tensor_tensor(jd(T[3][:, s, :]), jd(out_banks[s % len(out_banks)][:, :]),
                                      inv_count[:, bass.ds(g * J, J)].unsqueeze(2).to_broadcast([P, J, D]),
                                      ALU.mult).then_inc(out_done, 1)
                else:
                    dve.tensor_copy(T[3][:, s, :], out_banks[s % len(out_banks)][:, :]).then_inc(out_done, 1)

            def add(pool, g, k, s, first):
                wait_on_pool(pool, out_done, g + 1)
                wait_on_pool(pool, add_to_ready, g + 1)
                if not (first and g == 0):
                    wait_on_pool(pool, added[1 - s], 16 * J * (k + s))
                for a in range(J):
                    pool.indirect_dma_start(into, bass.IndirectOffsetOnAxis(ap=add_to[:, s, a:a + 1], axis=0),
                                            T[3][:, s, a * D:(a + 1) * D], None,
                                            compute_op=ALU.add).then_inc(added[s], 16)

            def all_added(pool):
                for n, q in enumerate(added):
                    pool.wait_ge(q, 16 * J * uses(NG, 2, n))

            return (load_row, compare, sum_equal, copy_sum, copy_rows, multiply, take_out, add, all_added,
                    sum_mm)

        def load_index(sp, idx, name, landed, used, per_group, g, k, s, first):
            if not first:
                sp.wait_ge(used[s], 16 * per_group * k)
            sp.dma_start(idx[:, s, :],
                         ins[name][bass.ds(g, 1), :, :].rearrange("a p j -> (a p) j")).then_inc(landed[s], 16)

        def gather(pool, into, idx, s, table_ap, done):
            for a in range(J):
                pool.indirect_dma_start(into[:, s, a * D:(a + 1) * D], None, table_ap,
                                        bass.IndirectOffsetOnAxis(ap=idx[:, s, a:a + 1], axis=0)).then_inc(done, 16)

        def edges_convolution(name, h, y, weight, lookup, after_dve=None, bias_fill=None, fill=None):
            (edge_load_row, edge_compare, edge_sum_equal, edge_copy_sum, edge_copy_rows, edge_multiply,
             edge_take_out, edge_add, edge_all_added, edge_sum_mm) = summed_edges(name, 1, y, weight, T[0], scaled=True)
            (start_dve, start_pe, start_act, encode_dve, pick_dve, turn_pe, rows_pe, take_act) = lookup
            idx_landed = sem2(name + "_idx_landed")
            gathered = sem2(name + "_gathered")
            filled = sem(name + "_filled")
            x_landed = sem4(name + "_x_landed")
            xb_done = sem(name + "_xb_done")
            xb_stored = sem4(name + "_xb_stored")

            with nc.Block() as block:
                @block.sync
                def _(sp):
                    def load(g, k, s, first):
                        load_index(sp, gather_a, "src_groups", idx_landed, gathered, J, g, k, s, first)
                        edge_load_row(sp, g, k, s, first)
                        if bias_fill is not None:
                            for n in range(2):
                                if not first:
                                    sp.wait_ge(xb_stored[2 * s + n], 16 * k)
                                sp.dma_start(T[4][:, 2 * s + n, :], block_rows(ins["x"], 2 * g + n)
                                             ).then_inc(x_landed[2 * s + n], 16)
                        if fill is not None:
                            fill_blocks(sp, fill, g, filled)
                    ring_loop(sp, NG, 2, [(0, load)])
                    if fill is not None:
                        sp.wait_ge(filled, 16 * NB)

                @block.gpsimd
                def _(pool):
                    def fetch(g, k, s, first):
                        wait_on_pool(pool, idx_landed[s], 16 * (k + 1))
                        if not first:
                            wait_on_pool(pool, edge_sum_mm, g - 1)
                        gather(pool, T[0], gather_a, s, h, gathered[s])

                    def add(g, k, s, first):
                        edge_add(pool, g, k, s, first)
                    ring_loop(pool, NG, 2, [(0, fetch), (2, add)])
                    edge_all_added(pool)

                @block.vector
                def _(dve):
                    def compare(g, k, s, first):
                        edge_compare(dve, g, k, s, first)

                    def take_out(g, k, s, first):
                        edge_take_out(dve, g, k, s, first)

                    def add_bias(g, k, s, first):
                        for n in range(2):
                            dve.wait_ge(x_landed[2 * s + n], 16 * (k + 1))
                            dve.tensor_tensor(jd(T[4][:, 2 * s + n, :]), jd(T[4][:, 2 * s + n, :]),
                                              across(rows["L0_gnn_b2"][:, :]), ALU.add).then_inc(xb_done, 1)
                    start_dve(dve)
                    ring_loop(dve, NG, 2, [(2, take_out), (0, encode_dve(dve)), (0, compare), (1, pick_dve(dve))]
                              + ([(1, add_bias)] if bias_fill is not None else []))
                    if after_dve is not None:
                        after_dve(dve)

                @block.scalar
                def _(act):
                    def copy_sum(g, k, s, first):
                        edge_copy_sum(act, g, k, s, first)

                    def copy_rows(g, k, s, first):
                        edge_copy_rows(act, g, k, s, first)

                    def store_xb(g, k, s, first):
                        for n in range(2):
                            act.wait_ge(xb_done, g * 2 + n + 1)
                            act.dma_start(block_rows(bias_fill, 2 * g + n), T[4][:, 2 * s + n, :]
                                          ).then_inc(xb_stored[2 * s + n], 16)
                    start_act(act)
                    ring_loop(act, NG, 2, [(0, take_act(act)), (0, copy_sum)]
                              + ([(1, store_xb)] if bias_fill is not None else []) + [(1, copy_rows)])
                    if bias_fill is not None:
                        all_landed(act, xb_stored, NB)

                @block.tensor
                def _(pe):
                    def sum_equal(g, k, s, first):
                        pe.wait_ge(gathered[s], 16 * J * (k + 1))
                        edge_sum_equal(pe, g, k, s, first)

                    def multiply(g, k, s, first):
                        edge_multiply(pe, g, k, s, first)
                    start_pe(pe)
                    ring_loop(pe, NG, 2, [(1, multiply), (0, turn_pe(pe)), (1, rows_pe(pe)), (0, sum_equal)])
            end_phase()

        def fill_blocks(sp, filling, g, filled):
            table_ap, start = filling
            for n in range(2):
                sp.dma_start(block_rows(table_ap, 2 * g + n), start).then_inc(filled, 16)

        def edges_first_convolution():
            at_least_one = sem("eB_at_least_one")
            inverse = sem("eB_inverse")
            kept = sem("eB_kept")

            def keep(dve, g):
                dve.tensor_scalar(count_cols[:, :], picked_cols[:, :], 1.0, None, ALU.max).then_inc(at_least_one, 1)
                dve.wait_ge(at_least_one, g + 1)
                dve.reciprocal(dup_cols[:, :], count_cols[:, :]).then_inc(inverse, 1)
                dve.wait_ge(inverse, g + 1)
                dve.tensor_copy(inv_count[:, bass.ds(g * J, J)], dup_cols[:, :]).then_inc(kept, 1)
                dve.wait_ge(kept, g + 1)
            lookup = node_lookup("eB_dst", 1, False, psum[4:6], psum[6:8], None, keep)
            edges_convolution("eB", h0, y1, weights["L0_gnn_W1l"][:, :], lookup, bias_fill=y2)

        def edges_second_convolution():
            kept = sem("eD_kept")
            placed = sem("eD_placed")

            def keep(dve, g):
                dve.tensor_copy(start_in[:, bass.ds(g * J, J)], picked_cols[:, :]).then_inc(kept, 1)
                dve.wait_ge(kept, g + 1)

            def places(dve):
                dve.wait_ge(kept, NG)
                dve.scalar_tensor_tensor(sort_pos[:, :], start_in[:, :], 1.0, dup[:, 0, :], ALU.add,
                                         ALU.add).then_inc(placed, 1)
                dve.wait_ge(placed, 1)
            lookup = node_lookup("eD_src", 0, True, [psum[4]], psum[6:8], psum[5], keep)
            edges_convolution("eD", h1, y2, weights["L0_gnn_W2l"][:, :], lookup, after_dve=places,
                              fill=(z1, z_init[:, :]))

        def edges_layer_1():
            (edge_load_row, edge_compare, edge_sum_equal, edge_copy_sum, edge_copy_rows, edge_multiply,
             edge_take_out, edge_add, edge_all_added, edge_sum_mm) = summed_edges("eF", 1, z1, weights["L1_gnn_Wn1"][:, :], T[1])
            idx_landed = sem2("eF_idx_landed")
            gathered = sem2("eF_gathered")
            ea_landed = sem2("eF_ea_landed")
            filled = sem("eF_filled")
            hid_mm = sem("eF_hid_mm")
            hid_ready = sem("eF_hid_ready")
            ew_mm = sem("eF_ew_mm")
            ew_done = sem("eF_ew_done")
            msg_done = sem("eF_msg_done")

            with nc.Block() as block:
                @block.sync
                def _(sp):
                    def load(g, k, s, first):
                        load_index(sp, gather_a, "src_groups", idx_landed, gathered, J, g, k, s, first)
                        edge_load_row(sp, g, k, s, first)
                        if not first:
                            sp.wait_ge(hid_mm, g - 1)
                        sp.dma_start(T[4][0:50, s, :], ins["edge50"][:, bass.ds(g * ROWS, ROWS)]
                                     ).then_inc(ea_landed[s], 16)
                        fill_blocks(sp, (y3, y3_init[:, :]), g, filled)
                    ring_loop(sp, NG, 2, [(0, load)])
                    sp.wait_ge(filled, 16 * NB)

                @block.gpsimd
                def _(pool):
                    def fetch(g, k, s, first):
                        wait_on_pool(pool, idx_landed[s], 16 * (k + 1))
                        if not first:
                            wait_on_pool(pool, msg_done, g - 1)
                        gather(pool, T[0], gather_a, s, h2, gathered[s])

                    def add(g, k, s, first):
                        edge_add(pool, g, k, s, first)
                    ring_loop(pool, NG, 2, [(0, fetch), (2, add)])
                    edge_all_added(pool)

                @block.vector
                def _(dve):
                    def compare(g, k, s, first):
                        edge_compare(dve, g, k, s, first)

                    def message(g, k, s, first):
                        dve.wait_ge(ew_mm, g + 1)
                        dve.tensor_tensor(jd(T[6][:, s, :]), jd(psum[5][:, :]), across(rows["L1_gnn_be2"][:, :]),
                                          ALU.add).then_inc(ew_done, 1)
                        dve.wait_ge(ew_done, g + 1)
                        dve.wait_ge(gathered[s], 16 * J * (k + 1))
                        if not first:
                            dve.wait_ge(edge_sum_mm, g - 1)
                        dve.tensor_tensor(T[1][:, s, :], T[0][:, s, :], T[6][:, s, :],
                                          ALU.mult).then_inc(msg_done, 1)

                    def take_out(g, k, s, first):
                        edge_take_out(dve, g, k, s, first)
                    ring_loop(dve, NG, 2, [(0, compare), (0, message), (1, take_out)])

                @block.scalar
                def _(act):
                    def silu(g, k, s, first):
                        act.wait_ge(hid_mm, g + 1)
                        if not first:
                            act.wait_ge(ew_mm, g - 1)
                        act.activation(T[5][:, s, :], psum[4][:, :], ACT.Silu,
                                       bias=be1[:, 0:1]).then_inc(hid_ready, 1)

                    def copy_sum(g, k, s, first):
                        edge_copy_sum(act, g, k, s, first)

                    def copy_rows(g, k, s, first):
                        edge_copy_rows(act, g, k, s, first)
                    ring_loop(act, NG, 2, [(0, silu), (1, copy_sum), (1, copy_rows)])

                @block.tensor
                def _(pe):
                    def hidden(g, k, s, first):
                        pe.wait_ge(ea_landed[s], 16 * (k + 1))
                        if not (first and g == 0):
                            pe.wait_ge(hid_ready, g)
                        pe.matmul(psum[4][:, :], w_e1[:, :], T[4][0:50, s, :], start=True,
                                  stop=True).then_inc(hid_mm, 1)

                    def edge_weight(g, k, s, first):
                        pe.wait_ge(hid_ready, g + 1)
                        if not (first and g == 0):
                            pe.wait_ge(ew_done, g)
                        products(pe, psum[5], T[5][:, s, :], weights["L1_gnn_We2"][:, :]).then_inc(ew_mm, 1)

                    def sum_equal(g, k, s, first):
                        pe.wait_ge(msg_done, g + 1)
                        edge_sum_equal(pe, g, k, s, first)

                    def multiply(g, k, s, first):
                        edge_multiply(pe, g, k, s, first)
                    ring_loop(pe, NG, 2, [(0, hidden), (1, sum_equal), (0, edge_weight), (1, multiply)])
            end_phase()

        def edges_layer_2():
            (edge_load_row, edge_compare, edge_sum_equal, edge_copy_sum, edge_copy_rows, edge_multiply,
             edge_take_out, edge_add, edge_all_added, edge_sum_mm) = summed_edges("eH", 1, y3, w_2[:, 1, :], T[1])
            a_landed = sem2("eH_src_idx_landed")
            b_landed = sem2("eH_dst_idx_landed")
            got_a = sem2("eH_src_gathered")
            got_b = sem2("eH_dst_gathered")
            ea_landed = sem2("eH_ea_landed")
            turned_mm = sem("eH_turned_mm")
            turned_ready = sem("eH_turned_ready")
            pre_mm = sem("eH_pre_mm")
            pre_done = sem("eH_pre_done")
            msg_done = sem("eH_msg_done")

            with nc.Block() as block:
                @block.sync
                def _(sp):
                    def load(g, k, s, first):
                        load_index(sp, gather_a, "src_groups", a_landed, got_a, J, g, k, s, first)
                        load_index(sp, gather_b, "dst_groups", b_landed, got_b, J, g, k, s, first)
                        edge_load_row(sp, g, k, s, first)
                        if not first:
                            sp.wait_ge(pre_mm, g - 1)
                        sp.dma_start(T[5][:, s, :], ins["edge128"][:, bass.ds(g * ROWS, ROWS)]
                                     ).then_inc(ea_landed[s], 16)
                    ring_loop(sp, NG, 2, [(0, load)])

                @block.gpsimd
                def _(pool):
                    def fetch(g, k, s, first):
                        wait_on_pool(pool, a_landed[s], 16 * (k + 1))
                        wait_on_pool(pool, b_landed[s], 16 * (k + 1))
                        if not first:
                            wait_on_pool(pool, turned_mm, g - 1)
                        gather(pool, T[0], gather_a, s, h3, got_a[s])
                        gather(pool, T[4], gather_b, s, h3, got_b[s])

                    def add(g, k, s, first):
                        edge_add(pool, g, k, s, first)
                    ring_loop(pool, NG, 2, [(0, fetch), (2, add)])
                    edge_all_added(pool)

                @block.vector
                def _(dve):
                    def compare(g, k, s, first):
                        edge_compare(dve, g, k, s, first)

                    def message(g, k, s, first):
                        dve.wait_ge(pre_mm, g + 1)
                        if not first:
                            dve.wait_ge(edge_sum_mm, g - 1)
                        dve.tensor_tensor(jd(T[1][:, s, :]), jd(psum[6][:, :]), across(c1[:, :]),
                                          ALU.add).then_inc(pre_done, 1)
                        dve.wait_ge(pre_done, g + 1)
                        dve.tensor_scalar(T[1][:, s, :], T[1][:, s, :], 0.0, None, ALU.max).then_inc(msg_done, 1)

                    def take_out(g, k, s, first):
                        edge_take_out(dve, g, k, s, first)
                    ring_loop(dve, NG, 2, [(0, compare), (1, take_out), (0, message)])

                @block.scalar
                def _(act):
                    def copy_turned(g, k, s, first):
                        act.wait_ge(turned_mm, g + 1)
                        if not first:
                            act.wait_ge(pre_mm, g - 1)
                        act.activation(T[6][:, s, :], psum[4][:, :], ACT.Copy)
                        act.activation(T[7][:, s, :], psum[5][:, :], ACT.Copy).then_inc(turned_ready, 1)

                    def copy_sum(g, k, s, first):
                        edge_copy_sum(act, g, k, s, first)

                    def copy_rows(g, k, s, first):
                        edge_copy_rows(act, g, k, s, first)
                    ring_loop(act, NG, 2, [(0, copy_turned), (1, copy_sum), (1, copy_rows)])

                @block.tensor
                def _(pe):
                    def turn(g, k, s, first):
                        pe.wait_ge(got_a[s], 16 * J * (k + 1))
                        if not (first and g == 0):
                            pe.wait_ge(turned_ready, g)
                        turn_tiles(pe, psum[4], T[0][:, s, :])
                        pe.wait_ge(got_b[s], 16 * J * (k + 1))
                        turn_tiles(pe, psum[5], T[4][:, s, :]).then_inc(turned_mm, 1)

                    def pre(g, k, s, first):
                        pe.wait_ge(turned_ready, g + 1)
                        pe.wait_ge(ea_landed[s], 16 * (k + 1))
                        if not (first and g == 0):
                            pe.wait_ge(pre_done, g)
                        for j in range(J):
                            o = psum[6][:, j * D:(j + 1) * D]
                            c = slice(j * P, (j + 1) * P)
                            pe.matmul(o, T[7][:, s, c], w_1[:, 0, :], start=True, stop=False)
                            pe.matmul(o, T[6][:, s, c], w_1[:, 1, :], start=False, stop=False)
                            last = pe.matmul(o, T[5][:, s, c], w_1[:, 2, :], start=False, stop=True)
                        last.then_inc(pre_mm, 1)

                    def sum_equal(g, k, s, first):
                        pe.wait_ge(msg_done, g + 1)
                        edge_sum_equal(pe, g, k, s, first)

                    def multiply(g, k, s, first):
                        edge_multiply(pe, g, k, s, first)
                    ring_loop(pe, NG, 2, [(0, turn), (1, sum_equal), (0, pre), (1, multiply)])
            end_phase()

        def edges_scores():
            a_landed = sem2("eJ_src_idx_landed")
            b_landed = sem2("eJ_dst_idx_landed")
            got_a = sem2("eJ_src_gathered")
            got_b = sem2("eJ_dst_gathered")
            ea_landed = sem2("eJ_ea_landed")
            turned_mm = sem("eJ_turned_mm")
            turned_ready = sem("eJ_turned_ready")
            q_mm = sem("eJ_q_mm")
            kv_mm = sem("eJ_kv_mm")
            kv_ready = sem("eJ_kv_ready")
            v_stored = sem2("eJ_v_stored")
            qk_done = sem("eJ_qk_done")
            vec = sem("eJ_vec")
            score_done = sem("eJ_score_done")
            place_ready = sem("eJ_place_ready")
            placed = sem2("eJ_placed")

            with nc.Block() as block:
                @block.sync
                def _(sp):
                    def load(g, k, s, first):
                        load_index(sp, gather_a, "src_groups", a_landed, got_a, J, g, k, s, first)
                        load_index(sp, gather_b, "dst_groups", b_landed, got_b, J, g, k, s, first)
                        if not first:
                            sp.wait_ge(kv_mm, g - 1)
                        sp.dma_start(T[5][:, s, :], ins["edge128"][:, bass.ds(g * ROWS, ROWS)]
                                     ).then_inc(ea_landed[s], 16)

                    def store(g, k, s, first):
                        sp.wait_ge(kv_ready, g + 1)
                        sp.dma_start(values[bass.ds(g, 1), :, :].rearrange("a p n -> (a p) n"), T[2][:, s, :]
                                     ).then_inc(v_stored[s], 16)
                    ring_loop(sp, NG, 2, [(0, load), (2, store)])
                    all_landed(sp, v_stored, NG)

                @block.gpsimd
                def _(pool):
                    def fetch(g, k, s, first):
                        wait_on_pool(pool, a_landed[s], 16 * (k + 1))
                        wait_on_pool(pool, b_landed[s], 16 * (k + 1))
                        if not first:
                            wait_on_pool(pool, turned_mm, g - 1)
                        gather(pool, T[0], gather_a, s, h4, got_a[s])
                        gather(pool, T[4], gather_b, s, h4, got_b[s])

                    def place(g, k, s, first):
                        wait_on_pool(pool, score_done, g + 1)
                        wait_on_pool(pool, place_ready, g + 1)
                        for a in range(J):
                            pool.indirect_dma_start(sorted_scores,
                                                    bass.IndirectOffsetOnAxis(ap=add_to[:, s, a:a + 1], axis=0),
                                                    score[:, s, a, :], None).then_inc(placed[s], 16)
                    ring_loop(pool, NG, 2, [(0, fetch), (2, place)])
                    for n, q in enumerate(placed):
                        pool.wait_ge(q, 16 * J * uses(NG, 2, n))

                @block.vector
                def _(dve):
                    def scores(g, k, s, first):
                        dve.wait_ge(q_mm, g + 1)
                        dve.wait_ge(kv_ready, g + 1)
                        dve.tensor_tensor(T[3][:, s, :], psum[6][:, :], T[1][:, s, :],
                                          ALU.mult).then_inc(qk_done, 1)
                        dve.wait_ge(qk_done, g + 1)
                        dve.tensor_reduce(qk_sum[:, s, :], T[3][:, s, :].rearrange("p (n d) -> p n d", d=HEAD_DIM),
                                          AX_X, ALU.add).then_inc(vec, 1)
                        dve.wait_ge(vec, g * 2 + 1)
                        for j in range(J):
                            last = dve.tensor_tensor(
                                mixed[:, j * 64:(j + 1) * 64].rearrange("p (o h) -> p o h", h=HEADS),
                                qk_sum[:, s, j * HEADS:(j + 1) * HEADS].unsqueeze(1).to_broadcast([P, HEADS, HEADS]),
                                w_exp[:, :].rearrange("p (o h) -> p o h", h=HEADS), ALU.mult)
                        last.then_inc(vec, 1)
                        dve.wait_ge(vec, g * 2 + 2)
                        if not first:
                            dve.wait_ge(placed[s], 16 * J * k)
                        dve.tensor_reduce(score[:, s, :, 0:HEADS],
                                          mixed[:, :].rearrange("p (j o h) -> p j o h", j=J, h=HEADS), AX_X, ALU.add)
                        dve.tensor_copy(score[:, s, :, HEADS], src_f[:, bass.ds(g * J, J)]
                                        ).then_inc(score_done, 1)
                    ring_loop(dve, NG, 2, [(1, scores)])

                @block.scalar
                def _(act):
                    def copy_turned(g, k, s, first):
                        act.wait_ge(turned_mm, g + 1)
                        if not first:
                            act.wait_ge(kv_mm, g - 1)
                        act.activation(T[6][:, s, :], psum[4][:, :], ACT.Copy)
                        act.activation(T[7][:, s, :], psum[5][:, :], ACT.Copy).then_inc(turned_ready, 1)

                    def copy_kv(g, k, s, first):
                        act.wait_ge(kv_mm, g + 1)
                        if not first:
                            act.wait_ge(qk_done, g - 1)
                            act.wait_ge(v_stored[s], 16 * k)
                        for n in range(2):
                            kv = psum[2 + n][:, :].rearrange("p (j w d) -> p j w d", j=2, w=2)
                            act.activation(T[1][:, s, n * 2 * D:(n + 1) * 2 * D].rearrange("p (j d) -> p j d", j=2),
                                           kv[:, :, 0, :], ACT.Copy, scale=SCALE)
                            last = act.activation(
                                T[2][:, s, n * 2 * D:(n + 1) * 2 * D].rearrange("p (j d) -> p j d", j=2),
                                kv[:, :, 1, :], ACT.Copy)
                        last.then_inc(kv_ready, 1)
                        if not first:
                            act.wait_ge(placed[s], 16 * J * k)
                        act.activation(add_to[:, s, :], sort_pos[:, bass.ds(g * J, J)],
                                       ACT.Copy).then_inc(place_ready, 1)
                    ring_loop(act, NG, 2, [(1, copy_kv), (0, copy_turned)])

                @block.tensor
                def _(pe):
                    def turn(g, k, s, first):
                        pe.wait_ge(got_a[s], 16 * J * (k + 1))
                        if not (first and g == 0):
                            pe.wait_ge(turned_ready, g)
                        turn_tiles(pe, psum[4], T[0][:, s, :])
                        pe.wait_ge(got_b[s], 16 * J * (k + 1))
                        turn_tiles(pe, psum[5], T[4][:, s, :]).then_inc(turned_mm, 1)

                    def project(g, k, s, first):
                        pe.wait_ge(turned_ready, g + 1)
                        if not (first and g == 0):
                            pe.wait_ge(qk_done, g)
                        products(pe, psum[6], T[6][:, s, :], weights["L3_gnn_Wq"][:, :]).then_inc(q_mm, 1)
                        pe.wait_ge(ea_landed[s], 16 * (k + 1))
                        if not (first and g == 0):
                            pe.wait_ge(kv_ready, g)
                        for j in range(J):
                            o = psum[2 + j // 2][:, (j % 2) * 2 * D:(j % 2 + 1) * 2 * D]
                            c = slice(j * P, (j + 1) * P)
                            pe.matmul(o, T[7][:, s, c], w_kv[:, :], start=True, stop=False)
                            last = pe.matmul(o, T[5][:, s, c], w_ekv[:, :], start=False, stop=True)
                        last.then_inc(kv_mm, 1)
                    ring_loop(pe, NG, 2, [(1, project), (0, turn)])
            end_phase()

        def softmax_by_source():
            landed = sem("sm_landed")
            v = sem("sm_v")
            turned_mm = sem("sm_turned")
            back = sem("sm_back")
            exp_done = sem("sm_exp_done")
            diff_done = sem("sm_diff_done")
            stored = sem("sm_stored")
            done = sem("sm_done")
            ask = sem("sm_ask")
            ask_back = sem("sm_ask_back")

            with nc.Block() as block:
                @block.sync
                def _(sp):
                    main = sorted_scores[1:EDGES + 1, :].rearrange("(p n) c -> p n c", p=P)
                    front = sorted_scores[0:EDGES, :].rearrange("(p n) c -> p n c", p=P)
                    behind = sorted_scores[2:EDGES + 2, :].rearrange("(p n) c -> p n c", p=P)
                    sp.dma_start(ss[:, 1:NT + 1, :], main).then_inc(landed, 16)
                    sp.dma_start(ss[:, 0, :], front[:, 0, :]).then_inc(landed, 16)
                    sp.dma_start(ss[:, NT + 1, :], behind[:, NT - 1, :]).then_inc(landed, 16)
                    sp.wait_ge(done, 1)
                    sp.dma_start(sorted_weights[1:EDGES + 1, :].rearrange("(p n) h -> p (n h)", p=P),
                                 ss[:, 0:NT // 2, :].rearrange("p n c -> p (n c)")).then_inc(stored, 16)
                    sp.wait_ge(stored, 16)

                @block.vector
                def _(dve):
                    count = [0]

                    def link(instruction):
                        instruction.then_inc(v, 1)
                        count[0] += 1
                        dve.wait_ge(v, count[0])

                    dve.wait_ge(landed, 48)
                    node = ss[:, :, HEADS]
                    link(dve.tensor_tensor(keep[:, 0, :], node[:, 1:NT + 1], node[:, 0:NT], ALU.is_equal))
                    link(dve.tensor_tensor(keep[:, 1, :], node[:, 1:NT + 1], node[:, 2:NT + 2], ALU.is_equal))
                    link(dve.tensor_scalar(drop[:, :, :], keep[:, :, :], -1.0, FAR, ALU.add, ALU.mult))

                    rounds = [0]

                    def scan(result, mask, source, op0, op1, neutral, backward):
                        n = rounds[0]
                        rounds[0] += 1

                        def way(ap):
                            return ap[:, ::-1] if backward else ap
                        for h in range(HEADS):
                            last = dve.tensor_tensor_scan(way(result[:, h, :]), way(mask), way(source[:, h, :]),
                                                          neutral, op0, op1)
                        link(last)
                        running_mask = cum[:, n // 2, n % 2, :]
                        link(dve.tensor_tensor_scan(way(running_mask), way(mask), way(mask), FAR, ALU.min, ALU.min))
                        end = 0 if backward else NT - 1
                        link(dve.tensor_copy(edge_in[:, 0, :], result[:, :, end]))
                        dve.tensor_copy(edge_in[:, 1, :], running_mask[:, end:end + 1].to_broadcast([P, HEADS])
                                        ).then_inc(ask, 1)
                        dve.wait_ge(turned_mm, n + 1)
                        link(dve.tensor_copy(turned[:, :, :].rearrange("h t p -> h (t p)"), psum[0][0:HEADS, 0:2 * P]))
                        link(dve.memset(carry[:, :], neutral))
                        place = carry[:, 0:P] if backward else carry[:, 1:P + 1]
                        dve.tensor_tensor_scan(way(place), way(turned[:, 1, :]), way(turned[:, 0, :]), neutral, op0,
                                               op1).then_inc(ask_back, 1)
                        dve.wait_ge(back, n + 1)
                        link(dve.tensor_copy(carry_in[:, :], psum[1][:, 0:HEADS]))
                        for h in range(HEADS):
                            last = dve.scalar_tensor_tensor(result[:, h, :], running_mask, carry_in[:, h:h + 1],
                                                            result[:, h, :], op0, op1)
                        link(last)

                    raw = ss[:, 1:NT + 1, 0:HEADS].rearrange("p n h -> p h n")
                    scan(scan_f, drop[:, 0, :], raw, ALU.add, ALU.max, -FAR, False)
                    scan(scan_b, drop[:, 1, :], raw, ALU.add, ALU.max, -FAR, True)
                    link(dve.tensor_tensor(scan_f[:, :, :], scan_f[:, :, :], scan_b[:, :, :], ALU.max))
                    dve.tensor_tensor(expd[:, :, :], raw, scan_f[:, :, :], ALU.subtract).then_inc(diff_done, 1)
                    dve.wait_ge(exp_done, 1)
                    scan(scan_f, keep[:, 0, :], expd, ALU.mult, ALU.add, 0.0, False)
                    scan(scan_b, keep[:, 1, :], expd, ALU.mult, ALU.add, 0.0, True)
                    link(dve.tensor_tensor(scan_b[:, :, :], scan_b[:, :, :], expd[:, :, :], ALU.subtract))
                    link(dve.tensor_tensor(scan_f[:, :, :], scan_f[:, :, :], scan_b[:, :, :], ALU.add))
                    link(dve.reciprocal(scan_b[:, :, :], scan_f[:, :, :]))
                    weights_out = ss[:, 0:NT // 2, :].rearrange("p n c -> p (n c)").rearrange("p (n h) -> p h n",
                                                                                             h=HEADS)
                    dve.tensor_tensor(weights_out, expd[:, :, :], scan_b[:, :, :], ALU.mult).then_inc(done, 1)

                @block.scalar
                def _(act):
                    act.wait_ge(diff_done, 1)
                    act.activation(expd[:, :, :], expd[:, :, :], ACT.Exp).then_inc(exp_done, 1)

                @block.tensor
                def _(pe):
                    for n in range(4):
                        pe.wait_ge(ask, n + 1)
                        pe.transpose(psum[0][0:HEADS, 0:P], edge_in[:, 0, :], ident[:, :])
                        pe.transpose(psum[0][0:HEADS, P:2 * P], edge_in[:, 1, :], ident[:, :]
                                     ).then_inc(turned_mm, 1)
                        pe.wait_ge(ask_back, n + 1)
                        off = n % 2
                        pe.transpose(psum[1][:, 0:HEADS], carry[:, off:off + P], ident[0:HEADS, 0:HEADS]
                                     ).then_inc(back, 1)
            end_phase()

        def edges_layer_3():
            (edge_load_row, edge_compare, edge_sum_equal, edge_copy_sum, edge_copy_rows, edge_multiply,
             edge_take_out, edge_add, edge_all_added, edge_sum_mm) = summed_edges("eK", 0, out, weights["L3_gnn_Wout"][:, :], T[1])
            v_landed = sem2("eK_v_landed")
            place_ready = sem("eK_place_ready")
            gathered = sem2("eK_gathered")
            factor_done = sem("eK_factor_done")
            msg_done = sem("eK_msg_done")

            with nc.Block() as block:
                @block.sync
                def _(sp):
                    def load(g, k, s, first):
                        edge_load_row(sp, g, k, s, first)
                        if not first:
                            sp.wait_ge(msg_done, g - 1)
                        sp.dma_start(T[0][:, s, :], values[bass.ds(g, 1), :, :].rearrange("a p n -> (a p) n")
                                     ).then_inc(v_landed[s], 16)
                    ring_loop(sp, NG, 2, [(0, load)])

                @block.gpsimd
                def _(pool):
                    def fetch(g, k, s, first):
                        wait_on_pool(pool, place_ready, g + 1)
                        if not first:
                            wait_on_pool(pool, factor_done, g - 1)
                        for a in range(J):
                            pool.indirect_dma_start(weight_in[:, s, a, :], None, sorted_weights,
                                                    bass.IndirectOffsetOnAxis(ap=gather_a[:, s, a:a + 1], axis=0)
                                                    ).then_inc(gathered[s], 16)

                    def add(g, k, s, first):
                        edge_add(pool, g, k, s, first)
                    ring_loop(pool, NG, 2, [(0, fetch), (2, add)])
                    edge_all_added(pool)

                @block.vector
                def _(dve):
                    def compare(g, k, s, first):
                        edge_compare(dve, g, k, s, first)

                    def message(g, k, s, first):
                        dve.wait_ge(gathered[s], 16 * J * (k + 1))
                        dve.tensor_tensor(self_minus[:, s, :, :],
                                          is_self[:, bass.ds(g * J, J)].unsqueeze(2).to_broadcast([P, J, HEADS]),
                                          weight_in[:, s, :, :], ALU.subtract).then_inc(factor_done, 1)
                        dve.wait_ge(factor_done, g + 1)
                        dve.wait_ge(v_landed[s], 16 * (k + 1))
                        if not first:
                            dve.wait_ge(edge_sum_mm, g - 1)
                        dve.tensor_tensor(T[1][:, s, :].rearrange("p (n d) -> p n d", d=HEAD_DIM),
                                          T[0][:, s, :].rearrange("p (n d) -> p n d", d=HEAD_DIM),
                                          self_minus[:, s, :, :].rearrange("p j h -> p (j h)").unsqueeze(2)
                                          .to_broadcast([P, J * HEADS, HEAD_DIM]), ALU.mult).then_inc(msg_done, 1)

                    def take_out(g, k, s, first):
                        edge_take_out(dve, g, k, s, first)
                    ring_loop(dve, NG, 2, [(1, take_out), (0, compare), (0, message)])

                @block.scalar
                def _(act):
                    def place(g, k, s, first):
                        if not first:
                            act.wait_ge(gathered[s], 16 * J * k)
                        act.activation(gather_a[:, s, :], sort_pos[:, bass.ds(g * J, J)],
                                       ACT.Copy).then_inc(place_ready, 1)

                    def copy_sum(g, k, s, first):
                        edge_copy_sum(act, g, k, s, first)

                    def copy_rows(g, k, s, first):
                        edge_copy_rows(act, g, k, s, first)
                    ring_loop(act, NG, 2, [(0, place), (1, copy_sum), (1, copy_rows)])

                @block.tensor
                def _(pe):
                    def sum_equal(g, k, s, first):
                        pe.wait_ge(msg_done, g + 1)
                        edge_sum_equal(pe, g, k, s, first)

                    def multiply(g, k, s, first):
                        edge_multiply(pe, g, k, s, first)
                    ring_loop(pe, NG, 2, [(1, multiply), (0, sum_equal)])
            end_phase()

        setup()
        nodes_into_layer_0()
        edges_first_convolution()
        nodes_between_convolutions()
        edges_second_convolution()
        nodes_into_layer_1()
        edges_layer_1()
        nodes_into_layer_2()
        edges_layer_2()
        nodes_into_layer_3()
        edges_scores()
        softmax_by_source()
        edges_layer_3()


def kernel(**inputs):
    import numpy as np
    import concourse.bacc as bacc
    from concourse.bass_utils import run_bass_kernel_spmd as run

    a = {n: np.asarray(v) for n, v in inputs.items()}
    n_nodes, n_edges = a["x"].shape[0], a["src"].shape[0]
    nodes, edges = padded(n_nodes, ROWS), padded(n_edges, ROWS)

    def pad_rows(v, n, fill=0):
        return np.concatenate([v, np.full((n - v.shape[0],) + v.shape[1:], fill, v.dtype)])

    src = pad_rows(a.pop("src"), edges, n_nodes)
    dst = pad_rows(a.pop("dst"), edges, n_nodes)
    feed = {"x": pad_rows(a.pop("x"), nodes)}
    for name, v in (("src", src), ("dst", dst)):
        feed[name + "_cols"] = v.reshape(edges // P, P).T
        feed[name + "_rows"] = v.reshape(edges // ROWS, ROWS)
        feed[name + "_groups"] = v.reshape(edges // ROWS, J, P).transpose(0, 2, 1).view(np.uint32)
    feed["edge50"] = pad_rows(a.pop("edge_attr_50"), edges).T
    feed["edge128"] = pad_rows(a.pop("edge_attr_128"), edges).T
    for name in ("L2_gnn_W1", "L2_gnn_W2"):
        feed[name] = a.pop(name).T
    feed["L3_gnn_Wexp"] = a.pop("L3_gnn_Wexp").T.reshape(-1)
    feed.update(a)
    feed = {n: np.ascontiguousarray(v) for n, v in feed.items()}

    nc = bacc.Bacc("TRN2", target_bir_lowering=False, num_devices=1)
    ins = {n: nc.dram_tensor(n, v.shape, mybir.dt.from_np(v.dtype), kind="ExternalInput").ap()
           for n, v in feed.items()}
    out = nc.dram_tensor("out", (nodes + ROWS, D), F32, kind="ExternalOutput").ap()
    gnn_kernel(nc, ins, out, n_nodes, n_edges)
    r = run(nc, [feed], core_ids=[0])
    return r.results[0]["out"][:n_nodes]
```

```python
import concourse.bass as bass
from concourse import mybir
from contextlib import ExitStack

F32 = mybir.dt.float32
F16 = mybir.dt.float16
I32 = mybir.dt.int32
U32 = mybir.dt.uint32
ALU = mybir.AluOpType
ACT = mybir.ActivationFunctionType
AX_X = mybir.AxisListType.X

P = 128
D = 128
J = 4
ROWS = J * P
HEADS = 8
HEAD_DIM = D // HEADS
SCALE = HEAD_DIM ** -0.5
EPS = 1e-5
LO_BITS = 9
LO = 1 << LO_BITS
KEYS = 16
SORT_W = KEYS + D
FAR = 1.0e38


def padded(n, unit):
    return -(-n // unit) * unit


def uses(steps, slots, slot):
    return -(-(steps - slot) // slots)


def ring_loop(eng, steps, slots, stages):
    def step(i, u):
        for lag, fn in stages:
            s = (u - lag) % slots
            if isinstance(i, int):
                b = i * slots + u - lag
                if 0 <= b < steps:
                    fn(b, b // slots, s, b < slots)
            else:
                fn(i * slots + (u - lag), i + (u - lag - s) // slots, s, False)

    most = max(lag for lag, _ in stages)
    head = padded(slots + most, slots) // slots
    whole = steps // slots
    for i in range(head):
        for u in range(slots):
            step(i, u)
    with eng.Fori(head, whole) as i:
        for u in range(slots):
            step(i, u)
    for t in range(whole * slots, steps + most):
        step(t // slots, t % slots)


def every_second(fn):
    def stage(b, k, s, first):
        if s % 2 == 0:
            if first:
                fn(b // 2, k, s // 2, True)
            else:
                fn(k * 2 + s // 2, k, s // 2, False)
    return stage


def quad(fn):
    def stage(b, k, s, first):
        fn(b, 2 * k + s // 4, s % 4, first and b < 4)
    return stage


def gnn_kernel(nc, ins, out, n_nodes, n_edges):
    NODES = padded(n_nodes, ROWS)
    EDGES = padded(n_edges, ROWS)
    NB = NODES // ROWS
    NG = EDGES // ROWS
    HI = NODES // LO
    NT = EDGES // P
    assert NB == 2 * NG
    TABLE = NODES + ROWS

    with ExitStack() as ctx:
        def sb(name, shape, dt=F32):
            return ctx.enter_context(nc.sbuf_tensor(name, shape, dt))

        in_use = []

        def sem(name):
            in_use.append(nc.alloc_semaphore(name=name))
            return in_use[-1]

        def sem2(name):
            return [sem(f"{name}_{n}") for n in range(2)]

        def sem4(name):
            return [sem(f"{name}_{n}") for n in range(4)]

        def dram(name, shape, dt=F32):
            return nc.dram_tensor(name, shape, dt, kind="Internal").ap()

        h0, h2 = [dram(n, (NODES, D)) for n in ("h0", "h2")]
        y1, y2, z1, y3 = [dram(n, (TABLE, D)) for n in ("y1", "y2", "z1", "y3")]
        x1h = dram("x1h", (NODES, D))
        x2 = dram("x2", (NODES, D))
        x3 = dram("x3", (NODES, D))
        source_hi = dram("source_hi", (NG * HI, ROWS), F16)
        sorted_rows = dram("sorted_rows", (EDGES + 2, SORT_W))
        source_rows = dram("source_rows", (NG, ROWS))

        psum = [ctx.enter_context(nc.psum_tensor(f"bank{n}", [P, ROWS], F32)) for n in range(8)]
        T = [sb(f"tile{n}", [P, 4 if n < 6 else 2, ROWS]) for n in range(8)]
        same = sb("same", [P, 2, J, ROWS])
        found = sb("found", [P, J, ROWS])
        idx_row = sb("idx_row", [P, 2, ROWS], I32)
        count_row = sb("count_row", [P, 2, ROWS], I32)
        source_row = T[6]

        ident = sb("ident", [P, P])
        ident16 = sb("ident16", [P, P], F16)
        ones = sb("ones", [P, P])
        iota_lo = sb("iota_lo", [P, LO], F16)
        before = sb("before", [P, J, ROWS])
        upper = sb("upper", [P, P])
        spare = sb("spare", [P, J])
        eps = sb("eps", [P, 1])
        zeros = sb("zeros", [P, ROWS])
        minus_ones = sb("minus_ones", [P, KEYS])
        one_on = sb("one_on", [P, P])

        weights = {}
        for name in ("L0_gnn_W1l", "L0_gnn_W1r", "L0_gnn_W2l", "L0_gnn_W2r", "L1_gnn_We2", "L1_gnn_Wn1",
                     "L1_gnn_Wn2", "L3_gnn_Wq", "L3_gnn_Wout"):
            weights[name] = sb("w_" + name, [P, D])
        w_e1 = sb("w_e1", [50, D])
        w_kv = sb("w_kv", [P, 2 * D])
        w_ekv = sb("w_ekv", [P, 2 * D])
        w_1 = sb("w_1", [P, 4, D])
        w_2 = sb("w_2", [P, 3, D])
        w_exp = sb("w_exp", [P, HEADS * HEADS])
        be1 = sb("be1", [P, 1])
        u0 = sb("u0", [P, 1])
        u_cols = sb("u_cols", [P, P])
        rows = {}
        for name in ("L0_gnn_b1", "L0_gnn_b2", "L1_gnn_be2", "L1_gnn_bn1", "L1_gnn_bn2", "L2_gnn_b1",
                     "L2_gnn_b2", "L3_gnn_bout"):
            rows[name] = sb("b_" + name, [P, D])
        z_init = sb("z_init", [P, ROWS])
        y3_init = sb("y3_init", [P, ROWS])
        c1 = sb("c1", [P, D])
        c2 = sb("c2", [P, D])

        src_i = sb("src_i", [P, NT], I32)
        dst_i = sb("dst_i", [P, NT], I32)
        hl_i = sb("hl_i", [P, 4, NT], I32)
        src_f = sb("src_f", [P, NT])
        dst_f = sb("dst_f", [P, NT])
        hl_f = sb("hl_f", [P, 4, NT])
        hi_16 = sb("hi_16", [P, 2, NT], F16)
        dup = sb("dup", [P, 2, NT])
        flag = sb("flag", [P, NT])
        tmp_t = sb("tmp_t", [P, NT])
        dst_add = sb("dst_add", [P, NT])
        sorted_src = sb("sorted_src", [P, NT])
        sorted_add = sb("sorted_add", [P, NT])
        inv_count = sb("inv_count", [P, NT])
        sort_pos = sb("sort_pos", [P, NT])
        is_self = sb("is_self", [P, NT])

        stats = sb("stats", [P, 4, J, 6])
        mean_var = sb("mean_var", [P, 4, J, 2])
        std = sb("std", [P, 4, J])
        rstd = sb("rstd", [P, 4, J])
        shift = sb("shift", [P, 4, J])

        gather_a = sb("gather_a", [P, 2, J], U32)
        gather_b = sb("gather_b", [P, 2, J], U32)
        add_to = sb("add_to", [P, 2, J], U32)

        onehot_hi = sb("onehot_hi", [P, 2, J, HI], F16)
        onehot_lo = sb("onehot_lo", [P, 2, J, LO], F16)
        hi_turned = sb("hi_turned", [HI, 2, J, P], F16)
        hist = sb("hist", [HI, LO])
        hist_run = sb("hist_run", [HI, LO])
        hist_base = sb("hist_base", [HI, LO])
        table = sb("table", [HI, 2, 2, LO], F16)
        row_off = sb("row_off", [HI, 1])
        picked = sb("picked", [P, 2, LO])
        idx_cols = sb("idx_cols", [P, 2, J])
        count_cols = sb("count_cols", [P, J])
        dup_cols = sb("dup_cols", [P, J])
        picked_cols = sb("picked_cols", [P, J])

        score = sb("score", [P, 2, J, SORT_W])
        qk_sum = sb("qk_sum", [P, 2, J * HEADS])
        mixed = sb("mixed", [P, J * HEADS * HEADS])

        ss = sb("ss", [P, NT + 2, KEYS])
        keep = sb("keep", [P, 2, NT])
        drop = sb("drop", [P, 2, NT])
        cum = sb("cum", [P, 2, 2, NT])
        scan_f = sb("scan_f", [P, HEADS, NT])
        scan_b = sb("scan_b", [P, HEADS, NT])
        expd = T[4][:, :, :].rearrange("p s n -> p (s n)")[:, 0:HEADS * NT].rearrange("p (h n) -> p h n", h=HEADS)
        edge_in = sb("edge_in", [P, 2, HEADS])
        turned = sb("turned", [HEADS, 2, P])
        carry = sb("carry", [HEADS, P + 1])
        carry_in = sb("carry_in", [P, HEADS])

        def wait_on_pool(pool, s, value):
            pool.wait_ge(s, value)
            pool.sem_inc(pool_waits, 1)

        pool_waits = nc.alloc_semaphore(name="pool_waits")
        dve_waits = nc.alloc_semaphore(name="dve_waits")

        def block_rows(table_ap, b):
            return table_ap[bass.ds(b * ROWS, ROWS), :].rearrange("(p j) d -> p (j d)", j=J)

        def group_row(table_ap, g):
            return table_ap[bass.ds(g, 1), :].rearrange("a e -> (a e)").partition_broadcast(P)

        def across(row, n=J):
            return row.unsqueeze(1).to_broadcast([P, n, D])

        def jd(ap):
            return ap.rearrange("p (j d) -> p j d", j=J)

        def end_phase():
            nc.clear_and_free_semaphores(in_use)
            in_use.clear()
            nc.all_engine_barrier()

        def setup():
            loads = sem("setup_loads")
            consts = sem("setup_consts")
            vec = sem("setup_vec")
            u_ready = sem("setup_u_cols")
            c_mm = sem("setup_c_products")
            n_loads = [0]

            with nc.Block() as block:
                @block.sync
                def _(sp):
                    def load(dst, src):
                        sp.dma_start(dst, src).then_inc(loads, 16)
                        n_loads[0] += 1
                    load(src_i[:, :], ins["src_cols"])
                    load(dst_i[:, :], ins["dst_cols"])
                    for name, t in weights.items():
                        load(t[:, :], ins[name])
                    load(w_e1[:, :], ins["L1_gnn_We1"])
                    load(w_kv[:, 0:D], ins["L3_gnn_Wk"])
                    load(w_kv[:, D:2 * D], ins["L3_gnn_Wv"])
                    load(w_ekv[:, 0:D], ins["L3_gnn_Wek"])
                    load(w_ekv[:, D:2 * D], ins["L3_gnn_Wev"])
                    load(w_1[:, :, :], ins["L2_gnn_W1"].rearrange("(k p) n -> p k n", p=P))
                    load(w_2[:, :, :], ins["L2_gnn_W2"].rearrange("(k p) n -> p k n", p=P))
                    load(w_exp[:, :], ins["L3_gnn_Wexp"].partition_broadcast(P))
                    load(be1[:, :], ins["L1_gnn_be1"].rearrange("(p a) -> p a", a=1))
                    load(u0[:, :], ins["L2_gnn_u"][0, :].rearrange("(p a) -> p a", a=1))
                    for name, t in rows.items():
                        load(t[:, :], ins[name].partition_broadcast(P))
                    sp.wait_ge(consts, 14)
                    for t in (y1, y2, z1, y3, out):
                        load(t[NODES:TABLE, :].rearrange("(p j) d -> p (j d)", j=J), zeros[:, :])
                    load(sorted_rows[0:1, 0:KEYS], minus_ones[0:1, :])
                    load(sorted_rows[EDGES + 1:EDGES + 2, 0:KEYS], minus_ones[0:1, :])
                    sp.wait_ge(loads, 16 * n_loads[0])

                @block.gpsimd
                def _(pool):
                    pool.memset(ident[:, :], 0.0).then_inc(consts, 1)
                    pool.memset(ones[:, :], 1.0).then_inc(consts, 1)
                    pool.memset(before[:, :, :], 1.0).then_inc(consts, 1)
                    pool.memset(eps[:, :], EPS).then_inc(consts, 1)
                    pool.memset(zeros[:, :], 0.0).then_inc(consts, 1)
                    pool.memset(minus_ones[:, :], -1.0).then_inc(consts, 1)
                    pool.memset(one_on[:, :], 0.0).then_inc(consts, 1)
                    pool.wait_ge(consts, 7)
                    pool.affine_select(out=one_on[:, :], in_=one_on[:, :], compare_op=ALU.not_equal, fill=1.0, base=1,
                                       pattern=[[-1, P]], channel_multiplier=1).then_inc(consts, 1)
                    pool.affine_select(out=ident[:, :], in_=ident[:, :], compare_op=ALU.not_equal, fill=1.0, base=0,
                                       pattern=[[-1, P]], channel_multiplier=1).then_inc(consts, 1)
                    pool.affine_select(out=before[:, :, :], in_=before[:, :, :], compare_op=ALU.is_gt, fill=0.0, base=0,
                                       pattern=[[P, J], [-1, ROWS]], channel_multiplier=1).then_inc(consts, 1)
                    pool.affine_select(out=upper[:, :], in_=ones[:, :], compare_op=ALU.is_gt, fill=0.0, base=0,
                                       pattern=[[1, P]], channel_multiplier=-1).then_inc(consts, 1)
                    pool.iota(found[:, 0, :], [[1, LO]], base=0, channel_multiplier=0,
                              allow_small_or_imprecise_dtypes=True).then_inc(consts, 1)
                    pool.iota(spare[:, :], [[P, J]], base=NODES, channel_multiplier=1,
                              allow_small_or_imprecise_dtypes=True).then_inc(consts, 1)
                    pool.memset(score[:, :, :, :], 0.0).then_inc(consts, 1)

                @block.vector
                def _(dve):
                    dve.wait_ge(consts, 14)
                    dve.wait_ge(loads, 16 * n_loads[0])
                    dve.tensor_copy(ident16[:, :], ident[:, :]).then_inc(vec, 1)
                    dve.tensor_copy(iota_lo[:, :], found[:, 0, :]).then_inc(vec, 1)
                    dve.tensor_copy(u_cols[:, :], u0[:, 0:1].to_broadcast([P, P])).then_inc(u_ready, 1)
                    dve.tensor_copy(jd(z_init[:, :]), across(rows["L1_gnn_bn1"][:, :])).then_inc(vec, 1)
                    for n, (t, f) in enumerate(((src_i, src_f), (dst_i, dst_f))):
                        dve.tensor_copy(f[:, :], t[:, :]).then_inc(vec, 1)
                        dve.tensor_scalar(hl_i[:, 2 * n, :], t[:, :], LO_BITS, None,
                                          ALU.logical_shift_right).then_inc(vec, 1)
                        dve.tensor_scalar(hl_i[:, 2 * n + 1, :], t[:, :], LO - 1, None, ALU.bitwise_and).then_inc(vec, 1)
                    dve.wait_ge(vec, 9)
                    dve.tensor_copy(hl_f[:, :, :], hl_i[:, :, :]).then_inc(vec, 1)
                    for n in range(2):
                        dve.tensor_copy(hi_16[:, n, :], hl_i[:, 2 * n, :]).then_inc(vec, 1)
                    dve.tensor_tensor(is_self[:, :], src_f[:, :], dst_f[:, :], ALU.is_equal).then_inc(vec, 1)
                    dve.wait_ge(c_mm, 1)
                    dve.tensor_tensor(c1[:, :], psum[0][:, 0:D], rows["L2_gnn_b1"][:, :], ALU.add).then_inc(vec, 1)
                    dve.tensor_tensor(c2[:, :], psum[1][:, 0:D], rows["L2_gnn_b2"][:, :], ALU.add).then_inc(vec, 1)
                    dve.wait_ge(vec, 15)
                    dve.tensor_copy(jd(y3_init[:, :]), across(c2[:, :])).then_inc(vec, 1)

                @block.tensor
                def _(pe):
                    pe.wait_ge(u_ready, 1)
                    pe.matmul(psum[0][:, 0:D], u_cols[:, :], w_1[:, 3, :], start=True, stop=True)
                    pe.matmul(psum[1][:, 0:D], u_cols[:, :], w_2[:, 2, :], start=True, stop=True).then_inc(c_mm, 1)
            end_phase()

        def build_onehots(dve, which, g, s):
            dve.tensor_tensor(onehot_hi[:, s, :, :], iota_lo[:, 0:HI].unsqueeze(1).to_broadcast([P, J, HI]),
                              hi_16[:, which, bass.ds(g * J, J)].unsqueeze(2).to_broadcast([P, J, HI]),
                              ALU.is_equal)
            for a in range(J):
                last = dve.tensor_scalar(onehot_lo[:, s, a, :], iota_lo[:, :],
                                         hl_f[:, 2 * which + 1, bass.ds(g * J + a, 1)], None, ALU.is_equal)
            return last

        def node_counting(name, which, bank, row_landed, idx_row, turn_bank=None):
            idx_f = (src_f, dst_f)[which]
            dup_done = sem(name + "_dup_done")
            dup_taken = sem(name + "_dup_taken")
            cols_taken = sem(name + "_cols_taken")
            onehots = sem(name + "_onehots")
            counted = sem(name + "_counted")
            hist_ready = sem(name + "_hist_ready")
            vec = sem(name + "_vec")
            turned_taken = sem(name + "_turned_taken")
            turned_stored = sem2(name + "_turned_stored")

            def repeats_dve(dve):
                def repeats(g, k, s, first):
                    if not first:
                        dve.wait_ge(counted, g - 1)
                    if not (first and g == 0):
                        dve.wait_ge(dup_taken, g)
                    dve.tensor_copy(idx_cols[:, s, :], idx_f[:, bass.ds(g * J, J)]).then_inc(cols_taken, 1)
                    build_onehots(dve, which, g, s).then_inc(onehots, 1)
                    dve.wait_ge(cols_taken, g + 1)
                    dve.wait_ge(row_landed[s], 16 * (k + 1))
                    for a in range(J):
                        w = (a + 1) * P
                        last = dve.scalar_tensor_tensor(found[:, a, 0:w], idx_row[:, s, 0:w],
                                                        idx_cols[:, s, a:a + 1], before[:, a, 0:w],
                                                        ALU.is_equal, ALU.mult, accum_out=dup_cols[:, a:a + 1])
                    last.then_inc(dup_done, 1)
                    dve.wait_ge(dup_done, g + 1)
                    dve.tensor_copy(dup[:, which, bass.ds(g * J, J)], dup_cols[:, :]).then_inc(dup_taken, 1)
                return repeats

            def count_pe(pe):
                def count(g, k, s, first):
                    pe.wait_ge(onehots, g + 1)
                    for a in range(J):
                        last = pe.matmul(bank[0:HI, :], onehot_hi[:, s, a, :], onehot_lo[:, s, a, :],
                                         start=(first and g == 0 and a == 0), stop=False, skip_group_check=True)
                    if turn_bank is not None:
                        if not (first and g == 0):
                            pe.wait_ge(turned_taken, g)
                        for a in range(J):
                            last = pe.transpose(turn_bank[0:HI, :].bitcast(F16)[:, a * P:(a + 1) * P],
                                                onehot_hi[:, s, a, :], ident16[:, :])
                    last.then_inc(counted, 1)
                return count

            def take_turned_act(act):
                def take(g, k, s, first):
                    act.wait_ge(counted, g + 1)
                    if not first:
                        act.wait_ge(turned_stored[s], 16 * k)
                    act.activation(hi_turned[:, s, :, :].rearrange("h a p -> h (a p)"),
                                   turn_bank[0:HI, :].bitcast(F16)[:, 0:ROWS], ACT.Copy).then_inc(turned_taken, 1)
                return take

            def store_turned_act(act):
                def store(g, k, s, first):
                    act.wait_ge(turned_taken, g + 1)
                    act.dma_start(source_hi[bass.ds(g * HI, HI), :],
                                  hi_turned[:, s, :, :].rearrange("h a p -> h (a p)")).then_inc(turned_stored[s], 16)
                return store

            def finish_act(act):
                act.wait_ge(counted, NG)
                act.activation(hist[:, :], bank[0:HI, :], ACT.Copy).then_inc(hist_ready, 1)

            def finish_dve(dve):
                dve.wait_ge(dup_taken, NG)
                dve.tensor_scalar(flag[:, :], dup[:, which, :], 1.0, None, ALU.min).then_inc(vec, 1)
                dve.tensor_tensor(tmp_t[:, :].rearrange("p (g a) -> p g a", a=J),
                                  spare[:, :].unsqueeze(1).to_broadcast([P, NG, J]),
                                  idx_f[:, :].rearrange("p (g a) -> p g a", a=J), ALU.subtract).then_inc(vec, 1)
                dve.wait_ge(vec, 2)
                dve.tensor_tensor(tmp_t[:, :], tmp_t[:, :], flag[:, :], ALU.mult).then_inc(vec, 1)
                dve.wait_ge(vec, 3)
                dve.tensor_tensor(dst_add[:, :], tmp_t[:, :], idx_f[:, :], ALU.add).then_inc(vec, 1)

            return (repeats_dve, count_pe, finish_act, finish_dve, dup_done, take_turned_act, store_turned_act,
                    turned_stored)

        def node_lookup(name, which, running, turn_banks, row_banks, table_bank, keep, turned_landed=None):
            encoded = sem(name + "_encoded")
            turned_mm = sem(name + "_turned_mm")
            turned_ready = sem(name + "_turned_ready")
            rounded = sem(name + "_rounded")
            table_ready = sem(name + "_table_ready")
            row_mm = sem(name + "_row_mm")
            picked_done = sem(name + "_picked_done")
            counted = sem(name + "_counted")
            vec = sem(name + "_vec")
            off_mm = sem(name + "_off_mm")
            base_in = sem(name + "_base_in")
            NTB, NRB = len(turn_banks), len(row_banks)

            def start_dve(dve):
                if running:
                    dve.tensor_tensor_scan(hist_run[:, :], zeros[0:HI, 0:LO], hist[:, :], 0.0, ALU.add,
                                           ALU.add).then_inc(vec, 1)
                    dve.wait_ge(vec, 1)
                    dve.tensor_tensor(hist_base[:, :], hist_run[:, :], hist[:, :], ALU.subtract).then_inc(vec, 1)
                    dve.wait_ge(off_mm, 1)
                    dve.tensor_copy(row_off[:, :], row_banks[0][0:HI, 0:1]).then_inc(vec, 1)
                    dve.wait_ge(vec, 3)
                    dve.tensor_scalar(hist_base[:, :], hist_base[:, :], row_off[:, 0:1], None,
                                      ALU.add).then_inc(vec, 1)
                else:
                    dve.tensor_copy(table[:, 0, 0, :], hist[:, :]).then_inc(vec, 1)
                    dve.wait_ge(vec, 1)
                    dve.tensor_tensor(table[:, 0, 1, :], hist[:, :], table[:, 0, 0, :],
                                      ALU.subtract).then_inc(table_ready, 1)

            def start_pe(pe):
                if running:
                    pe.wait_ge(vec, 2)
                    pe.matmul(row_banks[0][0:HI, 0:1], upper[0:HI, 0:HI], hist_run[:, LO - 1:LO], start=True,
                              stop=True).then_inc(off_mm, 1)
                    pe.wait_ge(vec, 4)
                    pe.matmul(table_bank[0:HI, :], ident[0:HI, 0:HI], hist_base[:, :], start=True, stop=False,
                              skip_group_check=True).then_inc(base_in, 1)
                else:
                    pe.wait_ge(table_ready, 1)

            def encode_dve(dve):
                def encode(g, k, s, first):
                    if not first:
                        dve.wait_ge(picked_done, J * (g - 1))
                        if running:
                            dve.wait_ge(counted, g - 1)
                        else:
                            dve.wait_ge(turned_mm, g - 1)
                    build_onehots(dve, which, g, s).then_inc(encoded, 1)
                    if running:
                        dve.wait_ge(rounded, g + 1)
                        if not first:
                            dve.wait_ge(row_mm, J * (g - 1))
                        dve.tensor_tensor(table[:, s, 1, :], table_bank[0:HI, :], table[:, s, 0, :],
                                          ALU.subtract).then_inc(table_ready, 1)
                return encode

            def pick_dve(dve):
                def pick(g, k, s, first):
                    for a in range(J):
                        dve.wait_ge(row_mm, g * J + (a + 1))
                        if not (first and g == 0 and a < 2):
                            dve.wait_ge(picked_done, g * J + (a - 1))
                        dve.tensor_tensor_reduce(picked[:, a % 2, :], row_banks[a % NRB][:, :],
                                                 onehot_lo[:, s, a, :], 1.0, 0.0, ALU.mult, ALU.add,
                                                 picked_cols[:, a:a + 1]).then_inc(picked_done, 1)
                    dve.wait_ge(picked_done, J * (g + 1))
                    keep(dve, g)
                return pick

            def turn_pe(pe):
                def turn(g, k, s, first):
                    pe.wait_ge(encoded, g + 1)
                    if not first or g >= NTB:
                        pe.wait_ge(turned_ready, g - (NTB - 1))
                    for a in range(J):
                        last = pe.transpose(turn_banks[s % NTB][0:HI, :].bitcast(F16)[:, a * P:(a + 1) * P],
                                            onehot_hi[:, s, a, :], ident16[:, :])
                    last.then_inc(turned_mm, 1)
                return turn

            def count_pe(pe):
                def count(g, k, s, first):
                    pe.wait_ge(encoded, g + 1)
                    pe.wait_ge(table_ready, g + 1)
                    for a in range(J):
                        last = pe.matmul(table_bank[0:HI, :], onehot_hi[:, s, a, :], onehot_lo[:, s, a, :],
                                         start=False, stop=False, skip_group_check=True)
                    last.then_inc(counted, 1)
                return count

            def load_turned_sp(sp):
                def load(g, k, s, first):
                    if not first:
                        sp.wait_ge(row_mm, J * (g - 1))
                    sp.dma_start(hi_turned[:, s, :, :].rearrange("h a p -> h (a p)"),
                                 source_hi[bass.ds(g * HI, HI), :]).then_inc(turned_landed[s], 16)
                return load

            def rows_pe(pe):
                def rows_of(g, k, s, first):
                    if turned_landed is not None:
                        pe.wait_ge(turned_landed[s], 16 * (k + 1))
                        pe.wait_ge(table_ready, g + 1)
                    else:
                        pe.wait_ge(turned_ready, g + 1)
                    t = s if running else 0
                    for a in range(J):
                        if not (first and g == 0 and a < NRB):
                            pe.wait_ge(picked_done, g * J + (a + 1 - NRB))
                        for part in range(2):
                            last = pe.matmul(row_banks[a % NRB][:, :], hi_turned[:, s, a, :],
                                             table[:, t, part, :], start=(part == 0), stop=(part == 1))
                        last.then_inc(row_mm, 1)
                return rows_of

            def start_act(act):
                if running:
                    act.wait_ge(base_in, 1)

            def round_act(act):
                def round_table(g, k, s, first):
                    if not first:
                        act.wait_ge(row_mm, J * (g - 1))
                    if not (first and g == 0):
                        act.wait_ge(counted, g)
                    act.activation(table[:, s, 0, :], table_bank[0:HI, :], ACT.Copy).then_inc(rounded, 1)
                return round_table

            def take_act(act):
                def take(g, k, s, first):
                    if not first:
                        act.wait_ge(row_mm, J * (g - 1))
                    act.wait_ge(turned_mm, g + 1)
                    act.activation(hi_turned[:, s, :, :].rearrange("h a p -> h (a p)"),
                                   turn_banks[s % NTB][0:HI, :].bitcast(F16)[:, 0:ROWS],
                                   ACT.Copy).then_inc(turned_ready, 1)
                return take

            return (start_dve, start_pe, start_act, encode_dve, pick_dve, turn_pe, rows_pe, round_act, take_act,
                    count_pe, load_turned_sp)

        def norm_semaphores(name):
            return [sem(name + n) for n in ("_stats_done", "_var_ready", "_std_ready", "_rstd_done",
                                            "_shift_ready")]

        def norm_measure(norm, dve, x, b, s):
            stats_done, _, _, _, _ = norm
            for j in range(J):
                last = dve.bn_stats(stats[:, s, j, :], x[:, j * D:(j + 1) * D])
            last.then_inc(stats_done, 1)

        def norm_gather(norm, dve, b, s):
            stats_done, var_ready, _, _, _ = norm
            dve.wait_ge(stats_done, b + 1)
            dve.sem_inc(dve_waits, 1)
            for j in range(J):
                last = dve.bn_aggr(mean_var[:, s, j, :], stats[:, s, j, :])
            last.then_inc(var_ready, 1)

        def norm_statistics(norm, dve, x, b, s):
            norm_measure(norm, dve, x, b, s)
            norm_gather(norm, dve, b, s)

        def norm_root(norm, act, b, s):
            _, var_ready, std_ready, _, _ = norm
            act.wait_ge(var_ready, b + 1)
            act.activation(std[:, s, :], mean_var[:, s, :, 1], ACT.Sqrt, bias=eps[:, 0:1]).then_inc(std_ready, 1)

        def norm_scale(norm, dve, b, s):
            _, _, std_ready, rstd_done, _ = norm
            dve.wait_ge(std_ready, b + 1)
            dve.reciprocal(rstd[:, s, :], std[:, s, :]).then_inc(rstd_done, 1)

        def norm_shift(norm, dve, b, s):
            _, _, _, rstd_done, shift_ready = norm
            dve.wait_ge(rstd_done, b + 1)
            dve.scalar_tensor_tensor(shift[:, s, :], mean_var[:, s, :, 0], -1.0, rstd[:, s, :], ALU.mult,
                                     ALU.mult).then_inc(shift_ready, 1)

        def norm_factors(norm, dve, b, s):
            norm_scale(norm, dve, b, s)
            norm_shift(norm, dve, b, s)

        def norm_apply(norm, act, out_t, x, b, s):
            _, _, _, _, shift_ready = norm
            act.wait_ge(shift_ready, b + 1)
            for j in range(J):
                last = act.activation(out_t[:, j * D:(j + 1) * D], x[:, j * D:(j + 1) * D], ACT.Relu,
                                      bias=shift[:, s, j:j + 1], scale=rstd[:, s, j:j + 1])
            return last

        def products(pe, bank, left, right, width=D):
            for j in range(J):
                last = pe.matmul(bank[:, j * width:(j + 1) * width], left[:, j * P:(j + 1) * P], right,
                                 start=True, stop=True)
            return last

        def turn_tiles(pe, bank, t):
            for j in range(J):
                last = pe.transpose(bank[:, j * P:(j + 1) * P], t[:, j * D:(j + 1) * D], ident[:, :])
            return last

        def all_landed(eng, sems, steps):
            for n, q in enumerate(sems):
                eng.wait_ge(q, 16 * uses(steps, len(sems), n))

        def nodes_into_layer_0():
            norm = norm_semaphores("nA")
            x_landed = sem4("nA_x_landed")
            h_stored = sem4("nA_h_stored")
            y_stored = sem4("nA_y_stored")
            h_done = sem("nA_h_done")
            turned_mm = sem("nA_turned_mm")
            ht_ready = sem("nA_ht_ready")
            y_mm = sem("nA_y_mm")
            y_done = sem("nA_y_done")
            yb_done = sem("nA_yb_done")
            row_landed = sem2("nA_row_landed")
            (repeats_dve, count_pe, finish_act, finish_dve, dup_done, _, _,
             _) = node_counting("nA", 1, psum[7], row_landed, idx_row)

            with nc.Block() as block:
                @block.sync
                def _(sp):
                    def load(b, k, s, first):
                        if not first:
                            sp.wait_ge(h_done, b - 3)
                        sp.dma_start(T[0][:, s, :], block_rows(ins["x"], b)).then_inc(x_landed[s], 16)

                    def load_row(g, k, s, first):
                        if not first:
                            sp.wait_ge(dup_done, g - 1)
                        sp.dma_start(idx_row[:, s, :], group_row(ins["dst_rows"], g)).then_inc(row_landed[s], 16)

                    def store_h(b, k, s, first):
                        sp.wait_ge(h_done, b + 1)
                        sp.dma_start(block_rows(h0, b), T[1][:, s, :]).then_inc(h_stored[s], 16)

                    def store_y(b, k, s, first):
                        sp.wait_ge(yb_done, b + 1)
                        sp.dma_start(block_rows(y1, b), T[2][:, s, :]).then_inc(y_stored[s], 16)
                    ring_loop(sp, NB, 4, [(0, load), (0, every_second(load_row)), (4, store_h), (9, store_y)])
                    all_landed(sp, h_stored, NB)
                    all_landed(sp, y_stored, NB)

                @block.gpsimd
                def _(pool):
                    def add_bias(b, k, s, first):
                        wait_on_pool(pool, y_done, b + 1)
                        pool.tensor_tensor(jd(T[2][:, s, :]), jd(T[2][:, s, :]), across(rows["L0_gnn_b1"][:, :]),
                                           ALU.add).then_inc(yb_done, 1)
                    ring_loop(pool, NB, 4, [(0, add_bias)])

                @block.vector
                def _(dve):
                    def measure(b, k, s, first):
                        dve.wait_ge(x_landed[s], 16 * (k + 1))
                        norm_measure(norm, dve, T[0][:, s, :], b, s)

                    def scale(b, k, s, first):
                        if not first:
                            dve.wait_ge(h_done, b - 3)
                        norm_scale(norm, dve, b, s)

                    def gather_stats(b, k, s, first):
                        norm_gather(norm, dve, b, s)

                    def shift_of(b, k, s, first):
                        norm_shift(norm, dve, b, s)
                    ring_loop(dve, NB, 4, [(0, measure), (1, scale), (0, gather_stats), (1, shift_of),
                                           (0, every_second(repeats_dve(dve)))])
                    finish_dve(dve)

                @block.scalar
                def _(act):
                    def copy_turned(b, k, s, first):
                        act.wait_ge(turned_mm, b + 1)
                        if not first or b >= 2:
                            act.wait_ge(y_mm, b - 1)
                        act.activation(T[6][:, s % 2, :], psum[s % 2][:, :], ACT.Copy).then_inc(ht_ready, 1)

                    def finish(b, k, s, first):
                        act.wait_ge(y_mm, b + 1)
                        if not first:
                            act.wait_ge(y_stored[s], 16 * k)
                        act.activation(T[2][:, s, :], psum[2 + s % 2][:, :], ACT.Copy).then_inc(y_done, 1)

                    def root(b, k, s, first):
                        norm_root(norm, act, b, s)

                    def normalise(b, k, s, first):
                        if not first:
                            act.wait_ge(h_stored[s], 16 * k)
                            act.wait_ge(turned_mm, b - 3)
                        norm_apply(norm, act, T[1][:, s, :], T[0][:, s, :], b, s).then_inc(h_done, 1)
                    ring_loop(act, NB, 4, [(6, finish), (4, copy_turned), (2, normalise), (0, root)])
                    finish_act(act)

                @block.tensor
                def _(pe):
                    def multiply(b, k, s, first):
                        pe.wait_ge(ht_ready, b + 1)
                        if not first or b >= 2:
                            pe.wait_ge(y_done, b - 1)
                        products(pe, psum[2 + s % 2], T[6][:, s % 2, :],
                                 weights["L0_gnn_W1r"][:, :]).then_inc(y_mm, 1)

                    def turn(b, k, s, first):
                        pe.wait_ge(h_done, b + 1)
                        if not first or b >= 2:
                            pe.wait_ge(ht_ready, b - 1)
                        turn_tiles(pe, psum[s % 2], T[1][:, s, :]).then_inc(turned_mm, 1)
                    ring_loop(pe, NB, 4, [(5, multiply), (3, turn), (1, every_second(count_pe(pe)))])
            end_phase()

        def nodes_into_layer_1():
            norm = norm_semaphores("nE")
            y_landed = sem4("nE_y_landed")
            y1_landed = sem4("nE_y1_landed")
            h_stored = sem4("nE_h_stored")
            xh_stored = sem4("nE_xh_stored")
            turned_mm = sem("nE_turned_mm")
            ht_ready = sem("nE_ht_ready")
            x_mm = sem("nE_x_mm")
            x_done = sem("nE_x_done")
            xb_done = sem("nE_xb_done")
            h_done = sem("nE_h_done")
            xh_done = sem("nE_xh_done")

            with nc.Block() as block:
                @block.sync
                def _(sp):
                    def load(b, k, s, first):
                        if not first:
                            sp.wait_ge(turned_mm, b - 3)
                        sp.dma_start(T[1][:, s, :], block_rows(y1, b)).then_inc(y1_landed[s], 16)
                        if not first:
                            sp.wait_ge(x_done, b - 3)
                        sp.dma_start(T[0][:, s, :], block_rows(y2, b)).then_inc(y_landed[s], 16)

                    def store(b, k, s, first):
                        sp.wait_ge(h_done, b + 1)
                        sp.dma_start(block_rows(h2, b), T[3][:, s, :]).then_inc(h_stored[s], 16)
                        sp.wait_ge(xh_done, b + 1)
                        sp.dma_start(block_rows(x1h, b), T[4][:, s, :]).then_inc(xh_stored[s], 16)
                    ring_loop(sp, NB, 4, [(0, load), (6, store)])
                    all_landed(sp, h_stored, NB)
                    all_landed(sp, xh_stored, NB)

                @block.gpsimd
                def _(pool):
                    def add_bias(b, k, s, first):
                        wait_on_pool(pool, x_done, b + 1)
                        if not first:
                            wait_on_pool(pool, xh_stored[s], 16 * k)
                        pool.tensor_tensor(jd(T[4][:, s, :]), jd(T[2][:, s, :]), across(rows["L1_gnn_bn2"][:, :]),
                                           ALU.add).then_inc(xb_done, 1)
                    ring_loop(pool, NB, 4, [(0, add_bias)])

                @block.vector
                def _(dve):
                    def add_h(b, k, s, first):
                        dve.wait_ge(h_done, b + 1)
                        dve.wait_ge(xb_done, b + 1)
                        dve.tensor_tensor(T[4][:, s, :], T[4][:, s, :], T[3][:, s, :], ALU.add).then_inc(xh_done, 1)

                    def add_y(b, k, s, first):
                        dve.wait_ge(x_mm, b + 1)
                        dve.wait_ge(y_landed[s], 16 * (k + 1))
                        if not first:
                            dve.wait_ge(h_done, b - 3)
                            dve.wait_ge(xb_done, b - 3)
                        dve.tensor_tensor(T[2][:, s, :], psum[2 + s % 2][:, :], T[0][:, s, :],
                                          ALU.add).then_inc(x_done, 1)

                    def measure(b, k, s, first):
                        dve.wait_ge(x_done, b + 1)
                        norm_measure(norm, dve, T[2][:, s, :], b, s)

                    def scale(b, k, s, first):
                        norm_scale(norm, dve, b, s)

                    def gather_stats(b, k, s, first):
                        norm_gather(norm, dve, b, s)

                    def shift_of(b, k, s, first):
                        norm_shift(norm, dve, b, s)
                    ring_loop(dve, NB, 4, [(0, add_y), (1, scale), (0, measure), (1, shift_of), (3, add_h),
                                           (0, gather_stats)])

                @block.scalar
                def _(act):
                    def copy_turned(b, k, s, first):
                        act.wait_ge(turned_mm, b + 1)
                        if not first or b >= 2:
                            act.wait_ge(x_mm, b - 1)
                        act.activation(T[6][:, s % 2, :], psum[s % 2][:, :], ACT.Relu).then_inc(ht_ready, 1)

                    def root(b, k, s, first):
                        norm_root(norm, act, b, s)

                    def normalise(b, k, s, first):
                        if not first:
                            act.wait_ge(h_stored[s], 16 * k)
                            act.wait_ge(xh_done, b - 3)
                        norm_apply(norm, act, T[3][:, s, :], T[2][:, s, :], b, s).then_inc(h_done, 1)
                    ring_loop(act, NB, 4, [(0, copy_turned), (2, root), (3, normalise)])

                @block.tensor
                def _(pe):
                    def multiply(b, k, s, first):
                        pe.wait_ge(ht_ready, b + 1)
                        if not first or b >= 2:
                            pe.wait_ge(x_done, b - 1)
                        products(pe, psum[2 + s % 2], T[6][:, s % 2, :],
                                 weights["L0_gnn_W2r"][:, :]).then_inc(x_mm, 1)

                    def turn(b, k, s, first):
                        pe.wait_ge(y1_landed[s], 16 * (k + 1))
                        if not first or b >= 2:
                            pe.wait_ge(ht_ready, b - 1)
                        turn_tiles(pe, psum[s % 2], T[1][:, s, :]).then_inc(turned_mm, 1)
                    ring_loop(pe, NB, 4, [(0, turn), (1, multiply)])
            end_phase()

        def nodes_into_layer_2():
            z_landed = sem4("nG_z_landed")
            x_landed = sem4("nG_x_landed")
            x2_stored = sem4("nG_x2_stored")
            silu_done = sem("nG_silu_done")
            turned_mm = sem("nG_turned_mm")
            st_ready = sem("nG_st_ready")
            x_mm = sem("nG_x_mm")
            x_done = sem("nG_x_done")

            with nc.Block() as block:
                @block.sync
                def _(sp):
                    def load(b, k, s, first):
                        if not first:
                            sp.wait_ge(silu_done, b - 3)
                        sp.dma_start(T[0][:, s, :], block_rows(z1, b)).then_inc(z_landed[s], 16)

                    def load_x(b, k, s, first):
                        if not first:
                            sp.wait_ge(x_done, b - 3)
                        sp.dma_start(T[1][:, s, :], block_rows(x1h, b)).then_inc(x_landed[s], 16)
                    ring_loop(sp, NB, 4, [(0, load), (2, load_x)])

                @block.scalar
                def _(act):
                    def store(b, k, s, first):
                        act.wait_ge(x_done, b + 1)
                        act.dma_start(block_rows(x2, b), T[3][:, s, :]).then_inc(x2_stored[s], 16)

                    def silu(b, k, s, first):
                        act.wait_ge(z_landed[s], 16 * (k + 1))
                        if not first:
                            act.wait_ge(turned_mm, b - 3)
                        act.activation(T[2][:, s, :], T[0][:, s, :], ACT.Silu).then_inc(silu_done, 1)
                    ring_loop(act, NB, 4, [(0, silu), (3, store)])
                    all_landed(act, x2_stored, NB)

                @block.vector
                def _(dve):
                    def add_x(b, k, s, first):
                        dve.wait_ge(x_mm, b + 1)
                        dve.wait_ge(x_landed[s], 16 * (k + 1))
                        if not first:
                            dve.wait_ge(x2_stored[s], 16 * k)
                        dve.tensor_tensor(T[3][:, s, :], psum[2 + s % 2][:, :], T[1][:, s, :],
                                          ALU.add).then_inc(x_done, 1)

                    def copy_turned(b, k, s, first):
                        dve.wait_ge(turned_mm, b + 1)
                        if not first or b >= 2:
                            dve.wait_ge(x_mm, b - 1)
                        dve.tensor_copy(T[6][:, s % 2, :], psum[s % 2][:, :]).then_inc(st_ready, 1)
                    ring_loop(dve, NB, 4, [(2, add_x), (0, copy_turned)])

                @block.tensor
                def _(pe):
                    def multiply(b, k, s, first):
                        pe.wait_ge(st_ready, b + 1)
                        if not first or b >= 2:
                            pe.wait_ge(x_done, b - 1)
                        products(pe, psum[2 + s % 2], T[6][:, s % 2, :],
                                 weights["L1_gnn_Wn2"][:, :]).then_inc(x_mm, 1)

                    def turn(b, k, s, first):
                        pe.wait_ge(silu_done, b + 1)
                        if not first or b >= 2:
                            pe.wait_ge(st_ready, b - 1)
                        turn_tiles(pe, psum[s % 2], T[2][:, s, :]).then_inc(turned_mm, 1)
                    ring_loop(pe, NB, 4, [(1, multiply), (0, turn)])
            end_phase()

        def nodes_into_layer_3():
            norm = norm_semaphores("nI")
            x_landed = [sem(f"nI_x_landed_{n}") for n in range(8)]
            y_landed = sem4("nI_y_landed")
            x3_stored = sem4("nI_x3_stored")
            h_done = sem("nI_h_done")
            turned_mm = sem("nI_turned_mm")
            ht_ready = sem("nI_ht_ready")
            y_mm = sem("nI_y_mm")
            y_done = sem("nI_y_done")
            x3_done = sem("nI_x3_done")
            o_done = sem("nI_o_done")
            o_stored = sem4("nI_o_stored")

            def x_tile(s8):
                return (T[2], T[3])[s8 // 4][:, s8 % 4, :]

            with nc.Block() as block:
                @block.sync
                def _(sp):
                    def load_x(b, k, s, first):
                        if not first:
                            sp.wait_ge(x3_done, b - 7)
                        sp.dma_start(x_tile(s), block_rows(x2, b)).then_inc(x_landed[s], 16)

                    def load_y(b, k, s, first):
                        if not first:
                            sp.wait_ge(x3_done, b - 3)
                        sp.dma_start(T[0][:, s, :], block_rows(y3, b)).then_inc(y_landed[s], 16)

                    def store(b, k, s, first):
                        sp.wait_ge(x3_done, b + 1)
                        sp.dma_start(block_rows(x3, b), T[4][:, s, :]).then_inc(x3_stored[s], 16)

                    def store_out(b, k, s, first):
                        sp.wait_ge(o_done, b + 1)
                        sp.dma_start(block_rows(out, b), T[5][:, s, :]).then_inc(o_stored[s], 16)
                    ring_loop(sp, NB, 8, [(0, load_x), (3, quad(load_y)), (7, quad(store)), (8, quad(store_out))])
                    all_landed(sp, x3_stored, NB)
                    all_landed(sp, o_stored, NB)

                @block.gpsimd
                def _(pool):
                    def add_bias(b, k, s, first):
                        wait_on_pool(pool, x3_done, b + 1)
                        if not first:
                            wait_on_pool(pool, o_stored[s], 16 * k)
                        pool.tensor_tensor(jd(T[5][:, s, :]), jd(T[4][:, s, :]), across(rows["L3_gnn_bout"][:, :]),
                                           ALU.add).then_inc(o_done, 1)
                    ring_loop(pool, NB, 4, [(0, add_bias)])

                @block.vector
                def _(dve):
                    def finish(b, k, s, first):
                        s4 = s % 4
                        dve.wait_ge(y_mm, b + 1)
                        dve.wait_ge(y_landed[s4], 16 * (2 * k + s // 4 + 1))
                        dve.tensor_tensor(T[0][:, s4, :], psum[2 + s % 2][:, :], T[0][:, s4, :],
                                          ALU.add).then_inc(y_done, 1)
                        dve.wait_ge(y_done, b + 1)
                        if not first or s >= 4:
                            dve.wait_ge(x3_stored[s4], 16 * (2 * k + s // 4))
                            dve.wait_ge(o_done, b - 3)
                        dve.scalar_tensor_tensor(T[4][:, s4, :], T[0][:, s4, :], 0.0, x_tile(s), ALU.max,
                                                 ALU.add).then_inc(x3_done, 1)

                    def measure(b, k, s, first):
                        dve.wait_ge(x_landed[s], 16 * (k + 1))
                        norm_measure(norm, dve, x_tile(s), b, s % 4)

                    def scale(b, k, s, first):
                        if not first:
                            dve.wait_ge(h_done, b - 3)
                        norm_scale(norm, dve, b, s)

                    def gather_stats(b, k, s, first):
                        norm_gather(norm, dve, b, s)

                    def shift_of(b, k, s, first):
                        norm_shift(norm, dve, b, s)
                    ring_loop(dve, NB, 8, [(0, measure), (1, quad(scale)), (0, quad(gather_stats)),
                                           (1, quad(shift_of)), (5, finish)])

                @block.scalar
                def _(act):
                    def copy_turned(b, k, s, first):
                        act.wait_ge(turned_mm, b + 1)
                        if not first or b >= 2:
                            act.wait_ge(y_mm, b - 1)
                        act.activation(T[6][:, s % 2, :], psum[s % 2][:, :], ACT.Copy).then_inc(ht_ready, 1)

                    def normalise(b, k, s, first):
                        if not first or s >= 4:
                            act.wait_ge(turned_mm, b - 3)
                        norm_apply(norm, act, T[1][:, s % 4, :], x_tile(s), b, s % 4).then_inc(h_done, 1)

                    def root(b, k, s, first):
                        norm_root(norm, act, b, s)
                    ring_loop(act, NB, 8, [(3, quad(copy_turned)), (2, normalise), (0, quad(root))])

                @block.tensor
                def _(pe):
                    def multiply(b, k, s, first):
                        pe.wait_ge(ht_ready, b + 1)
                        if not first or b >= 2:
                            pe.wait_ge(x3_done, b - 1)
                        products(pe, psum[2 + s % 2], T[6][:, s % 2, :], w_2[:, 0, :]).then_inc(y_mm, 1)

                    def turn(b, k, s, first):
                        pe.wait_ge(h_done, b + 1)
                        if not first or b >= 2:
                            pe.wait_ge(ht_ready, b - 1)
                        turn_tiles(pe, psum[s % 2], T[1][:, s, :]).then_inc(turned_mm, 1)
                    ring_loop(pe, NB, 4, [(4, multiply), (2, turn)])
            end_phase()

        def summed_edges(name, which, into, weight, messages, scaled=False, sum_banks=psum[0:2],
                         out_banks=psum[2:4]):

            idx_f = (sorted_src, dst_f)[which]
            idx_rows = (source_rows, ins["dst_rows"])[which]
            add_rows = (sorted_add, dst_add)[which]
            row_in = (source_row, idx_row)[which]
            row_landed = sem2(name + "_row_landed")
            same_ready = sem(name + "_same_ready")
            sum_mm = sem(name + "_sum_mm")
            sum_ready = sem(name + "_sum_ready")
            out_mm = sem(name + "_out_mm")
            out_done = sem(name + "_out_done")
            add_to_ready = sem(name + "_add_to_ready")
            added = sem2(name + "_added")

            def load_row(sp, g, k, s, first):
                if not first:
                    sp.wait_ge(same_ready, g - 1)
                sp.dma_start(row_in[:, s, :], group_row(idx_rows, g)).then_inc(row_landed[s], 16)

            def compare(dve, g, k, s, first):
                dve.wait_ge(row_landed[s], 16 * (k + 1))
                if not first:
                    dve.wait_ge(sum_mm, g - 1)
                for a in range(J):
                    last = dve.tensor_scalar(same[:, s, a, :], row_in[:, s, :],
                                             idx_f[:, bass.ds(g * J + a, 1)], None, ALU.is_equal)
                last.then_inc(same_ready, 1)

            def sum_equal(pe, g, k, s, first):
                pe.wait_ge(same_ready, g + 1)
                n = len(sum_banks)
                if not first or g >= n:
                    pe.wait_ge(sum_ready, g - (n - 1))
                for a in range(J):
                    last = pe.matmul(sum_banks[s % n][:, :], messages[:, s, a * D:(a + 1) * D], same[:, s, a, :],
                                     start=(a == 0), stop=(a == J - 1))
                last.then_inc(sum_mm, 1)

            def copy_sum(act, g, k, s, first):
                act.wait_ge(sum_mm, g + 1)
                if not first:
                    act.wait_ge(out_mm, g - 1)
                act.activation(T[2][:, s, :], sum_banks[s % len(sum_banks)][:, :], ACT.Copy).then_inc(sum_ready, 1)

            def copy_rows(act, g, k, s, first):
                if not first:
                    act.wait_ge(added[s], 16 * J * k)
                act.activation(add_to[:, s, :], add_rows[:, bass.ds(g * J, J)],
                               ACT.Copy).then_inc(add_to_ready, 1)

            def multiply(pe, g, k, s, first):
                pe.wait_ge(sum_ready, g + 1)
                n = len(out_banks)
                if not first or g >= n:
                    pe.wait_ge(out_done, g - (n - 1))
                products(pe, out_banks[s % n], T[2][:, s, :], weight).then_inc(out_mm, 1)

            def take_out(dve, g, k, s, first):
                dve.wait_ge(out_mm, g + 1)
                if not first:
                    dve.wait_ge(added[s], 16 * J * k)
                if scaled:
                    dve.tensor_tensor(jd(T[3][:, s, :]), jd(out_banks[s % len(out_banks)][:, :]),
                                      inv_count[:, bass.ds(g * J, J)].unsqueeze(2).to_broadcast([P, J, D]),
                                      ALU.mult).then_inc(out_done, 1)
                else:
                    dve.tensor_copy(T[3][:, s, :], out_banks[s % len(out_banks)][:, :]).then_inc(out_done, 1)

            def add(pool, g, k, s, first):
                wait_on_pool(pool, out_done, g + 1)
                wait_on_pool(pool, add_to_ready, g + 1)
                if not (first and g == 0):
                    wait_on_pool(pool, added[1 - s], 16 * J * (k + s))
                for a in range(J):
                    pool.indirect_dma_start(into, bass.IndirectOffsetOnAxis(ap=add_to[:, s, a:a + 1], axis=0),
                                            T[3][:, s, a * D:(a + 1) * D], None,
                                            compute_op=ALU.add).then_inc(added[s], 16)

            def all_added(pool):
                for n, q in enumerate(added):
                    pool.wait_ge(q, 16 * J * uses(NG, 2, n))

            return (load_row, compare, sum_equal, copy_sum, copy_rows, multiply, take_out, add, all_added,
                    sum_mm)

        def load_index(sp, idx, name, landed, used, per_group, g, k, s, first):
            if not first:
                sp.wait_ge(used[s], 16 * per_group * k)
            sp.dma_start(idx[:, s, :],
                         ins[name][bass.ds(g, 1), :, :].rearrange("a p j -> (a p) j")).then_inc(landed[s], 16)

        def gather(pool, into, idx, s, table_ap, done):
            for a in range(J):
                pool.indirect_dma_start(into[:, s, a * D:(a + 1) * D], None, table_ap,
                                        bass.IndirectOffsetOnAxis(ap=idx[:, s, a:a + 1], axis=0)).then_inc(done, 16)

        def edges_convolution(name, h, y, weight, lookup=None, counting=None, bias_fill=None, fill=None):
            (edge_load_row, edge_compare, edge_sum_equal, edge_copy_sum, edge_copy_rows, edge_multiply,
             edge_take_out, edge_add, edge_all_added, edge_sum_mm) = summed_edges(
                 name, 1, y, weight, T[0] if lookup is not None else T[1], scaled=True)
            if lookup is not None:
                (start_dve, start_pe, start_act, encode_dve, pick_dve, turn_pe, rows_pe, _, take_act,
                 _, _) = lookup
            if counting is not None:
                (repeats_dve, count_pe, finish_act, _, dup_done, take_turned_act, store_turned_act,
                 turned_stored), src_row_landed = counting
                relu_done = sem(name + "_relu_done")
            idx_landed = sem2(name + "_idx_landed")
            gathered = sem2(name + "_gathered")
            filled = sem(name + "_filled")
            x_landed = sem4(name + "_x_landed")
            xb_done = sem(name + "_xb_done")
            xb_stored = sem4(name + "_xb_stored")

            with nc.Block() as block:
                @block.sync
                def _(sp):
                    def load(g, k, s, first):
                        load_index(sp, gather_a, "src_groups", idx_landed, gathered, J, g, k, s, first)
                        edge_load_row(sp, g, k, s, first)
                        if bias_fill is not None:
                            for n in range(2):
                                if not first:
                                    sp.wait_ge(xb_stored[2 * s + n], 16 * k)
                                sp.dma_start(T[4][:, 2 * s + n, :], block_rows(ins["x"], 2 * g + n)
                                             ).then_inc(x_landed[2 * s + n], 16)
                        if counting is not None:
                            if not first:
                                sp.wait_ge(dup_done, g - 1)
                            sp.dma_start(count_row[:, s, :], group_row(ins["src_rows"], g)
                                         ).then_inc(src_row_landed[s], 16)
                        if fill is not None:
                            fill_blocks(sp, fill, g, filled)
                    ring_loop(sp, NG, 2, [(0, load)])
                    if fill is not None:
                        sp.wait_ge(filled, 16 * NB)

                @block.gpsimd
                def _(pool):
                    def fetch(g, k, s, first):
                        wait_on_pool(pool, idx_landed[s], 16 * (k + 1))
                        if not first:
                            wait_on_pool(pool, edge_sum_mm if counting is None else relu_done, g - 1)
                        gather(pool, T[0], gather_a, s, h, gathered[s])

                    def add(g, k, s, first):
                        edge_add(pool, g, k, s, first)
                    ring_loop(pool, NG, 2, [(0, fetch), (2, add)])
                    edge_all_added(pool)

                @block.vector
                def _(dve):
                    def compare(g, k, s, first):
                        edge_compare(dve, g, k, s, first)

                    def take_out(g, k, s, first):
                        edge_take_out(dve, g, k, s, first)

                    def add_bias(g, k, s, first):
                        for n in range(2):
                            dve.wait_ge(x_landed[2 * s + n], 16 * (k + 1))
                            dve.tensor_tensor(jd(T[4][:, 2 * s + n, :]), jd(T[4][:, 2 * s + n, :]),
                                              across(rows["L0_gnn_b2"][:, :]), ALU.add).then_inc(xb_done, 1)
                    if lookup is not None:
                        start_dve(dve)
                        ring_loop(dve, NG, 2, [(2, take_out), (0, encode_dve(dve)), (0, compare),
                                               (1, pick_dve(dve)), (1, add_bias)])
                    else:
                        ring_loop(dve, NG, 2, [(2, take_out), (0, compare), (0, repeats_dve(dve))])

                @block.scalar
                def _(act):
                    def copy_sum(g, k, s, first):
                        edge_copy_sum(act, g, k, s, first)

                    def copy_rows(g, k, s, first):
                        edge_copy_rows(act, g, k, s, first)

                    def store_xb(g, k, s, first):
                        for n in range(2):
                            act.wait_ge(xb_done, g * 2 + n + 1)
                            act.dma_start(block_rows(bias_fill, 2 * g + n), T[4][:, 2 * s + n, :]
                                          ).then_inc(xb_stored[2 * s + n], 16)

                    def relu(g, k, s, first):
                        act.wait_ge(gathered[s], 16 * J * (k + 1))
                        if not first:
                            act.wait_ge(edge_sum_mm, g - 1)
                        act.activation(T[1][:, s, :], T[0][:, s, :], ACT.Relu).then_inc(relu_done, 1)
                    if lookup is not None:
                        start_act(act)
                        ring_loop(act, NG, 2, [(1, copy_rows), (0, take_act(act)), (0, copy_sum), (1, store_xb)])
                        all_landed(act, xb_stored, NB)
                    else:
                        ring_loop(act, NG, 2, [(3, store_turned_act(act)), (2, take_turned_act(act)),
                                               (1, copy_rows), (0, relu), (0, copy_sum)])
                        finish_act(act)
                        all_landed(act, turned_stored, NG)

                @block.tensor
                def _(pe):
                    def sum_equal(g, k, s, first):
                        if lookup is not None:
                            pe.wait_ge(gathered[s], 16 * J * (k + 1))
                        else:
                            pe.wait_ge(relu_done, g + 1)
                        edge_sum_equal(pe, g, k, s, first)

                    def multiply(g, k, s, first):
                        edge_multiply(pe, g, k, s, first)
                    if lookup is not None:
                        start_pe(pe)
                        ring_loop(pe, NG, 2, [(1, multiply), (0, turn_pe(pe)), (1, rows_pe(pe)), (0, sum_equal)])
                    else:
                        ring_loop(pe, NG, 2, [(1, multiply), (1, count_pe(pe)), (0, sum_equal)])
            end_phase()

        def fill_blocks(sp, filling, g, filled):
            table_ap, start = filling
            for n in range(2):
                sp.dma_start(block_rows(table_ap, 2 * g + n), start).then_inc(filled, 16)

        def edges_first_convolution():
            at_least_one = sem("eB_at_least_one")
            inverse = sem("eB_inverse")
            kept = sem("eB_kept")

            def keep(dve, g):
                dve.tensor_scalar(count_cols[:, :], picked_cols[:, :], 1.0, None, ALU.max).then_inc(at_least_one, 1)
                dve.wait_ge(at_least_one, g + 1)
                dve.reciprocal(dup_cols[:, :], count_cols[:, :]).then_inc(inverse, 1)
                dve.wait_ge(inverse, g + 1)
                dve.tensor_copy(inv_count[:, bass.ds(g * J, J)], dup_cols[:, :]).then_inc(kept, 1)
                dve.wait_ge(kept, g + 1)
            lookup = node_lookup("eB_dst", 1, False, psum[4:6], psum[6:8], None, keep)
            edges_convolution("eB", h0, y1, weights["L0_gnn_W1l"][:, :], lookup, bias_fill=y2)

        def edges_second_convolution():
            row_landed = sem2("eD_src_row_landed")
            counting = (node_counting("eD_src", 0, psum[7], row_landed, count_row, psum[4]),
                        row_landed)
            edges_convolution("eD", y1, y2, weights["L0_gnn_W2l"][:, :], counting=counting,
                              fill=(z1, z_init[:, :]))

        def edges_layer_1():
            (edge_load_row, edge_compare, edge_sum_equal, edge_copy_sum, edge_copy_rows, edge_multiply,
             edge_take_out, edge_add, edge_all_added, edge_sum_mm) = summed_edges(
                 "eF", 1, z1, weights["L1_gnn_Wn1"][:, :], T[1])
            idx_landed = sem2("eF_idx_landed")
            gathered = sem2("eF_gathered")
            ea_landed = sem2("eF_ea_landed")
            filled = sem("eF_filled")
            hid_mm = sem("eF_hid_mm")
            hid_ready = sem("eF_hid_ready")
            ew_mm = sem("eF_ew_mm")
            ew_done = sem("eF_ew_done")
            msg_done = sem("eF_msg_done")

            with nc.Block() as block:
                @block.sync
                def _(sp):
                    def load(g, k, s, first):
                        load_index(sp, gather_a, "src_groups", idx_landed, gathered, J, g, k, s, first)
                        edge_load_row(sp, g, k, s, first)
                        if not first:
                            sp.wait_ge(hid_mm, g - 1)
                        sp.dma_start(T[4][0:50, s, :], ins["edge50"][:, bass.ds(g * ROWS, ROWS)]
                                     ).then_inc(ea_landed[s], 16)
                        fill_blocks(sp, (y3, y3_init[:, :]), g, filled)
                    ring_loop(sp, NG, 2, [(0, load)])
                    sp.wait_ge(filled, 16 * NB)

                @block.gpsimd
                def _(pool):
                    def fetch(g, k, s, first):
                        wait_on_pool(pool, idx_landed[s], 16 * (k + 1))
                        if not first:
                            wait_on_pool(pool, msg_done, g - 1)
                        gather(pool, T[0], gather_a, s, h2, gathered[s])

                    def add(g, k, s, first):
                        edge_add(pool, g, k, s, first)
                    ring_loop(pool, NG, 2, [(0, fetch), (2, add)])
                    edge_all_added(pool)

                @block.vector
                def _(dve):
                    def compare(g, k, s, first):
                        edge_compare(dve, g, k, s, first)

                    def message(g, k, s, first):
                        dve.wait_ge(ew_mm, g + 1)
                        dve.tensor_tensor(jd(T[6][:, s, :]), jd(psum[5][:, :]), across(rows["L1_gnn_be2"][:, :]),
                                          ALU.add).then_inc(ew_done, 1)
                        dve.wait_ge(ew_done, g + 1)
                        dve.wait_ge(gathered[s], 16 * J * (k + 1))
                        if not first:
                            dve.wait_ge(edge_sum_mm, g - 1)
                        dve.tensor_tensor(T[1][:, s, :], T[0][:, s, :], T[6][:, s, :],
                                          ALU.mult).then_inc(msg_done, 1)

                    def take_out(g, k, s, first):
                        edge_take_out(dve, g, k, s, first)
                    ring_loop(dve, NG, 2, [(0, compare), (0, message), (1, take_out)])

                @block.scalar
                def _(act):
                    def silu(g, k, s, first):
                        act.wait_ge(hid_mm, g + 1)
                        if not first:
                            act.wait_ge(ew_mm, g - 1)
                        act.activation(T[5][:, s, :], psum[4][:, :], ACT.Silu,
                                       bias=be1[:, 0:1]).then_inc(hid_ready, 1)

                    def copy_sum(g, k, s, first):
                        edge_copy_sum(act, g, k, s, first)

                    def copy_rows(g, k, s, first):
                        edge_copy_rows(act, g, k, s, first)
                    ring_loop(act, NG, 2, [(1, copy_rows), (0, silu), (1, copy_sum)])

                @block.tensor
                def _(pe):
                    def hidden(g, k, s, first):
                        pe.wait_ge(ea_landed[s], 16 * (k + 1))
                        if not (first and g == 0):
                            pe.wait_ge(hid_ready, g)
                        pe.matmul(psum[4][:, :], w_e1[:, :], T[4][0:50, s, :], start=True,
                                  stop=True).then_inc(hid_mm, 1)

                    def edge_weight(g, k, s, first):
                        pe.wait_ge(hid_ready, g + 1)
                        if not (first and g == 0):
                            pe.wait_ge(ew_done, g)
                        products(pe, psum[5], T[5][:, s, :], weights["L1_gnn_We2"][:, :]).then_inc(ew_mm, 1)

                    def sum_equal(g, k, s, first):
                        pe.wait_ge(msg_done, g + 1)
                        edge_sum_equal(pe, g, k, s, first)

                    def multiply(g, k, s, first):
                        edge_multiply(pe, g, k, s, first)
                    ring_loop(pe, NG, 2, [(0, hidden), (1, sum_equal), (0, edge_weight), (1, multiply)])
            end_phase()

        def measure_ends(dve, norm, got_a, got_b):
            def measure(g, k, s, first):
                for n, (t, got) in enumerate(((T[0], got_a), (T[4], got_b))):
                    dve.wait_ge(got[s], 16 * J * (k + 1))
                    norm_statistics(norm, dve, t[:, s, :], g * 2 + n, 2 * s + n)
            return measure

        def factors_ends(dve, norm, h_done):
            def factors(g, k, s, first):
                if not first:
                    dve.wait_ge(h_done, g * 2 - 2)
                for n in range(2):
                    norm_factors(norm, dve, g * 2 + n, 2 * s + n)
            return factors

        def root_ends(act, norm):
            def root(g, k, s, first):
                for n in range(2):
                    norm_root(norm, act, g * 2 + n, 2 * s + n)
            return root

        def apply_ends(act, norm, h_done):
            def apply(g, k, s, first):
                for n, t in enumerate((T[0], T[4])):
                    norm_apply(norm, act, t[:, s, :], t[:, s, :], g * 2 + n, 2 * s + n).then_inc(h_done, 1)
            return apply

        def edges_layer_2():
            (edge_load_row, edge_compare, edge_sum_equal, edge_copy_sum, edge_copy_rows, edge_multiply,
             edge_take_out, edge_add, edge_all_added, edge_sum_mm) = summed_edges("eH", 1, y3, w_2[:, 1, :], T[1])
            a_landed = sem2("eH_src_idx_landed")
            b_landed = sem2("eH_dst_idx_landed")
            got_a = sem2("eH_src_gathered")
            got_b = sem2("eH_dst_gathered")
            ea_landed = sem2("eH_ea_landed")
            turned_mm = sem("eH_turned_mm")
            turned_ready = sem("eH_turned_ready")
            pre_mm = sem("eH_pre_mm")
            pre_done = sem("eH_pre_done")
            msg_done = sem("eH_msg_done")
            norm = norm_semaphores("eH")
            h_done = sem("eH_h_done")

            with nc.Block() as block:
                @block.sync
                def _(sp):
                    def load(g, k, s, first):
                        load_index(sp, gather_a, "src_groups", a_landed, got_a, J, g, k, s, first)
                        load_index(sp, gather_b, "dst_groups", b_landed, got_b, J, g, k, s, first)
                        edge_load_row(sp, g, k, s, first)
                        if not first:
                            sp.wait_ge(pre_mm, g - 1)
                        sp.dma_start(T[5][:, s, :], ins["edge128"][:, bass.ds(g * ROWS, ROWS)]
                                     ).then_inc(ea_landed[s], 16)
                    ring_loop(sp, NG, 2, [(0, load)])

                @block.gpsimd
                def _(pool):
                    def fetch(g, k, s, first):
                        wait_on_pool(pool, a_landed[s], 16 * (k + 1))
                        wait_on_pool(pool, b_landed[s], 16 * (k + 1))
                        if not first:
                            wait_on_pool(pool, turned_mm, g - 1)
                        gather(pool, T[0], gather_a, s, x2, got_a[s])
                        gather(pool, T[4], gather_b, s, x2, got_b[s])

                    def add(g, k, s, first):
                        edge_add(pool, g, k, s, first)
                    ring_loop(pool, NG, 2, [(0, fetch), (3, add)])
                    edge_all_added(pool)

                @block.vector
                def _(dve):
                    def compare(g, k, s, first):
                        edge_compare(dve, g, k, s, first)

                    def message(g, k, s, first):
                        dve.wait_ge(pre_mm, g + 1)
                        if not first:
                            dve.wait_ge(edge_sum_mm, g - 1)
                        dve.tensor_tensor(jd(T[1][:, s, :]), jd(psum[6][:, :]), across(c1[:, :]),
                                          ALU.add).then_inc(pre_done, 1)
                        dve.wait_ge(pre_done, g + 1)
                        dve.tensor_scalar(T[1][:, s, :], T[1][:, s, :], 0.0, None, ALU.max).then_inc(msg_done, 1)

                    def take_out(g, k, s, first):
                        edge_take_out(dve, g, k, s, first)
                    ring_loop(dve, NG, 2, [(1, measure_ends(dve, norm, got_a, got_b)), (1, compare),
                                           (1, factors_ends(dve, norm, h_done)), (2, message), (3, take_out)])

                @block.scalar
                def _(act):
                    def copy_turned(g, k, s, first):
                        act.wait_ge(turned_mm, g + 1)
                        if not first:
                            act.wait_ge(pre_mm, g - 1)
                        act.activation(T[6][:, s, :], psum[4][:, :], ACT.Copy)
                        act.activation(T[7][:, s, :], psum[5][:, :], ACT.Copy).then_inc(turned_ready, 1)

                    def copy_sum(g, k, s, first):
                        edge_copy_sum(act, g, k, s, first)

                    def copy_rows(g, k, s, first):
                        edge_copy_rows(act, g, k, s, first)
                    ring_loop(act, NG, 2, [(3, copy_rows), (1, root_ends(act, norm)),
                                           (1, apply_ends(act, norm, h_done)), (2, copy_sum), (1, copy_turned)])

                @block.tensor
                def _(pe):
                    def turn(g, k, s, first):
                        if not (first and g == 0):
                            pe.wait_ge(turned_ready, g)
                        pe.wait_ge(h_done, g * 2 + 1)
                        turn_tiles(pe, psum[4], T[0][:, s, :])
                        pe.wait_ge(h_done, g * 2 + 2)
                        turn_tiles(pe, psum[5], T[4][:, s, :]).then_inc(turned_mm, 1)

                    def pre(g, k, s, first):
                        pe.wait_ge(turned_ready, g + 1)
                        pe.wait_ge(ea_landed[s], 16 * (k + 1))
                        if not (first and g == 0):
                            pe.wait_ge(pre_done, g)
                        for j in range(J):
                            o = psum[6][:, j * D:(j + 1) * D]
                            c = slice(j * P, (j + 1) * P)
                            pe.matmul(o, T[7][:, s, c], w_1[:, 0, :], start=True, stop=False)
                            pe.matmul(o, T[6][:, s, c], w_1[:, 1, :], start=False, stop=False)
                            last = pe.matmul(o, T[5][:, s, c], w_1[:, 2, :], start=False, stop=True)
                        last.then_inc(pre_mm, 1)

                    def sum_equal(g, k, s, first):
                        pe.wait_ge(msg_done, g + 1)
                        edge_sum_equal(pe, g, k, s, first)

                    def multiply(g, k, s, first):
                        edge_multiply(pe, g, k, s, first)
                    ring_loop(pe, NG, 2, [(2, pre), (3, multiply), (2, sum_equal), (1, turn)])
            end_phase()

        def edges_scores():
            a_landed = sem2("eJ_src_idx_landed")
            b_landed = sem2("eJ_dst_idx_landed")
            got_a = sem2("eJ_src_gathered")
            got_b = sem2("eJ_dst_gathered")
            ea_landed = sem2("eJ_ea_landed")
            turned_mm = sem("eJ_turned_mm")
            turned_ready = sem("eJ_turned_ready")
            q_mm = sem("eJ_q_mm")
            kv_mm = sem("eJ_kv_mm")
            kv_ready = sem("eJ_kv_ready")
            qk_done = sem("eJ_qk_done")
            vec = sem("eJ_vec")
            norm = norm_semaphores("eJ")
            h_done = sem("eJ_h_done")
            kept = sem("eJ_kept")
            hi_landed = sem2("eJ_hi_landed")

            def keep(dve, g):
                dve.scalar_tensor_tensor(sort_pos[:, bass.ds(g * J, J)], picked_cols[:, :], 1.0,
                                         dup[:, 0, bass.ds(g * J, J)], ALU.add, ALU.add).then_inc(kept, 1)
                dve.wait_ge(kept, g + 1)
            (start_dve, start_pe, start_act, encode_dve, pick_dve, _, rows_pe, round_act, _, count_pe,
             load_turned_sp) = node_lookup("eJ_src", 0, True, [], [psum[7], psum[0]], psum[1], keep, hi_landed)
            score_done = sem("eJ_score_done")
            place_ready = sem("eJ_place_ready")
            placed = sem2("eJ_placed")

            with nc.Block() as block:
                @block.sync
                def _(sp):
                    def load(g, k, s, first):
                        load_index(sp, gather_a, "src_groups", a_landed, got_a, J, g, k, s, first)
                        load_index(sp, gather_b, "dst_groups", b_landed, got_b, J, g, k, s, first)
                        if not first:
                            sp.wait_ge(kv_mm, g - 1)
                        sp.dma_start(T[5][:, s, :], ins["edge128"][:, bass.ds(g * ROWS, ROWS)]
                                     ).then_inc(ea_landed[s], 16)
                    ring_loop(sp, NG, 2, [(0, load), (0, load_turned_sp(sp))])

                @block.gpsimd
                def _(pool):
                    def fetch(g, k, s, first):
                        wait_on_pool(pool, a_landed[s], 16 * (k + 1))
                        wait_on_pool(pool, b_landed[s], 16 * (k + 1))
                        if not first:
                            wait_on_pool(pool, turned_mm, g - 1)
                        gather(pool, T[0], gather_a, s, x3, got_a[s])
                        gather(pool, T[4], gather_b, s, x3, got_b[s])

                    def place(g, k, s, first):
                        wait_on_pool(pool, score_done, g + 1)
                        wait_on_pool(pool, place_ready, g + 1)
                        for a in range(J):
                            pool.indirect_dma_start(sorted_rows,
                                                    bass.IndirectOffsetOnAxis(ap=add_to[:, s, a:a + 1], axis=0),
                                                    score[:, s, a, :], None).then_inc(placed[s], 16)
                    ring_loop(pool, NG, 2, [(0, fetch), (3, place)])
                    for n, q in enumerate(placed):
                        pool.wait_ge(q, 16 * J * uses(NG, 2, n))

                @block.vector
                def _(dve):
                    def scores(g, k, s, first):
                        dve.wait_ge(q_mm, g + 1)
                        dve.wait_ge(kv_ready, g + 1)
                        dve.tensor_tensor(T[3][:, s, :], psum[6][:, :], T[1][:, s, :],
                                          ALU.mult).then_inc(qk_done, 1)
                        dve.wait_ge(qk_done, g + 1)
                        dve.tensor_reduce(qk_sum[:, s, :], T[3][:, s, :].rearrange("p (n d) -> p n d", d=HEAD_DIM),
                                          AX_X, ALU.add).then_inc(vec, 1)
                        dve.wait_ge(vec, g * 2 + 1)
                        for j in range(J):
                            last = dve.tensor_tensor(
                                mixed[:, j * 64:(j + 1) * 64].rearrange("p (o h) -> p o h", h=HEADS),
                                qk_sum[:, s, j * HEADS:(j + 1) * HEADS].unsqueeze(1).to_broadcast([P, HEADS, HEADS]),
                                w_exp[:, :].rearrange("p (o h) -> p o h", h=HEADS), ALU.mult)
                        last.then_inc(vec, 1)
                        dve.wait_ge(vec, g * 2 + 2)
                        if not first:
                            dve.wait_ge(placed[s], 16 * J * k)
                        dve.tensor_reduce(score[:, s, :, 0:HEADS],
                                          mixed[:, :].rearrange("p (j o h) -> p j o h", j=J, h=HEADS), AX_X, ALU.add)
                        dve.tensor_copy(score[:, s, :, HEADS + 1], is_self[:, bass.ds(g * J, J)])
                        dve.tensor_copy(score[:, s, :, HEADS], src_f[:, bass.ds(g * J, J)]
                                        ).then_inc(score_done, 1)
                    start_dve(dve)
                    ring_loop(dve, NG, 2, [(1, measure_ends(dve, norm, got_a, got_b)),
                                           (1, factors_ends(dve, norm, h_done)), (0, encode_dve(dve)),
                                           (1, pick_dve(dve)), (3, scores)])

                @block.scalar
                def _(act):
                    def copy_turned(g, k, s, first):
                        act.wait_ge(turned_mm, g + 1)
                        if not first:
                            act.wait_ge(q_mm, g - 1)
                        act.activation(T[6][:, s, :], psum[4][:, :], ACT.Copy)
                        act.activation(T[7][:, s, :], psum[5][:, :], ACT.Copy).then_inc(turned_ready, 1)

                    def copy_kv(g, k, s, first):
                        act.wait_ge(kv_mm, g + 1)
                        if not first:
                            act.wait_ge(qk_done, g - 1)
                            act.wait_ge(placed[s], 16 * J * k)
                        for n in range(2):
                            kv = psum[2 + n][:, :].rearrange("p (j w d) -> p j w d", j=2, w=2)
                            act.activation(T[1][:, s, n * 2 * D:(n + 1) * 2 * D].rearrange("p (j d) -> p j d", j=2),
                                           kv[:, :, 0, :], ACT.Copy, scale=SCALE)
                            last = act.activation(score[:, s, 2 * n:2 * n + 2, KEYS:SORT_W], kv[:, :, 1, :],
                                                  ACT.Copy)
                        last.then_inc(kv_ready, 1)
                        act.wait_ge(kept, g + 1)
                        act.activation(add_to[:, s, :], sort_pos[:, bass.ds(g * J, J)],
                                       ACT.Copy).then_inc(place_ready, 1)
                    start_act(act)
                    ring_loop(act, NG, 2, [(0, round_act(act)), (1, root_ends(act, norm)),
                                           (1, apply_ends(act, norm, h_done)), (2, copy_kv), (1, copy_turned)])

                @block.tensor
                def _(pe):
                    def turn(g, k, s, first):
                        if not (first and g == 0):
                            pe.wait_ge(turned_ready, g)
                        pe.wait_ge(h_done, g * 2 + 1)
                        turn_tiles(pe, psum[4], T[0][:, s, :])
                        pe.wait_ge(h_done, g * 2 + 2)
                        turn_tiles(pe, psum[5], T[4][:, s, :]).then_inc(turned_mm, 1)

                    def project_kv(g, k, s, first):
                        pe.wait_ge(turned_ready, g + 1)
                        pe.wait_ge(ea_landed[s], 16 * (k + 1))
                        if not (first and g == 0):
                            pe.wait_ge(kv_ready, g)
                        for j in range(J):
                            o = psum[2 + j // 2][:, (j % 2) * 2 * D:(j % 2 + 1) * 2 * D]
                            c = slice(j * P, (j + 1) * P)
                            pe.matmul(o, T[7][:, s, c], w_kv[:, :], start=True, stop=False)
                            last = pe.matmul(o, T[5][:, s, c], w_ekv[:, :], start=False, stop=True)
                        last.then_inc(kv_mm, 1)

                    def project_q(g, k, s, first):
                        if not (first and g == 0):
                            pe.wait_ge(qk_done, g)
                        products(pe, psum[6], T[6][:, s, :], weights["L3_gnn_Wq"][:, :]).then_inc(q_mm, 1)
                    start_pe(pe)
                    ring_loop(pe, NG, 2, [(1, count_pe(pe)), (2, project_kv), (1, rows_pe(pe)), (1, turn),
                                          (2, project_q)])
            end_phase()

        def softmax_by_source():
            landed = sem("sm_landed")
            v = sem("sm_v")
            turned_mm = sem("sm_turned")
            back = sem("sm_back")
            exp_done = sem("sm_exp_done")
            diff_done = sem("sm_diff_done")
            stored = sem("sm_stored")
            src_ready = sem("sm_src_ready")
            shifted_mm = sem("sm_shifted_mm")
            rows_ready = sem("sm_rows_ready")
            ask = sem("sm_ask")
            ask_back = sem("sm_ask_back")

            with nc.Block() as block:
                @block.sync
                def _(sp):
                    main = sorted_rows[1:EDGES + 1, :].rearrange("(p n) c -> p n c", p=P)
                    front = sorted_rows[0:EDGES, :].rearrange("(p n) c -> p n c", p=P)
                    behind = sorted_rows[2:EDGES + 2, :].rearrange("(p n) c -> p n c", p=P)
                    sp.dma_start(ss[:, 0, :], front[:, 0, 0:KEYS]).then_inc(landed, 16)
                    sp.dma_start(ss[:, NT + 1, :], behind[:, NT - 1, 0:KEYS]).then_inc(landed, 16)
                    for n in range(J):
                        sp.dma_start(ss[:, 1 + n * NG:1 + (n + 1) * NG, :], main[:, n * NG:(n + 1) * NG, 0:KEYS]
                                     ).then_inc(landed, 16)
                    tiles = source_rows.rearrange("g (a p) -> (g a) p", a=J)
                    sp.wait_ge(rows_ready, 1)
                    sp.dma_start(tiles[0:P, :], T[7][:, 0, 0:P]).then_inc(stored, 16)
                    sp.dma_start(tiles[P:NT, :], T[7][0:NT - P, 0, P:2 * P]).then_inc(stored, 16)
                    sp.wait_ge(stored, 32)

                @block.vector
                def _(dve):
                    count = [0]

                    def link(instruction):
                        instruction.then_inc(v, 1)
                        count[0] += 1
                        dve.wait_ge(v, count[0])

                    dve.wait_ge(landed, 16 * (J + 2))
                    node = ss[:, :, HEADS]
                    dve.tensor_copy(sorted_src[:, :], node[:, 1:NT + 1])
                    dve.tensor_scalar(tmp_t[:, :], node[:, 1:NT + 1], 1.0, None, ALU.add).then_inc(src_ready, 1)
                    dve.wait_ge(src_ready, 1)
                    link(dve.tensor_tensor(keep[:, 0, :], node[:, 1:NT + 1], node[:, 0:NT], ALU.is_equal))
                    link(dve.tensor_tensor(keep[:, 1, :], node[:, 1:NT + 1], node[:, 2:NT + 2], ALU.is_equal))
                    link(dve.tensor_scalar(drop[:, :, :], keep[:, :, :], -1.0, FAR, ALU.add, ALU.mult))

                    dve.wait_ge(shifted_mm, 1)
                    by_group = flag[:, :].rearrange("p (g a) -> p g a", a=J)
                    link(dve.tensor_copy(flag[:, :], keep[:, 0, :]))
                    link(dve.tensor_tensor(by_group[:, :, 0], psum[2][:, 0:NG],
                                           tmp_t[:, :].rearrange("p (g a) -> p g a", a=J)[:, :, 0], ALU.is_equal))
                    link(dve.tensor_tensor(sorted_add[:, :].rearrange("p (g a) -> p g a", a=J),
                                           spare[:, :].unsqueeze(1).to_broadcast([P, NG, J]),
                                           sorted_src[:, :].rearrange("p (g a) -> p g a", a=J), ALU.subtract))
                    link(dve.tensor_tensor(sorted_add[:, :], sorted_add[:, :], flag[:, :], ALU.mult))
                    link(dve.tensor_tensor(sorted_add[:, :], sorted_add[:, :], sorted_src[:, :], ALU.add))

                    rounds = [0]

                    def scan(result, mask, source, op0, op1, neutral, backward):
                        n = rounds[0]
                        rounds[0] += 1

                        def way(ap):
                            return ap[:, ::-1] if backward else ap
                        for h in range(HEADS):
                            last = dve.tensor_tensor_scan(way(result[:, h, :]), way(mask), way(source[:, h, :]),
                                                          neutral, op0, op1)
                        link(last)
                        running_mask = cum[:, n // 2, n % 2, :]
                        link(dve.tensor_tensor_scan(way(running_mask), way(mask), way(mask), FAR, ALU.min, ALU.min))
                        end = 0 if backward else NT - 1
                        link(dve.tensor_copy(edge_in[:, 0, :], result[:, :, end]))
                        dve.tensor_copy(edge_in[:, 1, :], running_mask[:, end:end + 1].to_broadcast([P, HEADS])
                                        ).then_inc(ask, 1)
                        dve.wait_ge(turned_mm, n + 1)
                        link(dve.tensor_copy(turned[:, :, :].rearrange("h t p -> h (t p)"), psum[0][0:HEADS, 0:2 * P]))
                        link(dve.memset(carry[:, :], neutral))
                        place = carry[:, 0:P] if backward else carry[:, 1:P + 1]
                        dve.tensor_tensor_scan(way(place), way(turned[:, 1, :]), way(turned[:, 0, :]), neutral, op0,
                                               op1).then_inc(ask_back, 1)
                        dve.wait_ge(back, n + 1)
                        link(dve.tensor_copy(carry_in[:, :], psum[1][:, 0:HEADS]))
                        for h in range(HEADS):
                            last = dve.scalar_tensor_tensor(result[:, h, :], running_mask, carry_in[:, h:h + 1],
                                                            result[:, h, :], op0, op1)
                        link(last)

                    raw = ss[:, 1:NT + 1, 0:HEADS].rearrange("p n h -> p h n")
                    scan(scan_f, drop[:, 0, :], raw, ALU.add, ALU.max, -FAR, False)
                    scan(scan_b, drop[:, 1, :], raw, ALU.add, ALU.max, -FAR, True)
                    link(dve.tensor_tensor(scan_f[:, :, :], scan_f[:, :, :], scan_b[:, :, :], ALU.max))
                    dve.tensor_tensor(expd[:, :, :], raw, scan_f[:, :, :], ALU.subtract).then_inc(diff_done, 1)
                    dve.wait_ge(exp_done, 1)
                    scan(scan_f, keep[:, 0, :], expd, ALU.mult, ALU.add, 0.0, False)
                    scan(scan_b, keep[:, 1, :], expd, ALU.mult, ALU.add, 0.0, True)
                    link(dve.tensor_tensor(scan_b[:, :, :], scan_b[:, :, :], expd[:, :, :], ALU.subtract))
                    link(dve.tensor_tensor(scan_f[:, :, :], scan_f[:, :, :], scan_b[:, :, :], ALU.add))
                    link(dve.reciprocal(scan_b[:, :, :], scan_f[:, :, :]))
                    link(dve.tensor_tensor(scan_b[:, :, :], expd[:, :, :], scan_b[:, :, :], ALU.mult))
                    link(dve.tensor_tensor(scan_f[:, :, :], ss[:, 1:NT + 1, HEADS + 1].unsqueeze(1)
                                           .to_broadcast([P, HEADS, NT]), scan_b[:, :, :], ALU.subtract))

                @block.scalar
                def _(act):
                    act.wait_ge(shifted_mm, 2)
                    act.activation(T[7][:, 0, 0:P], psum[3][:, 0:P], ACT.Copy)
                    act.activation(T[7][0:NT - P, 0, P:2 * P], psum[3][0:NT - P, P:2 * P],
                                   ACT.Copy).then_inc(rows_ready, 1)
                    act.wait_ge(diff_done, 1)
                    act.activation(expd[:, :, :], expd[:, :, :], ACT.Exp).then_inc(exp_done, 1)

                @block.tensor
                def _(pe):
                    pe.wait_ge(src_ready, 1)
                    pe.matmul(psum[2][:, 0:NG], one_on[:, :],
                              tmp_t[:, :].rearrange("p (g a) -> p g a", a=J)[:, :, J - 1],
                              start=True, stop=True).then_inc(shifted_mm, 1)
                    pe.transpose(psum[3][:, 0:P], sorted_src[:, 0:P], ident[:, :])
                    pe.transpose(psum[3][0:NT - P, P:2 * P], sorted_src[:, P:NT], ident[:, :]
                                 ).then_inc(shifted_mm, 1)
                    for n in range(4):
                        pe.wait_ge(ask, n + 1)
                        pe.transpose(psum[0][0:HEADS, 0:P], edge_in[:, 0, :], ident[:, :])
                        pe.transpose(psum[0][0:HEADS, P:2 * P], edge_in[:, 1, :], ident[:, :]
                                     ).then_inc(turned_mm, 1)
                        pe.wait_ge(ask_back, n + 1)
                        off = n % 2
                        pe.transpose(psum[1][:, 0:HEADS], carry[:, off:off + P], ident[0:HEADS, 0:HEADS]
                                     ).then_inc(back, 1)
            end_phase()

        def edges_layer_3():
            (edge_load_row, edge_compare, edge_sum_equal, edge_copy_sum, edge_copy_rows, edge_multiply,
             edge_take_out, edge_add, edge_all_added, edge_sum_mm) = summed_edges(
                 "eK", 0, out, weights["L3_gnn_Wout"][:, :], T[1])
            v_landed = sem2("eK_v_landed")
            msg_done = sem("eK_msg_done")

            with nc.Block() as block:
                @block.sync
                def _(sp):
                    by_partition = sorted_rows[1:EDGES + 1, :].rearrange("(p n) c -> p n c", p=P)

                    def load(g, k, s, first):
                        edge_load_row(sp, g, k, s, first)
                        if not first:
                            sp.wait_ge(msg_done, g - 1)
                        sp.dma_start(jd(T[0][:, s, :]), by_partition[:, bass.ds(g * J, J), KEYS:SORT_W]
                                     ).then_inc(v_landed[s], 16)
                    ring_loop(sp, NG, 2, [(0, load)])

                @block.gpsimd
                def _(pool):
                    def add(g, k, s, first):
                        edge_add(pool, g, k, s, first)
                    ring_loop(pool, NG, 2, [(0, add)])
                    edge_all_added(pool)

                @block.vector
                def _(dve):
                    def compare(g, k, s, first):
                        edge_compare(dve, g, k, s, first)

                    def message(g, k, s, first):
                        dve.wait_ge(v_landed[s], 16 * (k + 1))
                        if not first:
                            dve.wait_ge(edge_sum_mm, g - 1)
                        dve.tensor_tensor(T[1][:, s, :].rearrange("p (a h d) -> p a h d", a=J, h=HEADS),
                                          T[0][:, s, :].rearrange("p (a h d) -> p a h d", a=J, h=HEADS),
                                          scan_f[:, :, bass.ds(g * J, J)].rearrange("p h a -> p a h").unsqueeze(3)
                                          .to_broadcast([P, J, HEADS, HEAD_DIM]), ALU.mult).then_inc(msg_done, 1)

                    def take_out(g, k, s, first):
                        edge_take_out(dve, g, k, s, first)
                    ring_loop(dve, NG, 2, [(2, take_out), (0, compare), (0, message)])

                @block.scalar
                def _(act):
                    def copy_sum(g, k, s, first):
                        edge_copy_sum(act, g, k, s, first)

                    def copy_rows(g, k, s, first):
                        edge_copy_rows(act, g, k, s, first)
                    ring_loop(act, NG, 2, [(1, copy_rows), (0, copy_sum)])

                @block.tensor
                def _(pe):
                    def sum_equal(g, k, s, first):
                        pe.wait_ge(msg_done, g + 1)
                        edge_sum_equal(pe, g, k, s, first)

                    def multiply(g, k, s, first):
                        edge_multiply(pe, g, k, s, first)
                    ring_loop(pe, NG, 2, [(1, multiply), (0, sum_equal)])
            end_phase()

        setup()
        nodes_into_layer_0()
        edges_first_convolution()
        edges_second_convolution()
        nodes_into_layer_1()
        edges_layer_1()
        nodes_into_layer_2()
        edges_layer_2()
        nodes_into_layer_3()
        edges_scores()
        softmax_by_source()
        edges_layer_3()


def kernel(**inputs):
    import numpy as np
    import concourse.bacc as bacc
    from concourse.bass_utils import run_bass_kernel_spmd as run

    a = {n: np.asarray(v) for n, v in inputs.items()}
    n_nodes, n_edges = a["x"].shape[0], a["src"].shape[0]
    nodes, edges = padded(n_nodes, ROWS), padded(n_edges, ROWS)

    def pad_rows(v, n, fill=0):
        return np.concatenate([v, np.full((n - v.shape[0],) + v.shape[1:], fill, v.dtype)])

    src = pad_rows(a.pop("src"), edges, n_nodes)
    dst = pad_rows(a.pop("dst"), edges, n_nodes)
    feed = {"x": pad_rows(a.pop("x"), nodes)}
    for name, v in (("src", src), ("dst", dst)):
        feed[name + "_cols"] = v.reshape(edges // P, P).T
        feed[name + "_rows"] = v.reshape(edges // ROWS, ROWS)
        feed[name + "_groups"] = v.reshape(edges // ROWS, J, P).transpose(0, 2, 1).view(np.uint32)
    feed["edge50"] = pad_rows(a.pop("edge_attr_50"), edges).T
    feed["edge128"] = pad_rows(a.pop("edge_attr_128"), edges).T
    for name in ("L2_gnn_W1", "L2_gnn_W2"):
        feed[name] = a.pop(name).T
    feed["L3_gnn_Wexp"] = a.pop("L3_gnn_Wexp").T.reshape(-1)
    feed.update(a)
    feed = {n: np.ascontiguousarray(v) for n, v in feed.items()}

    nc = bacc.Bacc("TRN2", target_bir_lowering=False, num_devices=1)
    ins = {n: nc.dram_tensor(n, v.shape, mybir.dt.from_np(v.dtype), kind="ExternalInput").ap()
           for n, v in feed.items()}
    out = nc.dram_tensor("out", (nodes + ROWS, D), F32, kind="ExternalOutput").ap()
    gnn_kernel(nc, ins, out, n_nodes, n_edges)
    r = run(nc, [feed], core_ids=[0])
    return r.results[0]["out"][:n_nodes]
```
